# Optimizing a Trainium2 kernel written in Bass

```python
import numpy as np
import jax
import jax.numpy as jnp

def _softmax(x, axis=-1):
    return jax.nn.softmax(x, axis=axis)

def _gelu(x):
    return jax.nn.gelu(x, approximate=True)

def _silu(x):
    return jax.nn.silu(x)

def _sigmoid(x):
    return jax.nn.sigmoid(x)

def _layernorm(x, axis=-1, eps=1e-05):
    m = jnp.mean(x, axis=axis, keepdims=True)
    v = jnp.var(x, axis=axis, keepdims=True)
    return (x - m) / jnp.sqrt(v + eps)

def _scatter_add(tgt, idx, src, axis=0):
    return tgt.at[idx].add(src)

def _segment_sum(src, seg, n):
    return jax.ops.segment_sum(src, seg, n)
kernel_name = 'mk_vit_tower_d2_tok_img1024_r4_253b91'

def setup_inputs(seed: int=0):
    np.random.seed(seed)
    _w = jnp.asarray

    def _rec_inputs():
        import jax
        import jax.numpy as jnp
        _rk = jax.random.key(seed)
        x = -0.00016672 + 0.999947 * jax.random.normal(jax.random.fold_in(_rk, 1), (16, 3, 96, 96), jnp.float32)
        return x
    x = _rec_inputs()

    def _L0_tok_setup():
        import jax, jax.numpy as jnp
        import numpy as np
        PATCH = 16

        def _patchify(x, p):
            B, C, H, W = x.shape
            nh, nw = (H // p, W // p)
            x = x.reshape(B, C, nh, p, nw, p)
            x = x.transpose(0, 2, 4, 1, 3, 5)
            return x.reshape(B, nh * nw, C * p * p)
        key = jax.random.key(seed)
        k1, k2, k3, k4, k5 = jax.random.split(key, 5)
        B, C, H = (64, 3, 96)
        d_model = 256
        p = PATCH
        num_patches = (H // p) ** 2
        in_dim = p * p * C
        x = jax.random.normal(k1, (B, C, H, H), dtype=jnp.float32)
        bound = 1.0 / np.sqrt(in_dim)
        W = jax.random.uniform(k2, (d_model, in_dim), dtype=jnp.float32, minval=-bound, maxval=bound)
        b = jax.random.uniform(k3, (d_model,), dtype=jnp.float32, minval=-bound, maxval=bound)
        cls_token = jax.random.normal(k4, (1, 1, d_model), dtype=jnp.float32)
        pos_enc = jax.random.normal(k5, (1, num_patches + 1, d_model), dtype=jnp.float32)
        return {'x': x, 'W': W, 'b': b, 'cls_token': cls_token, 'pos_enc': pos_enc}
    _L0_tok_all = _L0_tok_setup()
    _L0_tok_in = {k: v for k, v in _L0_tok_all.items() if k in ('W', 'b', 'cls_token', 'pos_enc')}
    del _L0_tok_all

    def _L0_attn_setup():
        import jax, jax.numpy as jnp
        import numpy as np
        import math
        H = 16

        def quant4(x):
            xs = jax.lax.stop_gradient(x)
            ma = jnp.maximum(jnp.max(jnp.abs(xs), axis=-1, keepdims=True), 1e-06)
            q = jnp.clip(jnp.round(xs / ma * 7.0), -8.0, 7.0)
            return x + jax.lax.stop_gradient(q * ma / 7.0 - xs)

        def ternary_weight(w):
            thresh = jax.lax.stop_gradient(0.05 * jnp.mean(jnp.abs(w)))
            sign = jnp.where(jnp.abs(w) < thresh, 0.0, jnp.sign(w))
            alpha = jnp.mean(jnp.abs(w), axis=1, keepdims=True)
            return sign * alpha + (w - jax.lax.stop_gradient(w))

        def rotary(t, n):
            half = t.shape[-1] // 2
            inv = 1.0 / 10000.0 ** (jnp.arange(half, dtype=t.dtype) / half)
            ang = jnp.arange(n, dtype=t.dtype)[:, None] * inv
            c, s = (jnp.cos(ang), jnp.sin(ang))
            t1, t2 = (t[..., ::2], t[..., 1::2])
            return jnp.concatenate([t1 * c - t2 * s, t1 * s + t2 * c], axis=-1)
        key = jax.random.key(seed)
        k1, k2, k3, k4 = jax.random.split(key, 4)
        B, N, d, r = (2, 512, 256, 32)
        dk = d // H
        x = jax.random.normal(k1, (B, N, d), dtype=jnp.float32)
        Wqkv_w = jax.random.normal(k2, (d, d), dtype=jnp.float32) / math.sqrt(d)
        Wqkv_b = jnp.zeros((d,), dtype=jnp.float32)
        U = jax.random.normal(k3, (dk, r), dtype=jnp.float32) / math.sqrt(dk)
        Wo_w = jax.random.normal(k4, (d, d), dtype=jnp.float32) / math.sqrt(d)
        return {'x': x, 'Wqkv_w': Wqkv_w, 'Wqkv_b': Wqkv_b, 'U': U, 'Wo_w': Wo_w}
    _L0_attn_all = _L0_attn_setup()
    _L0_attn_in = {k: v for k, v in _L0_attn_all.items() if k in ('Wqkv_w', 'Wqkv_b', 'U', 'Wo_w')}
    del _L0_attn_all

    def _L0_ffn_setup():
        import jax, jax.numpy as jnp
        import numpy as np
        B, S, D = (4, 512, 256)
        F = 688
        E = 8
        TOPK = 2

        def _ffn(x, gw, uw, dw):
            return jax.nn.silu(x @ gw) * (x @ uw) @ dw
        key = jax.random.key(seed)
        ks = jax.random.split(key, 10)
        sc = 0.02
        return {'x': jax.random.normal(ks[0], (B, S, D), dtype=jnp.float32), 'router_w': jax.random.normal(ks[1], (D, E), dtype=jnp.float32) * sc, 'router_b': jnp.zeros((E,), dtype=jnp.float32), 'gate_w': jax.random.normal(ks[2], (E, D, F), dtype=jnp.float32) * sc, 'up_w': jax.random.normal(ks[3], (E, D, F), dtype=jnp.float32) * sc, 'down_w': jax.random.normal(ks[4], (E, F, D), dtype=jnp.float32) * sc, 'sh_gate_w': jax.random.normal(ks[5], (D, F), dtype=jnp.float32) * sc, 'sh_up_w': jax.random.normal(ks[6], (D, F), dtype=jnp.float32) * sc, 'sh_down_w': jax.random.normal(ks[7], (F, D), dtype=jnp.float32) * sc}
    _L0_ffn_all = _L0_ffn_setup()
    _L0_ffn_in = {k: v for k, v in _L0_ffn_all.items() if k in ('router_w', 'router_b', 'gate_w', 'up_w', 'down_w', 'sh_gate_w', 'sh_up_w', 'sh_down_w')}
    del _L0_ffn_all

    def _L1_attn_setup():
        import jax, jax.numpy as jnp
        import numpy as np
        D = 256
        H = 16
        KVH = 4
        HD = D // H
        LAT = 64
        WIN = 64
        B, S = (1, 512)
        BASE_G, BASE_L = (1000000.0, 10000.0)
        EPS = 1e-06

        def rmsnorm(x, w):
            return x * jax.lax.rsqrt(jnp.mean(x * x, axis=-1, keepdims=True) + EPS) * w

        def qk_norm(x):
            return x * jax.lax.rsqrt(jnp.mean(x * x, axis=-1, keepdims=True) + EPS)

        def rope(x, base):
            s, hd = (x.shape[-2], x.shape[-1])
            inv_freq = 1.0 / base ** (jnp.arange(0, hd, 2, dtype=jnp.float32) / hd)
            freqs = jnp.arange(s, dtype=jnp.float32)[:, None] * inv_freq[None, :]
            cos, sin = (jnp.cos(freqs), jnp.sin(freqs))
            xe, xo = (x[..., ::2], x[..., 1::2])
            out = jnp.stack([xe * cos - xo * sin, xe * sin + xo * cos], axis=-1)
            return out.reshape(x.shape)

        def split_heads(x, n_heads):
            b, s, _ = x.shape
            return x.reshape(b, s, n_heads, HD).transpose(0, 2, 1, 3)

        def repeat_kv(x):
            return jnp.repeat(x, H // KVH, axis=1)

        def sdpa(q, k, v, mask):
            scores = jnp.einsum('bhqd,bhkd->bhqk', q, k) / np.sqrt(HD).astype(np.float32)
            scores = jnp.where(mask, scores, jnp.float32(-1e+30))
            probs = jax.nn.softmax(scores, axis=-1)
            return jnp.einsum('bhqk,bhkd->bhqd', probs, v)

        def merge_heads(x):
            b, h, s, hd = x.shape
            return x.transpose(0, 2, 1, 3).reshape(b, s, h * hd)

        def global_latent_attn(x, wq, w_kv_down, w_k_up, w_v_up, wo):
            q = split_heads(x @ wq, H)
            latent = x @ w_kv_down
            k = split_heads(latent @ w_k_up, KVH)
            v = split_heads(latent @ w_v_up, KVH)
            q, k = (rope(q, BASE_G), rope(k, BASE_G))
            q, k = (qk_norm(q), qk_norm(k))
            k, v = (repeat_kv(k), repeat_kv(v))
            i = jnp.arange(x.shape[1])
            causal = i[:, None] >= i[None, :]
            return merge_heads(sdpa(q, k, v, causal)) @ wo

        def local_gqa_attn(x, wq, wk, wv, wo):
            q = split_heads(x @ wq, H)
            k = split_heads(x @ wk, KVH)
            v = split_heads(x @ wv, KVH)
            q, k = (rope(q, BASE_L), rope(k, BASE_L))
            q, k = (qk_norm(q), qk_norm(k))
            k, v = (repeat_kv(k), repeat_kv(v))
            i = jnp.arange(x.shape[1])
            diff = i[:, None] - i[None, :]
            mask = (diff >= 0) & (diff < WIN)
            return merge_heads(sdpa(q, k, v, mask)) @ wo
        key = jax.random.key(seed)
        ks = jax.random.split(key, 12)
        std = 0.02
        return {'hidden': jax.random.normal(ks[0], (B, S, D), dtype=jnp.float32), 'norm1_w': jnp.ones((D,), jnp.float32), 'norm2_w': jnp.ones((D,), jnp.float32), 'g_wq': jax.random.normal(ks[1], (D, H * HD), jnp.float32) * std, 'g_kv_down': jax.random.normal(ks[2], (D, LAT), jnp.float32) * std, 'g_k_up': jax.random.normal(ks[3], (LAT, KVH * HD), jnp.float32) * std, 'g_v_up': jax.random.normal(ks[4], (LAT, KVH * HD), jnp.float32) * std, 'g_wo': jax.random.normal(ks[5], (D, D), jnp.float32) * std, 'l_wq': jax.random.normal(ks[6], (D, H * HD), jnp.float32) * std, 'l_wk': jax.random.normal(ks[7], (D, KVH * HD), jnp.float32) * std, 'l_wv': jax.random.normal(ks[8], (D, KVH * HD), jnp.float32) * std, 'l_wo': jax.random.normal(ks[9], (D, D), jnp.float32) * std}
    _L1_attn_all = _L1_attn_setup()
    _L1_attn_in = {k: v for k, v in _L1_attn_all.items() if k in ('norm1_w', 'norm2_w', 'g_wq', 'g_kv_down', 'g_k_up', 'g_v_up', 'g_wo', 'l_wq', 'l_wk', 'l_wv', 'l_wo')}
    del _L1_attn_all

    def _L1_ffn_setup():
        import jax, jax.numpy as jnp
        import numpy as np
        MAX_VAL = 100.0
        key = jax.random.key(seed)
        k1, k2, k3 = jax.random.split(key, 3)
        B, S, D_IN, D_OUT = (4, 2048, 256, 256)
        x = jax.random.normal(k1, (B, S, D_IN), dtype=jnp.float32)
        weights = jax.random.normal(k2, (D_OUT, D_IN), dtype=jnp.float32)
        scale = jnp.ones((D_OUT,), dtype=jnp.float32)
        bias = jax.random.normal(k3, (D_OUT,), dtype=jnp.float32)
        return {'x': x, 'weights': weights, 'scale': scale, 'bias': bias}
    _L1_ffn_all = _L1_ffn_setup()
    _L1_ffn_in = {k: v for k, v in _L1_ffn_all.items() if k in ('weights', 'scale', 'bias')}
    del _L1_ffn_all
    return {'x': x, 'L0_tok_W': _L0_tok_in['W'], 'L0_tok_b': _L0_tok_in['b'], 'L0_tok_cls_token': _L0_tok_in['cls_token'], 'L0_tok_pos_enc': _L0_tok_in['pos_enc'], 'L0_attn_Wqkv_w': _L0_attn_in['Wqkv_w'], 'L0_attn_Wqkv_b': _L0_attn_in['Wqkv_b'], 'L0_attn_U': _L0_attn_in['U'], 'L0_attn_Wo_w': _L0_attn_in['Wo_w'], 'L0_ffn_router_w': _L0_ffn_in['router_w'], 'L0_ffn_router_b': _L0_ffn_in['router_b'], 'L0_ffn_gate_w': _L0_ffn_in['gate_w'], 'L0_ffn_up_w': _L0_ffn_in['up_w'], 'L0_ffn_down_w': _L0_ffn_in['down_w'], 'L0_ffn_sh_gate_w': _L0_ffn_in['sh_gate_w'], 'L0_ffn_sh_up_w': _L0_ffn_in['sh_up_w'], 'L0_ffn_sh_down_w': _L0_ffn_in['sh_down_w'], 'L1_attn_norm1_w': _L1_attn_in['norm1_w'], 'L1_attn_norm2_w': _L1_attn_in['norm2_w'], 'L1_attn_g_wq': _L1_attn_in['g_wq'], 'L1_attn_g_kv_down': _L1_attn_in['g_kv_down'], 'L1_attn_g_k_up': _L1_attn_in['g_k_up'], 'L1_attn_g_v_up': _L1_attn_in['g_v_up'], 'L1_attn_g_wo': _L1_attn_in['g_wo'], 'L1_attn_l_wq': _L1_attn_in['l_wq'], 'L1_attn_l_wk': _L1_attn_in['l_wk'], 'L1_attn_l_wv': _L1_attn_in['l_wv'], 'L1_attn_l_wo': _L1_attn_in['l_wo'], 'L1_ffn_weights': _L1_ffn_in['weights'], 'L1_ffn_scale': _L1_ffn_in['scale'], 'L1_ffn_bias': _L1_ffn_in['bias']}

def reference(x, L0_tok_W, L0_tok_b, L0_tok_cls_token, L0_tok_pos_enc, L0_attn_Wqkv_w, L0_attn_Wqkv_b, L0_attn_U, L0_attn_Wo_w, L0_ffn_router_w, L0_ffn_router_b, L0_ffn_gate_w, L0_ffn_up_w, L0_ffn_down_w, L0_ffn_sh_gate_w, L0_ffn_sh_up_w, L0_ffn_sh_down_w, L1_attn_norm1_w, L1_attn_norm2_w, L1_attn_g_wq, L1_attn_g_kv_down, L1_attn_g_k_up, L1_attn_g_v_up, L1_attn_g_wo, L1_attn_l_wq, L1_attn_l_wk, L1_attn_l_wv, L1_attn_l_wo, L1_ffn_weights, L1_ffn_scale, L1_ffn_bias):
    import jax
    import jax.numpy as jnp

    def _L0_tok_ref(x, W, b, cls_token, pos_enc):
        import jax, jax.numpy as jnp
        import numpy as np
        PATCH = 16

        def _patchify(x, p):
            B, C, H, W = x.shape
            nh, nw = (H // p, W // p)
            x = x.reshape(B, C, nh, p, nw, p)
            x = x.transpose(0, 2, 4, 1, 3, 5)
            return x.reshape(B, nh * nw, C * p * p)
        B = x.shape[0]
        patches = _patchify(x, PATCH)
        proj = jnp.einsum('bnf,df->bnd', patches, W) + b
        cls = jnp.broadcast_to(cls_token, (B, 1, cls_token.shape[-1]))
        out = jnp.concatenate([cls, proj], axis=1) + pos_enc
        return out

    def _L0_attn_ref(x, Wqkv_w, Wqkv_b, U, Wo_w):
        import jax, jax.numpy as jnp
        import numpy as np
        import math
        H = 16

        def quant4(x):
            xs = jax.lax.stop_gradient(x)
            ma = jnp.maximum(jnp.max(jnp.abs(xs), axis=-1, keepdims=True), 1e-06)
            q = jnp.clip(jnp.round(xs / ma * 7.0), -8.0, 7.0)
            return x + jax.lax.stop_gradient(q * ma / 7.0 - xs)

        def ternary_weight(w):
            thresh = jax.lax.stop_gradient(0.05 * jnp.mean(jnp.abs(w)))
            sign = jnp.where(jnp.abs(w) < thresh, 0.0, jnp.sign(w))
            alpha = jnp.mean(jnp.abs(w), axis=1, keepdims=True)
            return sign * alpha + (w - jax.lax.stop_gradient(w))

        def rotary(t, n):
            half = t.shape[-1] // 2
            inv = 1.0 / 10000.0 ** (jnp.arange(half, dtype=t.dtype) / half)
            ang = jnp.arange(n, dtype=t.dtype)[:, None] * inv
            c, s = (jnp.cos(ang), jnp.sin(ang))
            t1, t2 = (t[..., ::2], t[..., 1::2])
            return jnp.concatenate([t1 * c - t2 * s, t1 * s + t2 * c], axis=-1)
        B, N, d = x.shape
        h = H
        dk = d // h
        proj = quant4(x) @ ternary_weight(Wqkv_w).T + Wqkv_b
        q = proj.reshape(B, N, h, dk).transpose(0, 2, 1, 3)
        k = proj.reshape(B, h, N, dk)
        v = proj.reshape(B, h, N, dk)
        q, k = (rotary(q, N), rotary(k, N))
        ql, kl = (q @ U, k @ U)
        att = jnp.einsum('bhnr,bhmr->bhnm', ql, kl) / math.sqrt(dk)
        y = jax.nn.softmax(att, axis=-1) @ v
        y = y.transpose(0, 2, 1, 3).reshape(B, N, d)
        return quant4(y) @ ternary_weight(Wo_w).T

    def _L0_ffn_ref(x, router_w, router_b, gate_w, up_w, down_w, sh_gate_w, sh_up_w, sh_down_w):
        import jax, jax.numpy as jnp
        import numpy as np
        B, S, D = (4, 512, 256)
        F = 688
        E = 8
        TOPK = 2

        def _ffn(x, gw, uw, dw):
            return jax.nn.silu(x @ gw) * (x @ uw) @ dw
        b, s, d = x.shape
        xt = x.reshape(b * s, d)
        probs = jax.nn.softmax(xt @ router_w + router_b, axis=-1)
        rw, ids = jax.lax.top_k(probs, TOPK)
        rw = rw / (jnp.sum(rw, axis=-1, keepdims=True) + 1e-20)
        y = jnp.zeros_like(xt)
        for e in range(E):
            w_e = jnp.sum(jnp.where(ids == e, rw, 0.0), axis=-1)
            y = y + w_e[:, None] * _ffn(xt, gate_w[e], up_w[e], down_w[e])
        y = y + _ffn(xt, sh_gate_w, sh_up_w, sh_down_w)
        return y.reshape(b, s, d)

    def _L1_attn_ref(hidden, norm1_w, norm2_w, g_wq, g_kv_down, g_k_up, g_v_up, g_wo, l_wq, l_wk, l_wv, l_wo):
        import jax, jax.numpy as jnp
        import numpy as np
        D = 256
        H = 16
        KVH = 4
        HD = D // H
        LAT = 64
        WIN = 64
        B, S = (1, 512)
        BASE_G, BASE_L = (1000000.0, 10000.0)
        EPS = 1e-06

        def rmsnorm(x, w):
            return x * jax.lax.rsqrt(jnp.mean(x * x, axis=-1, keepdims=True) + EPS) * w

        def qk_norm(x):
            return x * jax.lax.rsqrt(jnp.mean(x * x, axis=-1, keepdims=True) + EPS)

        def rope(x, base):
            s, hd = (x.shape[-2], x.shape[-1])
            inv_freq = 1.0 / base ** (jnp.arange(0, hd, 2, dtype=jnp.float32) / hd)
            freqs = jnp.arange(s, dtype=jnp.float32)[:, None] * inv_freq[None, :]
            cos, sin = (jnp.cos(freqs), jnp.sin(freqs))
            xe, xo = (x[..., ::2], x[..., 1::2])
            out = jnp.stack([xe * cos - xo * sin, xe * sin + xo * cos], axis=-1)
            return out.reshape(x.shape)

        def split_heads(x, n_heads):
            b, s, _ = x.shape
            return x.reshape(b, s, n_heads, HD).transpose(0, 2, 1, 3)

        def repeat_kv(x):
            return jnp.repeat(x, H // KVH, axis=1)

        def sdpa(q, k, v, mask):
            scores = jnp.einsum('bhqd,bhkd->bhqk', q, k) / np.sqrt(HD).astype(np.float32)
            scores = jnp.where(mask, scores, jnp.float32(-1e+30))
            probs = jax.nn.softmax(scores, axis=-1)
            return jnp.einsum('bhqk,bhkd->bhqd', probs, v)

        def merge_heads(x):
            b, h, s, hd = x.shape
            return x.transpose(0, 2, 1, 3).reshape(b, s, h * hd)

        def global_latent_attn(x, wq, w_kv_down, w_k_up, w_v_up, wo):
            q = split_heads(x @ wq, H)
            latent = x @ w_kv_down
            k = split_heads(latent @ w_k_up, KVH)
            v = split_heads(latent @ w_v_up, KVH)
            q, k = (rope(q, BASE_G), rope(k, BASE_G))
            q, k = (qk_norm(q), qk_norm(k))
            k, v = (repeat_kv(k), repeat_kv(v))
            i = jnp.arange(x.shape[1])
            causal = i[:, None] >= i[None, :]
            return merge_heads(sdpa(q, k, v, causal)) @ wo

        def local_gqa_attn(x, wq, wk, wv, wo):
            q = split_heads(x @ wq, H)
            k = split_heads(x @ wk, KVH)
            v = split_heads(x @ wv, KVH)
            q, k = (rope(q, BASE_L), rope(k, BASE_L))
            q, k = (qk_norm(q), qk_norm(k))
            k, v = (repeat_kv(k), repeat_kv(v))
            i = jnp.arange(x.shape[1])
            diff = i[:, None] - i[None, :]
            mask = (diff >= 0) & (diff < WIN)
            return merge_heads(sdpa(q, k, v, mask)) @ wo
        x = hidden
        x = x + global_latent_attn(rmsnorm(x, norm1_w), g_wq, g_kv_down, g_k_up, g_v_up, g_wo)
        x = x + local_gqa_attn(rmsnorm(x, norm2_w), l_wq, l_wk, l_wv, l_wo)
        return x

    def _L1_ffn_ref(x, weights, scale, bias):
        import jax, jax.numpy as jnp
        import numpy as np
        MAX_VAL = 100.0
        w = (weights >= 0.0).astype(x.dtype) * 2.0 - 1.0
        y = jnp.einsum('bsi,oi->bso', x, w)
        y = y * scale + bias
        y = jnp.clip(y, -MAX_VAL, MAX_VAL)
        return y
    h = _L0_tok_ref(x, L0_tok_W, L0_tok_b, L0_tok_cls_token, L0_tok_pos_enc)
    h = h + _L0_attn_ref(_layernorm(h, axis=-1), L0_attn_Wqkv_w, L0_attn_Wqkv_b, L0_attn_U, L0_attn_Wo_w)
    h = h + _L0_ffn_ref(_layernorm(h, axis=-1), L0_ffn_router_w, L0_ffn_router_b, L0_ffn_gate_w, L0_ffn_up_w, L0_ffn_down_w, L0_ffn_sh_gate_w, L0_ffn_sh_up_w, L0_ffn_sh_down_w)
    h = h + _L1_attn_ref(_layernorm(h, axis=-1), L1_attn_norm1_w, L1_attn_norm2_w, L1_attn_g_wq, L1_attn_g_kv_down, L1_attn_g_k_up, L1_attn_g_v_up, L1_attn_g_wo, L1_attn_l_wq, L1_attn_l_wk, L1_attn_l_wv, L1_attn_l_wo)
    h = h + _L1_ffn_ref(_layernorm(h, axis=-1), L1_ffn_weights, L1_ffn_scale, L1_ffn_bias)
    return h

_drawn_inputs = setup_inputs


def setup_inputs(seed=0):
    import zlib

    import numpy as np

    out = dict(_drawn_inputs(seed))
    spreads = {'L0_attn_Wqkv_b': (0.0, 0.1),
     'L0_ffn_router_b': (0.0, 0.8),
     'L1_attn_norm1_w': (1.0, 0.6),
     'L1_attn_norm2_w': (1.0, 0.6),
     'L1_ffn_scale': (1.0, 0.2)}
    factors = {'L0_ffn_router_w': 4.083,
     'L0_ffn_gate_w': 3.484,
     'L0_ffn_up_w': 3.453,
     'L0_ffn_down_w': 3.409,
     'L1_attn_g_wq': 8.0,
     'L1_attn_g_kv_down': 8.0,
     'L1_attn_g_k_up': 8.0,
     'L1_attn_g_v_up': 8.0,
     'L1_attn_g_wo': 8.0,
     'L1_attn_l_wq': 4.788,
     'L1_attn_l_wk': 4.745,
     'L1_attn_l_wv': 2.868,
     'L1_attn_l_wo': 3.066}
    for name, (base, spread) in spreads.items():
        noise = np.random.default_rng([zlib.crc32(name.encode()), seed]).standard_normal(out[name].shape)
        drawn = base * np.exp(spread * noise) if base else spread * noise
        out[name] = jnp.asarray(drawn.astype(out[name].dtype))
    for name, factor in factors.items():
        out[name] = (out[name] * factor).astype(out[name].dtype)
    return out
```

```python
from contextlib import ExitStack

import numpy as np

import concourse.bass as bass
from concourse import mybir

F32 = mybir.dt.float32
BF16 = mybir.dt.bfloat16
ALU = mybir.AluOpType
ACT = mybir.ActivationFunctionType
AX_X = mybir.AxisListType.X

P = 128
B = 16
N = 37
D = 256
DC = D // P
T = B * N
TT = -(-T // P)
TP = TT * P
HT = T // 2
PC = 6
POSK = N + 2
H = 16
DH = D // H
R = 2 * DH
BG = 4
B4 = B // BG
G4T = B4 * N
PAIRS = B // 2
HG = 8
KV = 4
LAT = 64
E = 8
F = 688
FC = -(-F // P)
FL = F - (FC - 1) * P
WX = DC * F * 2 + FC * D
MAGIC = 1.5 * 2.0 ** 23
LN_EPS = 1e-5
RMS_EPS = 1e-6
NORMS = 6
BK = 512

C_ID, C_ONE, C_FOLD, C_MEAN = 0, P, 2 * P, 3 * P
C_CSQ = 4 * P
C_CSK = C_CSQ + N
C_CSG = C_CSK + T
C_CSL = C_CSG + N
C_MASK = C_CSL + N
C_HM = C_MASK + N
C_HALF = C_HM + 2
C_LT = C_HALF + 5
C_EPS = C_LT + E * E
CW = C_EPS + 1

S_BQ = 0
S_N1 = S_BQ + H
S_N2 = S_N1 + DC
S_SC = S_N2 + DC
S_BI = S_SC + D
S_RB = S_BI + D
SW = S_RB + E


def tower(nc, xT, tokW, sel, posb, const, small, wq0, u2t, wo0, rw, wexp,
          wqg, kvd, kug, vug, wog, wql, wvl, wol, wfin, out, dbg):
    ctx = ExitStack()
    with ctx:
        def sb(name, shape, dt=F32):
            return ctx.enter_context(nc.sbuf_tensor(name, shape, dt))

        sems = {}

        def S(name):
            if name not in sems:
                sems[name] = ctx.enter_context(nc.semaphore(name))
            return sems[name]

        ps = ctx.enter_context(nc.psum_tensor("ps", [P, 8 * BK], F32))
        psb = ps[:, :].bitcast(BF16)

        def bank(i, n=1):
            return ps[:, i * BK:(i + n) * BK]

        cst = sb("cst", [P, CW])
        sml = sb("sml", [P, SW])
        ident = cst[:, C_ID:C_ID + P]
        ones = cst[:, C_ONE:C_ONE + P]
        fold = cst[:, C_FOLD:C_FOLD + P]
        mean16 = cst[:, C_MEAN:C_MEAN + P]
        identb = sb("identb", [P, P], BF16)

        h = sb("h", [P, TT, D])
        xn = sb("xn", [P, TT, D])
        xnT = sb("xnT", [P, DC, TP])
        stats = sb("stats", [P, TT, 6])
        mv = sb("mv", [P, TT, 2])
        rstd = sb("rstd", [P, TT])
        vtmp = sb("vtmp", [P, TT])

        arena_a = sb("arena_a", [P, 10000])
        arena_b = sb("arena_b", [P, 13200])

        xT_s = arena_a[:, 0:PC * TP].rearrange("p (c t) -> p c t", c=PC)
        tokW_s = arena_a[:, PC * TP:PC * TP + PC * D].rearrange("p (c t) -> p c t", c=PC)
        o = PC * TP + PC * D
        sel_s = arena_a[:, o:o + TP]
        posb_s = arena_a[:, o + TP:o + TP + D]

        wq0_s = sb("wq0_s", [P, DC, H * R])
        wabs = sb("wabs", [P, DC, H * R])
        sg = sb("sg", [P, DC, H * R], BF16)
        sgn = sb("sgn", [P, DC, H * R], BF16)
        sq0 = sb("sq0", [P, DC, H * R], BF16)
        alq = sb("alq", [P, H])
        thr = sb("thr", [P, 4])
        u2t_s = sb("u2t_s", [R, R])
        m2 = sb("m2", [P, P])
        wo0_s = sb("wo0_s", [P, DC, D])
        wo0q = sb("wo0q", [P, DC, D])
        mab = sb("mab", [P, G4T])

        xq = sb("xq", [P, TT, D], BF16)
        xqT = sb("xqT", [P, DC, TP], BF16)
        ma = sb("ma", [P, TT])
        dg = sb("dg", [P, TT, P])
        G4 = B4 * T // B * H
        am = arena_a[:, 0:G4]
        pr = arena_a[:, G4:2 * G4]
        qcs = arena_a[:, 2 * G4:3 * G4]
        kcs = arena_a[:, 3 * G4:4 * G4]
        qf = arena_b[:, 0:G4]
        VW = DH + 1
        o = G4
        vbd = arena_b[:, o:o + B * HG * 2 * VW]
        o += B * HG * 2 * VW
        pe_ = [arena_b[:, o + i * H * N:o + (i + 1) * H * N] for i in range(2)]
        o += 2 * H * N
        ptT = [arena_b[:, o + i * HG * P:o + (i + 1) * HG * P] for i in range(2)]
        o += 2 * HG * P
        yq = arena_a[:, 0:PAIRS * D].rearrange("p (a d) -> p a d", a=PAIRS)
        yqT = arena_a[:, PAIRS * D:PAIRS * D + DC * TP].rearrange("p (c t) -> p c t", c=DC)
        mx = sb("mx", [P, 2, H])
        ma2 = sb("ma2", [P, PAIRS])
        rma = sb("rma", [P, PAIRS])
        rz = sb("rz", [P, 2, H])

        rw_s = sb("rw_s", [P, DC, E])
        lg = sb("lg", [P, TT, E])
        lmx = sb("lmx", [P, TT])
        gt = sb("gt", [P, TT, E, E])
        eq = sb("eq", [P, TT, E, E])
        rank = sb("rank", [P, TT, E])
        wts = sb("wts", [P, E + 1, TT])
        wbuf = [arena_a[:, i * WX:(i + 1) * WX] for i in range(2)]
        gact = [sb(f"gact{i}", [P, HT]) for i in range(2)]
        hid = arena_b[:, 0:FC * TP].rearrange("p (c t) -> p c t", c=FC)

        wl1 = {}
        for n in "gl":
            kd = KV + 1 if n == "l" else KV
            wl1[n] = dict(
                wq=sb(f"wq_{n}", [P, DC, kd, P]),
                wo=sb(f"wo_{n}", [P, KV, D]),
            )
        kvd_s = sb("kvd_s", [P, DC, LAT])
        kug_s = sb("kug_s", [LAT, P])
        vug_s = sb("vug_s", [LAT, KV * DH])
        wvl_s = sb("wvl_s", [P, DC, KV * DH])
        latT = sb("latT", [LAT, TP])
        xres = sb("xres", [P, TT, D])
        U5 = KV + 1
        qk = arena_a[:, 0:U5 * T].rearrange("p (u t) -> p u t", u=U5)
        sqr = arena_a[:, U5 * T:2 * U5 * T].rearrange("p (u t) -> p u t", u=U5)
        kf = arena_a[:, 2 * U5 * T:2 * U5 * T + TP]
        vo = arena_a[:, 2 * U5 * T + TP:2 * U5 * T + TP + PAIRS * KV * R].rearrange(
            "p (a g r) -> p a g r", a=PAIRS, g=KV)
        QT = 2 * 4 * N
        ex = [arena_b[:, i * KV * QT:(i + 1) * KV * QT].rearrange("p (g c) -> p g c", g=KV)
              for i in range(2)]
        oz = arena_b[:, 2 * KV * QT:2 * KV * QT + 4 * T].rearrange("p (u t) -> p u t", u=4)
        zs = arena_b[:, 2 * KV * QT + 4 * T:2 * KV * QT + 8 * T].rearrange("p (u t) -> p u t", u=4)
        ozp = sb("ozp", [P, KV, TP])

        wfin_s = sb("wfin_s", [P, DC, D])
        wfs = sb("wfs", [P, DC, D])

        def flat(t):
            return t.rearrange("p a b -> p (a b)")

        block = ctx.enter_context(nc.Block())

        @block.sync
        def _(sp):
            sp.dma_start(wq0_s[:, :, :], wq0).then_inc(S("d_wq0"), 16)
            sp.dma_start(cst[:, :], const).then_inc(S("d_cst"), 16)
            for c in range(PC):
                sp.dma_start(xT_s[:, c, :], xT[:, c, :]).then_inc(S("d_x"), 16)
                sp.dma_start(tokW_s[:, c, :], tokW[:, c, :]).then_inc(S("d_x"), 16)
                sp.wait_ge(S("d_x"), 32 * c + 32)
            sp.wait_ge(S("wo_mm"), TT)
            sp.dma_start(wbuf[0], wexp[0]).then_inc(S("d_wexp0"), 16)
            sp.dma_start(wbuf[1], wexp[1]).then_inc(S("d_wexp1"), 16)
            with sp.Fori(0, E // 2 - 1) as i:
                sp.wait_ge(S("expert_done"), 2 * i + 1)
                sp.dma_start(wbuf[0], wexp[2 * i + 2]).then_inc(S("d_wexp0"), 16)
                sp.wait_ge(S("expert_done"), 2 * i + 2)
                sp.dma_start(wbuf[1], wexp[2 * i + 3]).then_inc(S("d_wexp1"), 16)
            sp.wait_ge(S("expert_done"), E - 1)
            sp.dma_start(wbuf[0], wexp[E]).then_inc(S("d_wexp0"), 16)
            for t in range(TT):
                rows = min(P, T - t * P)
                sp.wait_ge(S("out_ready"), t + 1)
                sp.dma_start(out[t * P:t * P + rows, :], h[0:rows, t, :]).then_inc(S("d_out"), 16)
            sp.wait_ge(S("d_out"), 16 * TT)

        @block.scalar
        def _(act):
            A = nc.scalar.activation
            act.dma_start(sel_s[0:POSK, :], sel).then_inc(S("d_pos"), 16)
            act.dma_start(posb_s[0:POSK, :], posb).then_inc(S("d_pos"), 16)
            act.dma_start(sml[:, :], small).then_inc(S("d_sml"), 16)
            act.dma_start(u2t_s[:, :], u2t).then_inc(S("d_u2t"), 16)
            act.dma_start(wo0_s[:, :, :], wo0).then_inc(S("d_wo0"), 16)
            act.dma_start(rw_s[:, :, :], rw).then_inc(S("d_rw"), 16)
            for dst, src in ((wl1["g"]["wq"], wqg), (kvd_s, kvd), (wl1["g"]["wo"], wog),
                             (wl1["l"]["wq"], wql), (wvl_s, wvl), (wl1["l"]["wo"], wol),
                             (wfin_s, wfin)):
                act.dma_start(dst[:, :, :], src).then_inc(S("d_l1"), 16)
            act.dma_start(kug_s[:, :], kug).then_inc(S("d_l1"), 16)
            act.dma_start(vug_s[:, :], vug).then_inc(S("d_l1"), 16)

            act.wait_ge(S("d_wq0"), 16)
            A(wabs[:, :, :], wq0_s[:, :, :], ACT.Abs).then_inc(S("wabs"), 1)
            act.wait_ge(S("wabs_used"), 1)
            act.wait_ge(S("d_wo0"), 16)
            A(wabs[:, :, 0:D], wo0_s[:, :, :], ACT.Abs).then_inc(S("wabs"), 1)

            for t in range(TT):
                act.wait_ge(S("tok"), t + 1)
                A(h[:, t, :], bank(t)[:, 0:D], ACT.Copy).then_inc(S("h0"), 1)

            act.wait_ge(S("xq_t"), 1)
            A(xqT[:, 0, :], psb[:, 5 * 2 * BK:5 * 2 * BK + TP], ACT.Copy).then_inc(S("xqT"), 1)

            for c in range(5):
                w = min(BK, G4 - c * BK)
                act.wait_ge(S("qf_mm"), c + 1)
                A(qf[:, c * BK:c * BK + w], bank(4 + c % 2)[:, 0:w], ACT.Copy).then_inc(S("qf"), 1)

            def expo(p):
                act.wait_ge(S("shifted"), p + 1)
                A(pe_[p % 2], pe_[p % 2], ACT.Exp, scale=0.25).then_inc(S("expd"), 1)

            def evac_pt(p):
                act.wait_ge(S("pt_mm"), p + 1)
                if p >= 2:
                    act.wait_ge(S("y_mm"), p - 1)
                A(ptT[p % 2][0:2 * N, :], bank(4, 2)[0:2 * N, :], ACT.Copy).then_inc(S("pt"), 1)

            for p in range(PAIRS + 1):
                if p < PAIRS:
                    expo(p)
                if p >= 1:
                    evac_pt(p - 1)

            act.wait_ge(S("yT_mm"), 1)
            A(yqT[:, 0, 0:T].rearrange("p (a b n) -> p a b n", a=PAIRS, b=2),
              bank(0, 2).rearrange("p (a b n) -> p a b n", a=PAIRS, b=2)[:, :, :, 0:N],
              ACT.Copy).then_inc(S("yT"), 1)

            def evac_T(stage, scale):
                act.wait_ge(S("nT_mm"), stage)
                A(xnT[:, 0, :], bank(4, 2)[:, 0:TP], ACT.Copy if scale is None else ACT.Identity,
                  scale=1.0 if scale is None else scale).then_inc(S("nT"), 1)

            evac_T(1, None)

            act.wait_ge(S("lg_shift"), 1)
            A(lg[:, :, :], lg[:, :, :], ACT.Exp).then_inc(S("lg_exp"), 1)

            def silu(u, base):
                act.wait_ge(S("gu"), base + u + 1)
                if base is not 0 or u >= 2:
                    act.wait_ge(S("hid"), base + u - 1)
                w = P if u // 2 < FC - 1 else FL
                A(gact[u % 2][0:w, :], bank(2 * (u % 2))[0:w, 0:HT],
                  ACT.Silu).then_inc(S("silu"), 1)

            for u in range(2 * FC):
                silu(u, 0)
            with act.Fori(0, E) as i:
                base = (i + 1) * (2 * FC)
                for u in range(2 * FC):
                    silu(u, base)

            def l1(li):
                evac_T(li + 2, sml[:, (S_N1, S_N2)[li]:(S_N1, S_N2)[li] + 1])
                if li == 0:
                    for hf in range(2):
                        act.wait_ge(S("lat_mm"), hf + 1)
                        A(latT[:, hf * HT:(hf + 1) * HT], bank(4 + hf)[0:LAT, 0:HT],
                          ACT.Copy).then_inc(S("lat"), 1)
                U = 2 * U5

                def square(u):
                    act.wait_ge(S("qkcs"), U * li + u + 1)
                    A(sqr[:, u // 2, (u % 2) * HT:(u % 2 + 1) * HT],
                      qk[:, u // 2, (u % 2) * HT:(u % 2 + 1) * HT], ACT.Square).then_inc(S("sqr"), 1)

                def sqroot(u):
                    act.wait_ge(S("ms_mm"), U * li + u + 1)
                    A(sqr[:, u // 2, (u % 2) * HT:(u % 2 + 1) * HT], bank(4 + u % 4)[:, 0:HT],
                      ACT.Sqrt, bias=cst[:, C_EPS:C_EPS + 1]).then_inc(S("rt"), 1)

                for u in range(U + 2):
                    if u < U:
                        square(u)
                    if u >= 2:
                        sqroot(u - 2)
                for hf in range(2):
                    act.wait_ge(S("kf_mm"), 2 * li + hf + 1)
                    A(kf[:, hf * HT:(hf + 1) * HT], bank(4 + hf)[:, 0:HT],
                      ACT.Copy).then_inc(S("kf"), 1)

                def evac_o(grp):
                    for par in range(2):
                        act.wait_ge(S("o_mm"), 8 * li + 2 * grp + par + 1)
                        src = bank(4 + 2 * (grp % 2) + par)[:, 0:QT].rearrange(
                            "p (a u n) -> p a u n", a=2, u=4)
                        dst = oz.rearrange("p u (a b n) -> p b a u n", a=PAIRS, b=2)[
                            :, par, 2 * grp:2 * grp + 2]
                        A(dst, src, ACT.Copy).then_inc(S("o"), 1)

                for grp in range(4):
                    for g in range(KV):
                        act.wait_ge(S("s_mm"), 16 * li + 4 * grp + g + 1)
                        if grp >= 2:
                            act.wait_ge(S("o_mm"), 8 * li + 2 * (grp - 1))
                        A(ex[grp % 2][:, g, :], bank(g)[:, 0:QT], ACT.Exp,
                          scale=0.25).then_inc(S("ex"), 1)
                    if grp >= 1:
                        evac_o(grp - 1)
                evac_o(3)

            l1(0)
            l1(1)
            evac_T(4, None)

        @block.vector
        def _(dve):
            V = nc.vector
            chain = [0]

            def link(ins):
                chain[0] += 1
                ins.then_inc(S("dve_chain"), 1)
                dve.wait_ge(S("dve_chain"), chain[0])

            link(V.memset(bank(6, 2), 1.0))
            link(V.memset(m2[:, :], 0.0))
            link(V.memset(wts[:, :, :], 1.0))
            link(V.memset(latT[:, :], 0.0))
            link(V.memset(ozp[:, :, T:TP], 0.0))
            dve.wait_ge(S("d_cst"), 16)
            V.tensor_copy(identb[:, :], ident).then_inc(S("identb"), 1)

            def ternary(w, tmp_p, tmp_n, colsum, factor):
                link(V.reduce_sum(thr[:, 0:1], colsum, AX_X))
                link(V.tensor_scalar(thr[:, 1:2], thr[:, 0:1], factor, None, ALU.mult))
                link(V.tensor_scalar(thr[:, 2:3], thr[:, 1:2], -1.0, None, ALU.mult))
                link(V.tensor_scalar(tmp_p, w, thr[:, 1:2], None, ALU.is_ge))
                link(V.tensor_scalar(tmp_n, w, thr[:, 2:3], None, ALU.is_le))

            dve.wait_ge(S("wabs_used"), 1)
            ternary(wq0_s[:, :, :], sg[:, :, :], sgn[:, :, :], bank(5)[:, 0:H * R],
                    0.05 / (2.0 * D * D))
            V.tensor_tensor(sq0[:, :, :], sg[:, :, :], sgn[:, :, :], ALU.subtract).then_inc(S("sq0"), 1)
            link(V.tensor_scalar(alq[:, :], bank(6)[:, 0:H], 1.0 / D, None, ALU.mult))
            V.memset(bank(6)[:, 0:H], 1.0).then_inc(S("alq"), 1)
            dve.wait_ge(S("m2_mm"), 1)
            for q in range(4):
                r = slice(32 * q, 32 * q + 32)
                link(V.tensor_copy(m2[r, r], bank(7)[r, 0:R]))
            V.memset(bank(7)[:, 0:R], 1.0).then_inc(S("m2"), 1)

            dve.wait_ge(S("sq0"), 1)
            dve.wait_ge(S("wosum"), 1)
            ternary(wo0_s[:, :, :], sg[:, :, 0:D], sgn[:, :, 0:D], bank(5)[:, 0:D],
                    0.05 / (1.0 * D * D))
            link(V.tensor_tensor(wo0q[:, :, :], sg[:, :, 0:D], sgn[:, :, 0:D], ALU.subtract))
            link(V.tensor_scalar(dg[:, 0:2, :], bank(5)[:, 0:D].rearrange("p (a b) -> p a b", a=2),
                                 1.0 / D, None, ALU.mult))
            V.tensor_tensor(wo0q[:, :, :], wo0q[:, :, :],
                            dg[:, 0:2, :].rearrange("p a b -> p (a b)").unsqueeze(1).to_broadcast([P, DC, D]),
                            ALU.mult).then_inc(S("wo0q"), 1)

            norm_count = [0]

            def moments(src):
                for t in range(TT):
                    V.bn_stats(stats[:, t, :], src[:, t, :]).then_inc(S("bn"), 1)
                norm_count[0] += TT
                dve.wait_ge(S("bn"), norm_count[0])
                for t in range(TT):
                    V.bn_aggr(mv[:, t, :], stats[:, t, :]).then_inc(S("bn2"), 1)
                dve.wait_ge(S("bn2"), norm_count[0])

            pows = [0]

            def root():
                pows[0] += 1
                dve.wait_ge(S("rstd"), pows[0])

            def layernorm(src, dst):
                moments(src)
                V.tensor_scalar(vtmp[:, :], mv[:, :, 1], LN_EPS, None, ALU.add).then_inc(S("var"), 1)
                root()
                for t in range(TT):
                    last = V.tensor_scalar(dst[:, t, :], src[:, t, :], mv[:, t, 0:1], rstd[:, t:t + 1],
                                           ALU.subtract, ALU.mult)
                return last

            def rmsnorm(src, dst):
                moments(src)
                link(V.tensor_tensor(vtmp[:, :], mv[:, :, 0], mv[:, :, 0], ALU.mult))
                link(V.tensor_tensor(vtmp[:, :], vtmp[:, :], mv[:, :, 1], ALU.add))
                V.tensor_scalar(vtmp[:, :], vtmp[:, :], RMS_EPS, None, ALU.add).then_inc(S("var"), 1)
                root()
                for t in range(TT):
                    last = V.tensor_scalar(dst[:, t, :], src[:, t, :], rstd[:, t:t + 1], None, ALU.mult)
                return last

            dve.wait_ge(S("h0"), TT)
            link(layernorm(h, xn))
            link(V.tensor_reduce(ma[:, :], xn[:, :, :], AX_X, ALU.max, apply_absolute_value=True))
            link(V.tensor_scalar(ma[:, :], ma[:, :], 1e-6, None, ALU.max))
            link(V.reciprocal(vtmp[:, :], ma[:, :]))
            for t in range(TT):
                last = V.tensor_scalar(xn[:, t, :], xn[:, t, :], vtmp[:, t:t + 1], 7.0, ALU.mult, ALU.mult)
            link(last)
            link(V.tensor_scalar(xn[:, :, :], xn[:, :, :], MAGIC, None, ALU.add))
            V.tensor_scalar(xq[:, :, :], xn[:, :, :], MAGIC, None, ALU.subtract).then_inc(S("xq"), 1)
            V.tensor_tensor(dg[:, :, :], ident.unsqueeze(1).to_broadcast([P, TT, P]),
                            ma[:, :].unsqueeze(2).to_broadcast([P, TT, P]), ALU.mult).then_inc(S("dg"), 1)
            dve.wait_ge(S("xq_t"), 2)
            V.tensor_copy(xqT[:, 1, :], psb[:, 6 * 2 * BK:6 * 2 * BK + TP]).then_inc(S("xqT"), 1)
            dve.wait_ge(S("xqT"), 2)
            dve.wait_ge(S("mab_mm"), 1)
            for q in range(4):
                r = slice(32 * q, 32 * q + 32)
                last = V.tensor_scalar(mab[r, :], ps[r, 3 * BK + q * G4T:3 * BK + (q + 1) * G4T],
                                       1.0 / 7.0, None, ALU.mult)
            last.then_inc(S("mab"), 1)
            link(V.memset(bank(6), 1.0))
            link(V.tensor_tensor(am.rearrange("p (t j) -> p t j", j=H),
                                 mab[:, :].unsqueeze(2).to_broadcast([P, G4T, H]),
                                 alq[:, :].unsqueeze(1).to_broadcast([P, G4T, H]), ALU.mult))
            for jb in range(6):
                nj = min(3, H - 3 * jb)
                dve.wait_ge(S("pr_mm"), jb + 1)
                last = V.tensor_tensor(
                    pr.rearrange("p (t j) -> p j t", j=H)[:, 3 * jb:3 * jb + nj, :],
                    bank(jb)[:, 0:nj * G4T].rearrange("p (j t) -> p j t", j=nj),
                    am.rearrange("p (t j) -> p j t", j=H)[:, 3 * jb:3 * jb + nj, :], ALU.mult)
            link(last)
            bq = sml[:, S_BQ:S_BQ + H]
            V.tensor_tensor(pr.rearrange("p (t j) -> p t j", j=H), pr.rearrange("p (t j) -> p t j", j=H),
                            bq.unsqueeze(1).to_broadcast([P, G4T, H]), ALU.add).then_inc(S("pr"), 1)
            dve.wait_ge(S("pr"), 1)
            csq = cst[:, C_CSQ:C_CSQ + N]
            for b in range(B4):
                last = V.tensor_tensor(
                    qcs.rearrange("p (b j n) -> p b j n", b=B4, j=H)[:, b],
                    pr.rearrange("p (b n j) -> p b j n", b=B4, j=H)[:, b],
                    csq.unsqueeze(1).to_broadcast([P, H, N]), ALU.mult)
            last.then_inc(S("qcs"), 1)
            csk = cst[:, C_CSK:C_CSK + T]
            V.tensor_tensor(kcs.rearrange("p (b r) -> p b r", b=B4), pr.rearrange("p (b r) -> p b r", b=B4),
                            csk.unsqueeze(1).to_broadcast([P, B4, T]), ALU.mult).then_inc(S("kcs"), 1)
            vb = vbd.rearrange("p (b g k w) -> p b g k w", b=B, g=HG, k=2)
            for k in range(2):
                hm = cst[0:2 * N, C_HM + k:C_HM + k + 1]
                V.tensor_copy(vb[0:2 * N, :, :, k, DH].rearrange("p b g -> p (b g)"),
                              hm.to_broadcast([2 * N, B * HG]))
            for b in range(B4):
                dve.wait_ge(S("v_mm"), b + 1)
                for k in range(2):
                    hm = cst[0:2 * N, C_HM + k:C_HM + k + 1]
                    src = bank(2 * (b % 2), 2)[0:2 * N].rearrange("p (g q r) -> p g q r", g=HG, q=BG)
                    dst = vbd.rearrange("p (q b g k w) -> p b k g q w", q=BG, b=B4, g=HG, k=2)
                    last = V.tensor_scalar(dst[0:2 * N, b, k, :, :, 0:DH], src[:, :, :, 0:DH],
                                           hm, None, ALU.mult)
                last.then_inc(S("v"), 1)

            def shift(p):
                dve.wait_ge(S("sc_mm"), p + 1)
                s3 = bank(2 * (p % 2), 2).rearrange("p (a c) -> p a c", a=2)[:, :, 0:8 * N]
                for a in range(2):
                    last = V.reduce_max(mx[:, p % 2, 8 * a:8 * a + 8],
                                        s3[:, a].rearrange("p (j m) -> p j m", m=N), AX_X)
                link(last)
                if p >= 2:
                    dve.wait_ge(S("pt_mm"), p - 1)
                for a in range(2):
                    last = V.tensor_tensor(
                        pe_[p % 2].rearrange("p (a j m) -> p a j m", a=2, j=8)[:, a],
                        s3[:, a].rearrange("p (j m) -> p j m", m=N),
                        mx[:, p % 2, 8 * a:8 * a + 8].unsqueeze(2).to_broadcast([P, 8, N]), ALU.subtract)
                last.then_inc(S("shifted"), 1)

            def finish_y(p):
                dve.wait_ge(S("y_mm"), p + 1)
                yv = bank(6 + p % 2)[:, 0:H * VW].rearrange("p (j w) -> p j w", w=VW)
                link(V.reciprocal(rz[:, p % 2, :], yv[:, :, DH]))
                y = yq[:, p, :]
                V.tensor_tensor(y.rearrange("p (j w) -> p j w", w=DH), yv[:, :, 0:DH],
                                rz[:, p % 2, :].unsqueeze(2).to_broadcast([P, H, DH]),
                                ALU.mult).then_inc(S("y"), 1)
                dve.wait_ge(S("y"), p + 1)
                m = ma2[:, p:p + 1]
                link(V.tensor_reduce(m, y, AX_X, ALU.max, apply_absolute_value=True))
                link(V.tensor_scalar(m, m, 1e-6, None, ALU.max))
                link(V.reciprocal(rma[:, p:p + 1], m))
                link(V.tensor_scalar(y, y, rma[:, p:p + 1], 7.0, ALU.mult, ALU.mult))
                link(V.tensor_scalar(y, y, MAGIC, None, ALU.add))
                link(V.tensor_scalar(y, y, MAGIC, m, ALU.subtract, ALU.mult))
                V.tensor_scalar(y, y, 1.0 / 7.0, None, ALU.mult).then_inc(S("yq"), 1)

            for p in range(PAIRS + 2):
                if p < PAIRS:
                    shift(p)
                if p >= 2:
                    finish_y(p - 2)
            V.memset(yqT[:, :, T:TP], 0.0).then_inc(S("yqpad"), 1)
            dve.wait_ge(S("yT_mm"), 2)
            V.tensor_copy(yqT[:, 1, 0:T].rearrange("p (a b n) -> p a b n", a=PAIRS, b=2),
                          bank(2, 2).rearrange("p (a b n) -> p a b n", a=PAIRS, b=2)[:, :, :, 0:N]
                          ).then_inc(S("yT"), 1)
            for t in range(TT):
                dve.wait_ge(S("wo_mm"), min(TT, t // 2 * 2 + 2))
                last = V.tensor_tensor(h[:, t, :], h[:, t, :], bank(4 + t // 2)[:, (t % 2) * D:(t % 2 + 1) * D],
                                       ALU.add)
            link(last)

            def norm_T(norm, src, dst, stage, scale=None, keep=None):
                norm(src, dst).then_inc(S("xn"), 1)
                dve.wait_ge(S("nT_mm"), stage)
                if scale is None:
                    V.tensor_copy(xnT[:, 1, :], bank(6, 2)[:, 0:TP]).then_inc(S("nT"), 1)
                else:
                    V.tensor_scalar(xnT[:, 1, :], bank(6, 2)[:, 0:TP], scale, None,
                                    ALU.mult).then_inc(S("nT"), 1)

            norm_T(layernorm, h, xn, 1)

            dve.wait_ge(S("lg_mm"), 1)
            link(V.tensor_tensor(lg[:, :, :], bank(0)[:, 0:TT * E].rearrange("p (t e) -> p t e", e=E),
                                 sml[:, S_RB:S_RB + E].unsqueeze(1).to_broadcast([P, TT, E]), ALU.add))
            link(V.reduce_max(lmx[:, :], lg[:, :, :], AX_X))
            V.tensor_tensor(lg[:, :, :], lg[:, :, :], lmx[:, :].unsqueeze(2).to_broadcast([P, TT, E]),
                            ALU.subtract).then_inc(S("lg_shift"), 1)
            dve.wait_ge(S("lg_exp"), 1)
            link(V.reduce_sum(lmx[:, :], lg[:, :, :], AX_X))
            link(V.reciprocal(lmx[:, :], lmx[:, :]))
            link(V.tensor_tensor(lg[:, :, :], lg[:, :, :], lmx[:, :].unsqueeze(2).to_broadcast([P, TT, E]),
                                 ALU.mult))
            lt = cst[:, C_LT:C_LT + E * E].rearrange("p (e f) -> p e f", e=E)
            for t in range(TT):
                mine = lg[:, t, :].unsqueeze(2).to_broadcast([P, E, E])
                other = lg[:, t, :].unsqueeze(1).to_broadcast([P, E, E])
                V.tensor_tensor(gt[:, t], other, mine, ALU.is_gt)
                link(V.tensor_tensor(eq[:, t], other, mine, ALU.is_equal))
                link(V.tensor_tensor(eq[:, t], eq[:, t], lt, ALU.mult))
                link(V.tensor_tensor(gt[:, t], gt[:, t], eq[:, t], ALU.add))
            link(V.reduce_sum(rank[:, :, :], gt[:, :, :, :], AX_X))
            link(V.tensor_scalar(rank[:, :, :], rank[:, :, :], 2.0, None, ALU.is_lt))
            link(V.tensor_tensor(lg[:, :, :], lg[:, :, :], rank[:, :, :], ALU.mult))
            link(V.reduce_sum(lmx[:, :], lg[:, :, :], AX_X))
            link(V.tensor_scalar(lmx[:, :], lmx[:, :], 1e-20, None, ALU.add))
            link(V.reciprocal(lmx[:, :], lmx[:, :]))
            link(V.tensor_tensor(wts[:, 1:E + 1, :].rearrange("p e t -> p t e"), lg[:, :, :],
                                 lmx[:, :].unsqueeze(2).to_broadcast([P, TT, E]), ALU.mult))
            V.memset(hid[:, :, T:TP], 0.0).then_inc(S("hidpad"), 1)

            def hidden(u, base):
                c, hf = u // 2, u % 2
                w = P if c < FC - 1 else FL
                dve.wait_ge(S("silu"), base + u + 1)
                V.tensor_tensor(hid[0:w, c, hf * HT:(hf + 1) * HT], gact[u % 2][0:w, :],
                                bank(2 * (u % 2) + 1)[0:w, 0:HT], ALU.mult).then_inc(S("hid"), 1)

            def collect(e, scalars):
                dve.wait_ge(S("expert_done"), e + 1)
                for t in range(TT):
                    last = V.scalar_tensor_tensor(
                        h[:, t, :], bank(4 + t // 2)[:, (t % 2) * D:(t % 2 + 1) * D],
                        scalars[:, t:t + 1], h[:, t, :], ALU.mult, ALU.add)
                last.then_inc(S("collected"), 1)

            for u in range(2 * FC):
                hidden(u, 0)
            with dve.Fori(0, E) as i:
                base = (i + 1) * (2 * FC)
                for u in range(2 * FC):
                    hidden(u, base)
                    if u == 1:
                        collect(i, wts[:, i, :])
            collect(E, wts[:, E, :])
            dve.wait_ge(S("collected"), E + 1)

            def l1(li):
                src = h if li == 0 else xres
                if li == 0:
                    link(layernorm(h, xres))
                norm_T(rmsnorm, xres, xn, li + 2,
                       scale=sml[:, (S_N1, S_N2)[li] + 1:(S_N1, S_N2)[li] + 2])
                if li == 0:
                    link(V.memset(kf, 0.0))
                    V.memset(vo[:, :, :, DH:R], 1.0).then_inc(S("vo1"), 1)
                cs = cst[:, (C_CSG, C_CSL)[li]:(C_CSG, C_CSL)[li] + N]
                dve.wait_ge(S("v1_mm"), li + 1)
                V.tensor_copy(vo[:, :, :, 0:DH].rearrange("p a g d -> p (a g) d"),
                              bank(7)[:, 0:PAIRS * KV * DH].rearrange("p (c d) -> p c d", d=DH)
                              ).then_inc(S("vo"), 1)
                U = 2 * U5
                for u in range(U):
                    dve.wait_ge(S("qk_mm"), U * li + u + 1)
                    V.tensor_tensor(qk[:, u // 2, (u % 2) * HT:(u % 2 + 1) * HT].rearrange("p (b n) -> p b n", n=N),
                                    bank(u % 4)[:, 0:HT].rearrange("p (b n) -> p b n", n=N),
                                    cs.unsqueeze(1).to_broadcast([P, 8, N]), ALU.mult).then_inc(S("qkcs"), 1)
                for u in range(U):
                    s = (slice(None), u // 2, slice((u % 2) * HT, (u % 2 + 1) * HT))
                    dve.wait_ge(S("rt"), U * li + u + 1)
                    link(V.reciprocal(sqr[s], sqr[s]))
                    V.tensor_tensor(qk[s], qk[s], sqr[s], ALU.mult).then_inc(S("qkn"), 1)

                def mask(grp):
                    for g in range(KV):
                        dve.wait_ge(S("ex"), 16 * li + 4 * grp + g + 1)
                        x = ex[grp % 2][:, g, :].rearrange("p (c n) -> p c n", n=N)
                        V.tensor_tensor(x, x, cst[:, C_MASK:C_MASK + N].unsqueeze(1).to_broadcast([P, 8, N]),
                                        ALU.mult).then_inc(S("exm"), 1)

                def divide(grp):
                    dve.wait_ge(S("o"), 8 * li + 2 * grp + 2)
                    s = (slice(None), slice(None), slice(grp * 4 * N, (grp + 1) * 4 * N))
                    link(V.stream_shuffle(zs[s], oz[s], [DH + i % DH for i in range(32)]))
                    link(V.reciprocal(zs[s], zs[s]))
                    V.tensor_tensor(ozp[s], oz[s], zs[s], ALU.mult).then_inc(S("on"), 1)

                for grp in range(4):
                    mask(grp)
                    if grp >= 1:
                        divide(grp - 1)
                divide(3)
                for t in range(TT):
                    dve.wait_ge(S("wo1_mm"), TT * li + min(TT, t // 2 * 2 + 2))
                    last = V.tensor_tensor(xres[:, t, :], xres[:, t, :],
                                           bank(t // 2)[:, (t % 2) * D:(t % 2 + 1) * D], ALU.add)
                link(last)

            l1(0)
            l1(1)
            link(V.tensor_tensor(h[:, :, :], h[:, :, :], xres[:, :, :], ALU.add))
            dve.wait_ge(S("d_l1"), 16 * 9)
            link(V.tensor_scalar(wfs[:, :, :], wfin_s[:, :, :], 0.0, 2.0, ALU.is_ge, ALU.mult))
            V.tensor_scalar(wfs[:, :, :], wfs[:, :, :], 1.0, None, ALU.subtract).then_inc(S("wfs"), 1)
            norm_T(layernorm, h, xn, 4)
            for t in range(TT):
                dve.wait_ge(S("fin_mm"), min(TT, t // 2 * 2 + 2))
                link(V.tensor_tensor(xn[:, t, :], bank(t // 2)[:, (t % 2) * D:(t % 2 + 1) * D],
                                     sml[:, S_SC:S_SC + D], ALU.mult))
                link(V.tensor_tensor(xn[:, t, :], xn[:, t, :], sml[:, S_BI:S_BI + D], ALU.add))
                link(V.tensor_scalar(xn[:, t, :], xn[:, t, :], -100.0, 100.0, ALU.max, ALU.min))
                V.tensor_tensor(h[:, t, :], h[:, t, :], xn[:, t, :], ALU.add).then_inc(S("out_ready"), 1)

        @block.gpsimd
        def _(pool):
            pool.wait_ge(S("d_cst"), 16)
            for n in range(NORMS):
                pool.wait_ge(S("var"), n + 1)
                nc.gpsimd.tensor_tensor(rstd[:, :], vtmp[:, :], cst[:, C_HALF:C_HALF + TT],
                                        ALU.pow).then_inc(S("rstd"), 1)

        @block.tensor
        def _(pe):
            M = nc.tensor.matmul
            pe.wait_ge(S("dve_chain"), 1)
            pe.wait_ge(S("d_cst"), 16)
            pe.wait_ge(S("wabs"), 1)
            for k in range(DC):
                M(bank(5)[:, 0:H * R], ones, wabs[:, k, :], start=(k == 0), stop=(k == DC - 1))
            for j in range(H):
                for k in range(DC):
                    for q in range(4):
                        last = M(bank(6)[32 * q:32 * q + 32, j:j + 1], wabs[:, k, R * j:R * j + R],
                                 ones[:, 0:1], start=(k == 0), stop=(k == DC - 1), skip_group_check=True)
            last.then_inc(S("wabs_used"), 1)
            pe.wait_ge(S("d_u2t"), 16)
            for q in range(4):
                last = M(bank(7)[32 * q:32 * q + 32, 0:R], u2t_s[:, :], u2t_s[:, :], start=True, stop=True)
            last.then_inc(S("m2_mm"), 1)

            for c in range(PC):
                pe.wait_ge(S("d_x"), 32 * (c + 1))
                for t in range(TT):
                    M(bank(t)[:, 0:D], xT_s[:, c, t * P:(t + 1) * P], tokW_s[:, c, :],
                      start=(c == 0), stop=False)
            pe.wait_ge(S("d_pos"), 32)
            for t in range(TT):
                M(bank(t)[:, 0:D], sel_s[0:POSK, t * P:(t + 1) * P], posb_s[0:POSK, :],
                  start=False, stop=True).then_inc(S("tok"), 1)

            pe.wait_ge(S("wabs"), 2)
            pe.wait_ge(S("sq0"), 1)
            for k in range(DC):
                last = M(bank(5)[:, 0:D], ones, wabs[:, k, 0:D], start=(k == 0), stop=(k == DC - 1))
            last.then_inc(S("wosum"), 1)

            pe.wait_ge(S("xq"), 1)
            pe.wait_ge(S("wo0q"), 1)
            pe.wait_ge(S("identb"), 1)
            for k in range(DC):
                for t in range(TT):
                    last = nc.tensor.transpose(psb[:, (5 + k) * 2 * BK + t * P:(5 + k) * 2 * BK + (t + 1) * P],
                                               xq[:, t, k * P:(k + 1) * P], identb[:, :])
                last.then_inc(S("xq_t"), 1)
            pe.wait_ge(S("dg"), 1)
            M(bank(3), ones, dg[:, 0:4, :].rearrange("p a b -> p (a b)"), start=True, stop=True)
            M(bank(4)[:, 0:P], ones, dg[:, 4, :], start=True, stop=True).then_inc(S("mab_mm"), 1)
            pe.wait_ge(S("xqT"), 2)
            pe.wait_ge(S("mab"), 1)
            for j in range(H):
                for q in range(4):
                    for k in range(DC):
                        last = M(ps[32 * q:32 * q + 32, (j // 3) * BK + (j % 3) * G4T:(j // 3) * BK + (j % 3 + 1) * G4T],
                                 sq0[:, k, R * j:R * j + R], xqT[:, k, q * G4T:(q + 1) * G4T],
                                 start=(k == 0), stop=(k == DC - 1), skip_group_check=True)
                if j % 3 == 2 or j == H - 1:
                    last.then_inc(S("pr_mm"), 1)
            pe.wait_ge(S("m2"), 1)
            pe.wait_ge(S("qcs"), 1)
            for c in range(5):
                w = min(BK, G4 - c * BK)
                if c >= 2:
                    pe.wait_ge(S("qf"), c - 1)
                M(bank(4 + c % 2)[:, 0:w], m2[:, :], qcs[:, c * BK:c * BK + w],
                  start=True, stop=True).then_inc(S("qf_mm"), 1)
            pe.wait_ge(S("pr"), 1)
            for b in range(B4):
                if b >= 2:
                    pe.wait_ge(S("v"), b - 1)
                for g in range(HG):
                    last = nc.tensor.transpose(
                        ps[0:2 * N, 2 * (b % 2) * BK + g * P:2 * (b % 2) * BK + (g + 1) * P],
                        pr[:, b * T + 2 * N * g:b * T + 2 * N * (g + 1)], ident)
                last.then_inc(S("v_mm"), 1)

            def scores(p):
                q = p // 2
                if p == 0:
                    pe.wait_ge(S("qf"), 5)
                    pe.wait_ge(S("kcs"), 1)
                if p < 2:
                    pe.wait_ge(S("v"), 4)
                else:
                    pe.wait_ge(S("shifted"), p - 1)
                for j in range(H):
                    for par in range(2):
                        b = 2 * (p % 2) + par
                        last = M(ps[64 * par:64 * par + N, (2 * (p % 2) + j // 8) * BK + (j % 8) * N:
                                    (2 * (p % 2) + j // 8) * BK + (j % 8 + 1) * N],
                                 qf[32 * q:32 * q + 32, (b * H + j) * N:(b * H + j + 1) * N],
                                 kcs[32 * q:32 * q + 32, b * T + j * N:b * T + (j + 1) * N],
                                 start=True, stop=True, skip_group_check=True)
                last.then_inc(S("sc_mm"), 1)

            def probs_T(p):
                pe.wait_ge(S("expd"), p + 1)
                if p >= 1:
                    pe.wait_ge(S("pt"), p)
                for g in range(HG):
                    last = nc.tensor.transpose(ps[0:2 * N, 4 * BK + g * P:4 * BK + (g + 1) * P],
                                               pe_[p % 2][:, 2 * N * g:2 * N * (g + 1)], ident)
                last.then_inc(S("pt_mm"), 1)

            def values(p):
                pe.wait_ge(S("pt"), p + 1)
                if p >= 2:
                    pe.wait_ge(S("y"), p - 1)
                for g in range(HG):
                    for par in range(2):
                        o = ((2 * p + par) * HG + g) * 2 * VW
                        last = M(ps[64 * par:64 * par + N, (6 + p % 2) * BK + 2 * VW * g:(6 + p % 2) * BK + 2 * VW * (g + 1)],
                                 ptT[p % 2][0:2 * N, g * P + 64 * par:g * P + 64 * par + N],
                                 vbd[0:2 * N, o:o + 2 * VW], start=True, stop=True, skip_group_check=True)
                last.then_inc(S("y_mm"), 1)

            for p in range(PAIRS + 1):
                if p < PAIRS:
                    scores(p)
                if p == PAIRS - 1:
                    pass
                if p >= 1:
                    probs_T(p - 1)
                    values(p - 1)
            pe.wait_ge(S("yq"), PAIRS)
            for k in range(DC):
                for p in range(PAIRS):
                    last = nc.tensor.transpose(ps[:, 2 * k * BK + p * P:2 * k * BK + (p + 1) * P],
                                               yq[:, p, k * P:(k + 1) * P], ident)
                last.then_inc(S("yT_mm"), 1)
            pe.wait_ge(S("yT"), 2)
            pe.wait_ge(S("yqpad"), 1)
            for t in range(TT):
                for k in range(DC):
                    last = M(bank(4 + t // 2)[:, (t % 2) * D:(t % 2 + 1) * D], yqT[:, k, t * P:(t + 1) * P],
                             wo0q[:, k, :], start=(k == 0), stop=(k == DC - 1), skip_group_check=True)
                last.then_inc(S("wo_mm"), 1)

            def transposes(stage):
                pe.wait_ge(S("xn"), stage)
                for k in range(DC):
                    for t in range(TT):
                        last = nc.tensor.transpose(ps[:, (4 + 2 * k) * BK + t * P:(4 + 2 * k) * BK + (t + 1) * P],
                                                   xn[:, t, k * P:(k + 1) * P], ident)
                last.then_inc(S("nT_mm"), 1)

            transposes(1)
            pe.wait_ge(S("nT"), 2)
            pe.wait_ge(S("d_rw"), 16)
            for t in range(TT):
                for k in range(DC):
                    last = M(bank(0)[:, t * E:(t + 1) * E], xnT[:, k, t * P:(t + 1) * P], rw_s[:, k, :],
                             start=(k == 0), stop=(k == DC - 1), skip_group_check=True)
            last.then_inc(S("lg_mm"), 1)

            def gate_up(u, base, w):
                c, hf = u // 2, u % 2
                m = P if c < FC - 1 else FL
                if base is not 0 or u >= 2:
                    pe.wait_ge(S("hid"), base + u - 1)
                for part in range(2):
                    for k in range(DC):
                        o = (part * DC + k) * F + c * P
                        last = M(bank(2 * (u % 2) + part)[0:m, 0:HT], w[:, o:o + m],
                                 xnT[:, k, hf * HT:(hf + 1) * HT], start=(k == 0), stop=(k == DC - 1))
                last.then_inc(S("gu"), 1)

            def down(c, need, w):
                m = P if c < FC - 1 else FL
                pe.wait_ge(S("hid"), need)
                o = 2 * DC * F + c * D
                for t in range(TT):
                    last = M(bank(4 + t // 2)[:, (t % 2) * D:(t % 2 + 1) * D], hid[0:m, c, t * P:(t + 1) * P],
                             w[0:m, o:o + D], start=(c == 0 and t % 2 == 0), stop=(c == FC - 1),
                             skip_group_check=True)
                if c == FC - 1:
                    last.then_inc(S("expert_done"), 1)

            pe.wait_ge(S("lg_shift"), 1)
            pe.wait_ge(S("d_wexp0"), 16)
            pe.wait_ge(S("hidpad"), 1)
            for c in range(FC):
                for hf in range(2):
                    gate_up(2 * c + hf, 0, wbuf[0])
                if c >= 1:
                    down(c - 1, 2 * c, wbuf[0])
            with pe.Fori(0, E // 2) as i:
                for half in range(2):
                    base = (2 * i + half + 1) * (2 * FC)
                    w, prev = wbuf[1 - half], wbuf[half]
                    if half == 0:
                        pe.wait_ge(S("d_wexp1"), 16 * i + 16)
                    else:
                        pe.wait_ge(S("d_wexp0"), 16 * i + 32)
                    for c in range(FC):
                        for hf in range(2):
                            gate_up(2 * c + hf, base, w)
                        if c == 0:
                            down(FC - 1, base, prev)
                        if c == 1:
                            pe.wait_ge(S("collected"), 2 * i + half + 1)
                        if c >= 1:
                            down(c - 1, base + 2 * c, w)
            down(FC - 1, 2 * FC * (E + 1), wbuf[0])

            def l1(li):
                w = wl1["gl"[li]]
                transposes(li + 2)
                pe.wait_ge(S("nT"), 2 * (li + 2))
                if li == 0:
                    pe.wait_ge(S("d_l1"), 16 * 9)
                    for hf in range(2):
                        for k in range(DC):
                            last = M(bank(4 + hf)[0:LAT, 0:HT], kvd_s[:, k, :], xnT[:, k, hf * HT:(hf + 1) * HT],
                                     start=(k == 0), stop=(k == DC - 1))
                        last.then_inc(S("lat_mm"), 1)
                    pe.wait_ge(S("lat"), 2)
                    pe.wait_ge(S("vo1"), 1)
                for b in range(B):
                    dst = bank(7)[64 * (b % 2):64 * (b % 2) + 64, (b // 2) * LAT:(b // 2 + 1) * LAT]
                    if li == 0:
                        last = M(dst, latT[:, b * N:b * N + 64], vug_s[:, :], start=True, stop=True,
                                 skip_group_check=True)
                    else:
                        for k in range(DC):
                            last = M(dst, xnT[:, k, b * N:b * N + 64], wvl_s[:, k, :], start=(k == 0),
                                     stop=(k == DC - 1), skip_group_check=True)
                last.then_inc(S("v1_mm"), 1)
                U = 2 * U5

                def mean_sq(u):
                    pe.wait_ge(S("sqr"), U * li + u + 1)
                    if u == 3:
                        pe.wait_ge(S("vo"), li + 1)
                    if u >= 4:
                        pe.wait_ge(S("rt"), U * li + u - 3)
                    M(bank(4 + u % 4)[:, 0:HT], mean16, sqr[:, u // 2, (u % 2) * HT:(u % 2 + 1) * HT],
                      start=True, stop=True).then_inc(S("ms_mm"), 1)

                for u in range(U):
                    hf = u % 2
                    if u >= 4:
                        pe.wait_ge(S("qkcs"), U * li + u - 3)
                    dst = bank(u % 4)[:, 0:HT]
                    if li == 0 and u // 2 == KV:
                        last = M(dst, kug_s[:, :], latT[:, hf * HT:(hf + 1) * HT], start=True, stop=True)
                    else:
                        for k in range(DC):
                            last = M(dst, w["wq"][:, k, u // 2, :], xnT[:, k, hf * HT:(hf + 1) * HT],
                                     start=(k == 0), stop=(k == DC - 1))
                    last.then_inc(S("qk_mm"), 1)
                    if u >= 2:
                        mean_sq(u - 2)
                mean_sq(U - 2)
                mean_sq(U - 1)
                for hf in range(2):
                    pe.wait_ge(S("qkn"), U * li + U - 1 + hf)
                    M(bank(4 + hf)[:, 0:HT], fold, qk[:, KV, hf * HT:(hf + 1) * HT],
                      start=True, stop=True).then_inc(S("kf_mm"), 1)
                pe.wait_ge(S("kf"), 2 * (li + 1))

                def scores(grp, g):
                    if grp >= 1:
                        pe.wait_ge(S("ex"), 16 * li + 4 * (grp - 1) + g + 1)
                    for a in range(2):
                        for par in range(2):
                            b = 2 * (2 * grp + a) + par
                            last = M(ps[64 * par:64 * par + 64, g * BK + a * 4 * N:g * BK + (a + 1) * 4 * N],
                                     kf[32 * g:32 * g + 32, b * N:b * N + 64],
                                     qk[32 * g:32 * g + 32, 0:KV, b * N:(b + 1) * N],
                                     start=True, stop=True, skip_group_check=True)
                    last.then_inc(S("s_mm"), 1)

                def values(grp):
                    if grp >= 2:
                        pe.wait_ge(S("o"), 8 * li + 2 * (grp - 1))
                    for par in range(2):
                        pe.wait_ge(S("exm"), 16 * li + 4 * grp + 4)
                        for g in range(KV):
                            for a in range(2):
                                last = M(ps[32 * g:32 * g + 32, (4 + 2 * (grp % 2) + par) * BK + a * 4 * N:
                                            (4 + 2 * (grp % 2) + par) * BK + (a + 1) * 4 * N],
                                         vo[64 * par:64 * par + N, 2 * grp + a, g, :],
                                         ex[grp % 2][64 * par:64 * par + N, g, a * 4 * N:(a + 1) * 4 * N],
                                         start=True, stop=True, skip_group_check=True)
                        last.then_inc(S("o_mm"), 1)

                for grp in range(5):
                    if grp < 4:
                        for g in range(KV):
                            scores(grp, g)
                    if grp >= 1:
                        values(grp - 1)
                pe.wait_ge(S("on"), 4 * (li + 1))
                for t in range(TT):
                    for g in range(KV):
                        last = M(bank(t // 2)[:, (t % 2) * D:(t % 2 + 1) * D], ozp[:, g, t * P:(t + 1) * P],
                                 w["wo"][:, g, :], start=(g == 0), stop=(g == KV - 1), skip_group_check=True)
                    last.then_inc(S("wo1_mm"), 1)

            l1(0)
            l1(1)
            transposes(4)
            pe.wait_ge(S("nT"), 8)
            pe.wait_ge(S("wfs"), 1)
            for t in range(TT):
                for k in range(DC):
                    last = M(bank(t // 2)[:, (t % 2) * D:(t % 2 + 1) * D], xnT[:, k, t * P:(t + 1) * P],
                             wfs[:, k, :], start=(k == 0), stop=(k == DC - 1), skip_group_check=True)
                last.then_inc(S("fin_mm"), 1)


def constants():
    c = np.zeros((P, CW), np.float32)
    c[:, C_ID:C_ID + P] = np.eye(P)
    c[:, C_ONE:C_ONE + P] = 1.0
    p = np.arange(P)
    same = (p[:, None] // R) == (p[None, :] // R)
    c[:, C_FOLD:C_FOLD + P] = same & ((p[:, None] % DH) == (p[None, :] % DH))
    c[:, C_MEAN:C_MEAN + P] = np.where(same, 1.0 / DH, 0.0)
    half = DH // 2

    def rotary(base, pos):
        inv = (np.float32(1.0) / np.float32(base) ** (np.arange(half, dtype=np.float32) / np.float32(half)))
        ang = pos.astype(np.float32)[:, None] * inv.astype(np.float32)[None, :]
        cos, sin = np.cos(ang).T, np.sin(ang).T
        return np.tile(np.concatenate([cos, cos, -sin, sin]), (BG, 1))

    c[:, C_CSQ:C_CSQ + N] = rotary(10000.0, np.arange(N))
    c[:, C_CSK:C_CSK + T] = rotary(10000.0, np.arange(T) % N)
    c[:, C_CSG:C_CSG + N] = rotary(1000000.0, np.arange(N))
    c[:, C_CSL:C_CSL + N] = rotary(10000.0, np.arange(N))
    c[:, C_MASK:C_MASK + N] = (p[:, None] % 64) <= np.arange(N)[None, :]
    c[:, C_HM] = p < N
    c[:, C_HM + 1] = (p >= N) & (p < 2 * N)
    c[:, C_HALF:C_HALF + TT] = -0.5
    c[:, C_LT:C_LT + E * E] = np.tril(np.ones((E, E)), -1).reshape(-1)
    c[:, C_EPS] = RMS_EPS
    s = np.zeros((POSK, TP), np.float32)
    for n in range(N):
        s[n, n:T:N] = 1.0
    s[N, 0:T] = 1.0
    s[N, 0:T:N] = 0.0
    s[N + 1, 0:T:N] = 1.0
    return c, s


def layout(i):
    def arr(n):
        return np.asarray(i[n])

    def chunks(w):
        return np.ascontiguousarray(w.reshape(-1, P, w.shape[1]).transpose(1, 0, 2))

    const, sel = constants()
    out = {"const": const, "sel": sel}
    g = 96 // 16
    x = arr("x").reshape(B, 3, g, 16, g, 16).transpose(1, 3, 5, 0, 2, 4).reshape(PC * P, B, g * g)
    xt = np.zeros((PC * P, TP), np.float32)
    xt[:, 0:T].reshape(PC * P, B, N)[:, :, 1:] = x
    out["xT"] = chunks(xt)
    out["tokW"] = chunks(arr("L0_tok_W").T)
    out["posb"] = np.concatenate([arr("L0_tok_pos_enc")[0], arr("L0_tok_b")[None], arr("L0_tok_cls_token")[0]])

    even, odd = np.arange(0, DH, 2), np.arange(1, DH, 2)
    rows = np.concatenate([even, odd, odd, even])
    perm = np.concatenate([even, odd])
    wq = arr("L0_attn_Wqkv_w").reshape(H, DH, D)[:, rows, :]
    out["wq0"] = chunks(wq.reshape(H * R, D).T)
    bq = arr("L0_attn_Wqkv_b").reshape(H, DH)[:, rows].T
    out["u2t"] = np.concatenate([arr("L0_attn_U")] * 2).T
    wo = arr("L0_attn_Wo_w").T.reshape(H, DH, D)[:, perm, :].reshape(D, D)
    out["wo0"] = chunks(wo)
    sm = np.zeros((P, SW), np.float32)
    sm[:, S_BQ:S_BQ + H] = np.tile(bq, (BG, 1))
    sm[:, S_N1:S_N1 + DC] = arr("L1_attn_norm1_w").reshape(DC, P).T
    sm[:, S_N2:S_N2 + DC] = arr("L1_attn_norm2_w").reshape(DC, P).T
    sm[:, S_SC:S_SC + D] = arr("L1_ffn_scale")
    sm[:, S_BI:S_BI + D] = arr("L1_ffn_bias")
    sm[:, S_RB:S_RB + E] = arr("L0_ffn_router_b")
    out["small"] = sm
    out["rw"] = chunks(arr("L0_ffn_router_w"))

    gw = np.concatenate([arr("L0_ffn_sh_gate_w")[None], arr("L0_ffn_gate_w")])
    uw = np.concatenate([arr("L0_ffn_sh_up_w")[None], arr("L0_ffn_up_w")])
    dw = np.concatenate([arr("L0_ffn_sh_down_w")[None], arr("L0_ffn_down_w")])
    we = np.zeros((E + 1, P, WX), np.float32)
    for e in range(E + 1):
        we[e, :, 0:DC * F] = chunks(gw[e]).reshape(P, -1)
        we[e, :, DC * F:2 * DC * F] = chunks(uw[e]).reshape(P, -1)
        d = np.zeros((FC * P, D), np.float32)
        d[0:F] = dw[e]
        we[e, :, 2 * DC * F:] = chunks(d).reshape(P, -1)
    out["wexp"] = we

    def qrot(w):
        k = w.reshape(w.shape[0], KV, -1, DH)[:, :, :, rows].transpose(0, 2, 1, 3)
        return k.reshape(w.shape[0], -1, KV * R)

    def c3(w):
        return np.ascontiguousarray(w.reshape(-1, P, w.shape[1], w.shape[2]).transpose(1, 0, 2, 3))

    def wo1(w):
        z = np.zeros((KV, R, 4, D), np.float32)
        z[:, 0:DH] = w.reshape(KV, 4, DH, D).transpose(0, 2, 1, 3)
        return z.reshape(P, 4, D)

    out["wqg"] = c3(qrot(arr("L1_attn_g_wq")))
    out["kvd"] = chunks(arr("L1_attn_g_kv_down"))
    out["kug"] = qrot(arr("L1_attn_g_k_up"))[:, 0]
    out["vug"] = arr("L1_attn_g_v_up")
    out["wog"] = wo1(arr("L1_attn_g_wo"))
    out["wql"] = c3(np.concatenate([qrot(arr("L1_attn_l_wq")), qrot(arr("L1_attn_l_wk"))], 1))
    out["wvl"] = chunks(arr("L1_attn_l_wv"))
    out["wol"] = wo1(arr("L1_attn_l_wo"))
    out["wfin"] = chunks(arr("L1_ffn_weights").T)
    return {k: np.ascontiguousarray(v) for k, v in out.items()}


_NAMES = ["xT", "tokW", "sel", "posb", "const", "small", "wq0", "u2t", "wo0", "rw", "wexp",
          "wqg", "kvd", "kug", "vug", "wog", "wql", "wvl", "wol", "wfin"]
DEBUG = []


def kernel(**inputs):
    import concourse.bacc as _bacc
    from concourse.bass_utils import run_bass_kernel_spmd as _run

    nc = _bacc.Bacc("TRN2", target_bir_lowering=False, num_devices=1)
    laid = layout(inputs)
    arrays, args = {}, []
    for name in _NAMES:
        arrays[f"in_{name}"] = laid[name]
        args.append(nc.dram_tensor(f"in_{name}", laid[name].shape, F32, kind="ExternalInput").ap())
    out = nc.dram_tensor("out_0", (T, D), F32, kind="ExternalOutput").ap()
    tower(nc, *args, out, None)
    r = _run(nc, [arrays], core_ids=[0])
    return r.results[0]["out_0"].reshape(B, N, D)
```

```python
from contextlib import ExitStack

import numpy as np

import concourse.bass as bass
from concourse import mybir

F32 = mybir.dt.float32
FR = mybir.dt.float32r
I32 = mybir.dt.int32
BF16 = mybir.dt.bfloat16
ALU = mybir.AluOpType
ACT = mybir.ActivationFunctionType
AX_X = mybir.AxisListType.X

P = 128
B = 16
N = 37
D = 256
DC = D // P
T = B * N
TT = -(-T // P)
TP = TT * P
HT = T // 2
PC = 6
POSK = N + 2
H = 16
DH = D // H
R = 2 * DH
BG = 4
B4 = B // BG
G4T = B4 * N
PAIRS = B // 2
HG = 8
KV = 4
KS = 64
LAT = 64
E = 8
F = 688
FC = -(-F // P)
FP = FC * P
WPART = (DC * FP, DC * FP, FC * D)
WOFF = (0, DC * FP, 2 * DC * FP)
WX = sum(WPART)
CAP = 256
CT = CAP // P
SU = 2 * FC
MAGIC = 1.5 * 2.0 ** 23
LN_EPS = 1e-5
RMS_EPS = 1e-6
NORMS = 6
BK = 512

C_ID, C_ONE, C_FOLD, C_MEAN = 0, P, 2 * P, 3 * P
C_PICK = 4 * P
EARLY = C_PICK + R
C_CSQ = EARLY
C_CSK = C_CSQ + N
C_CSG = C_CSK + T
C_CSL = C_CSG + N
C_MASK = C_CSL + N
C_HM = C_MASK + N
C_HALF = C_HM + 2
C_LT = C_HALF + 5
C_EPS = C_LT + E * E
C_TRI = C_EPS + 1
C_IOTA = C_TRI + P
C_VALID = C_IOTA + CAP
CW = C_VALID + TT

S_BQ = 0
S_N1 = S_BQ + H
S_N2 = S_N1 + DC
S_SC = S_N2 + DC
S_BI = S_SC + D
S_RB = S_BI + D
SW = S_RB + E


def tower(nc, xT, tokW, sel, posb, const, small, wq0, u2t, wo0, rw, wexp,
          wqg, kvd, kug, vug, wog, wql, wvl, wol, wfin, out, dbg):
    ctx = ExitStack()
    with ctx:
        def sb(name, shape, dt=F32):
            return ctx.enter_context(nc.sbuf_tensor(name, shape, dt))

        sems = {}

        def S(name):
            if name not in sems:
                sems[name] = ctx.enter_context(nc.semaphore(name))
            return sems[name]

        ps = ctx.enter_context(nc.psum_tensor("ps", [P, 8 * BK], F32))
        psb = ps[:, :].bitcast(BF16)

        def bank(i, n=1):
            return ps[:, i * BK:(i + n) * BK]

        cst = sb("cst", [P, CW])
        sml = sb("sml", [P, SW])
        ident = cst[:, C_ID:C_ID + P]
        ones = cst[:, C_ONE:C_ONE + P]
        fold = cst[:, C_FOLD:C_FOLD + P]
        mean16 = cst[:, C_MEAN:C_MEAN + P]
        identb = sb("identb", [P, P], BF16)

        h = sb("h", [P, TT, D])
        xn = sb("xn", [P, TT, D])
        xnT = sb("xnT", [P, DC, TP])
        stats = sb("stats", [P, TT, 6])
        mv = sb("mv", [P, TT, 2])
        rstd = sb("rstd", [P, TT])
        vtmp = sb("vtmp", [P, TT])

        xh, xl = sb("xh", [P, TT, D], FR), sb("xl", [P, TT, D], FR)
        xTh, xTl = sb("xTh", [P, DC, TP], FR), sb("xTl", [P, DC, TP], FR)
        raw = sb("raw", [P, WX])

        sq0 = sb("sq0", [P, DC, H * R], BF16)
        alq = sb("alq", [P, H])
        thr = sb("thr", [P, 4])
        u2t_s = sb("u2t_s", [R, R])
        m2 = sb("m2", [P, P])
        wo0_s = sb("wo0_s", [P, DC, D])
        wo0q = sb("wo0q", [P, DC, D])
        mab = sb("mab", [P, G4T])
        ma = sb("ma", [P, TT])
        mx = sb("mx", [P, 2, H])
        ma2 = sb("ma2", [P, PAIRS])
        rma = sb("rma", [P, PAIRS])
        rz = sb("rz", [P, 2, H])
        rw_s = sb("rw_s", [P, DC, E])
        lg = sb("lg", [P, TT, E])
        lmx = sb("lmx", [P, TT])
        gt = sb("gt", [P, TT, E, E])
        eq = sb("eq", [P, TT, E, E])
        sel_e = sb("sel_e", [P, TT, E])
        wts = sb("wts", [P, E, TT])
        wthl = sb("wthl", [P, E, TT, 2], FR)
        wover = sb("wover", [P, E, TT])
        off = sb("off", [P, TT + 1, E])
        slot = sb("slot", [P, E, TT])
        iota = sb("iota", [P, CAP], BF16)
        over = sb("over", [P, 1], I32)

        L0 = 25824
        stage0 = ExitStack()
        arena = stage0.enter_context(nc.sbuf_tensor("stage_l0", [P, L0], F32))
        stage0.close()
        expert_stage = ExitStack()

        def eb(name, shape, dt=FR):
            return expert_stage.enter_context(nc.sbuf_tensor(name, shape, dt))

        wset = [(eb(f"w{i}h", [P, WX]), eb(f"w{i}l", [P, WX])) for i in range(2)]
        hwork = eb("hwork", [P, 2 * FC * TP])
        sf = eb("sf", [P, TT, CAP])
        xg = [eb(f"xg{n}", [P, DC, CAP]) for n in "hl"]
        sbf = eb("sbf", [P, TT, CAP], BF16)
        gact = [eb(f"gact{i}", [P, HT], F32) for i in range(2)]
        h32 = [eb(f"h32_{i}", [P, HT], F32) for i in range(2)]
        y32 = eb("y32", [P, CT, D], F32)
        wcur = eb("wcur", [P, TT, 2])
        wsl = eb("wsl", [P, CT], F32)
        hs = [hwork[:, i * FC * TP:(i + 1) * FC * TP].rearrange("p (c t) -> p c t", c=FC) for i in range(2)]
        hr = [hwork[:, i * FC * CAP:(i + 1) * FC * CAP].rearrange("p (c t) -> p c t", c=FC) for i in range(2)]
        o = 2 * FC * CAP
        stf = hwork[:, o:o + CT * TP].rearrange("p (s t) -> p s t", s=CT)
        o += CT * TP
        yhl = [hwork[:, o + i * CT * D:o + (i + 1) * CT * D].rearrange("p (s d) -> p s d", s=CT)
               for i in range(2)]
        expert_stage.close()
        hidf = [xn[:, :, :].rearrange("p a b -> p (a b)")[:, i * TP:(i + 1) * TP] for i in range(2)]

        xT_s = arena[:, 0:PC * TP].rearrange("p (c t) -> p c t", c=PC)
        tokW_s = arena[:, PC * TP:PC * TP + PC * D].rearrange("p (c t) -> p c t", c=PC)
        o = PC * TP + PC * D
        sel_s = arena[:, o:o + TP]
        posb_s = arena[:, o + TP:o + TP + D]

        G4 = B4 * T // B * H
        VW = DH + 1
        at = {}
        o = 0
        for name, width in (("am", G4), ("pr", G4), ("qcs", G4), ("wq0", DC * H * R), ("wabs", DC * H * R),
                            ("sg", DC * H * R // 2), ("sgn", DC * H * R // 2), ("kcs", G4), ("qf", G4),
                            ("vbd", B * HG * 2 * VW), ("pe", 2 * H * N), ("pt", 2 * HG * P),
                            ("yq", PAIRS * D), ("yqT", DC * TP)):
            at[name] = arena[:, o:o + width]
            o += width
        assert o == L0
        am = at["am"]
        pr = at["pr"]
        qcs = at["qcs"]
        kcs = at["kcs"]
        qf = at["qf"]
        vbd = at["vbd"]
        wq0_s = at["wq0"].rearrange("p (c m) -> p c m", c=DC)
        wabs = at["wabs"].rearrange("p (c m) -> p c m", c=DC)
        sg = at["sg"].bitcast(BF16).rearrange("p (c m) -> p c m", c=DC)
        sgn = at["sgn"].bitcast(BF16).rearrange("p (c m) -> p c m", c=DC)
        pe_ = [at["pe"][:, i * H * N:(i + 1) * H * N] for i in range(2)]
        ptT = [at["pt"][:, i * HG * P:(i + 1) * HG * P] for i in range(2)]
        yq = at["yq"].rearrange("p (a d) -> p a d", a=PAIRS)
        yqT = at["yqT"].rearrange("p (c t) -> p c t", c=DC)
        xq = at["kcs"][:, 0:TT * D // 2].bitcast(BF16).rearrange("p (t d) -> p t d", t=TT)
        xqT = at["kcs"][:, TT * D // 2:TT * D // 2 + DC * TP // 2].bitcast(BF16).rearrange(
            "p (c t) -> p c t", c=DC)
        dg = at["qf"][:, 0:TT * P].rearrange("p (t q) -> p t q", t=TT)

        stage1 = ExitStack()

        def ab(name, shape, dt=F32):
            return stage1.enter_context(nc.sbuf_tensor(name, shape, dt))

        wl1 = {}
        for n in "gl":
            kd = KV + 1 if n == "l" else KV
            wl1[n] = dict(
                wq=ab(f"wq_{n}", [P, DC, kd, P]),
                wo=ab(f"wo_{n}", [P, KV, D]),
            )
        kvd_s = ab("kvd_s", [P, DC, LAT])
        kug_s = ab("kug_s", [LAT, P])
        vug_s = ab("vug_s", [LAT, KV * DH])
        wvl_s = ab("wvl_s", [P, DC, KV * DH])
        latT = ab("latT", [LAT, TP])
        xres = ab("xres", [P, TT, D])
        U5 = KV + 1
        arena_a = ab("stage_l1a", [P, 2 * U5 * T])
        km = ab("km", [P, B, KV // 2, 2, KS])
        vo = ab("vo", [P, B, KV // 2, 2, R])
        arena_b = ab("stage_l1b", [P, 2 * KV * 2 * 4 * N + 8 * T])
        qk = arena_a[:, 0:U5 * T].rearrange("p (u t) -> p u t", u=U5)
        sqr = arena_a[:, U5 * T:2 * U5 * T].rearrange("p (u t) -> p u t", u=U5)
        QT = 2 * 4 * N
        ex = [arena_b[:, i * KV * QT:(i + 1) * KV * QT].rearrange("p (g c) -> p g c", g=KV)
              for i in range(2)]
        oz = arena_b[:, 2 * KV * QT:2 * KV * QT + 4 * T].rearrange("p (u t) -> p u t", u=4)
        zs = arena_b[:, 2 * KV * QT + 4 * T:2 * KV * QT + 8 * T].rearrange("p (u t) -> p u t", u=4)
        ozp = ab("ozp", [P, KV, TP])

        wfin_s = ab("wfin_s", [P, DC, D])
        wfs = ab("wfs", [P, DC, D])

        stage1.close()

        def value_rows(b, k):
            src = bank(2 * (b % 2), 2)[0:2 * N].rearrange("p (g q r) -> p g q r", g=HG, q=BG)
            dst = vbd.rearrange("p (q b g k w) -> p b k g q w", q=BG, b=B4, g=HG, k=2)
            return dst[0:2 * N, b, k, :, :, 0:DH], src[:, :, :, 0:DH], cst[0:2 * N, C_HM + k:C_HM + k + 1]

        def own_keys(g, hf):
            return km[R * g:R * (g + 1), hf * B // 2:(hf + 1) * B // 2, g // 2, g % 2, 0:N]

        def folded(g, hf):
            return bank(4 + hf)[R * g:R * (g + 1), 0:HT].rearrange("p (b n) -> p b n", n=N)

        block = ctx.enter_context(nc.Block())

        @block.sync
        def _(sp):
            sp.dma_start(wq0_s[:, :, :], wq0).then_inc(S("d_wq0"), 16)
            sp.dma_start(cst[:, 0:EARLY], const[:, 0:EARLY]).then_inc(S("d_cst"), 16)
            for c in range(PC):
                sp.dma_start(xT_s[:, c, :], xT[:, c, :]).then_inc(S(f"d_x{c}"), 16)
                sp.dma_start(tokW_s[:, c, :], tokW[:, c, :]).then_inc(S(f"d_x{c}"), 16)
            sp.dma_start(cst[:, EARLY:CW], const[:, EARLY:CW]).then_inc(S("d_tables"), 16)

            def load(x, part):
                o = WOFF[part]
                sp.dma_start(raw[:, o:o + WPART[part]], wexp[x, :, o:o + WPART[part]]).then_inc(
                    S(f"d_raw{part}"), 16)

            for part in range(3):
                load(0, part)
            with sp.Fori(0, E) as i:
                for part in range(3):
                    sp.wait_ge(S("w_lo"), 3 * i + part + 1)
                    load(i + 1, part)
            sp.wait_ge(S("over"), 1)
            more = sp.value_load(over[0:1, 0:1])
            with sp.If(more > 0):
                sp.wait_ge(S("w_lo"), 3 * (E + 1))
                sp.dma_start(raw[:, :], wexp[1]).then_inc(S("f_raw"), 16)
                with sp.Fori(0, E - 1) as i:
                    sp.wait_ge(S("f_dn"), i + 1)
                    sp.dma_start(raw[:, :], wexp[i + 2]).then_inc(S("f_raw"), 16)
            sp.wait_ge(S("moe"), 1)
            for dst, src in ((kvd_s, kvd), (wl1["g"]["wq"], wqg), (wl1["g"]["wo"], wog),
                             (wl1["l"]["wq"], wql), (wvl_s, wvl), (wl1["l"]["wo"], wol),
                             (wfin_s, wfin)):
                sp.dma_start(dst[:], src).then_inc(S("d_l1"), 16)
            sp.dma_start(kug_s[:, :], kug).then_inc(S("d_l1"), 16)
            sp.dma_start(vug_s[:, :], vug).then_inc(S("d_l1"), 16)
            for t in range(TT):
                rows = min(P, T - t * P)
                sp.wait_ge(S("out_ready"), t + 1)
                sp.dma_start(out[t * P:t * P + rows, :], h[0:rows, t, :]).then_inc(S("d_out"), 16)
            sp.wait_ge(S("d_out"), 16 * TT)

        @block.scalar
        def _(act):
            A = nc.scalar.activation
            act.dma_start(sel_s[0:POSK, :], sel).then_inc(S("d_pos"), 16)
            act.dma_start(posb_s[0:POSK, :], posb).then_inc(S("d_pos"), 16)
            act.dma_start(sml[:, :], small).then_inc(S("d_sml"), 16)
            act.dma_start(u2t_s[:, :], u2t).then_inc(S("d_u2t"), 16)
            act.dma_start(wo0_s[:, :, :], wo0).then_inc(S("d_wo0"), 16)
            act.dma_start(rw_s[:, :, :], rw).then_inc(S("d_rw"), 16)
            act.wait_ge(S("d_wq0"), 16)
            A(wabs[:, :, :], wq0_s[:, :, :], ACT.Abs).then_inc(S("wabs"), 1)
            act.wait_ge(S("wabs_used"), 1)
            act.wait_ge(S("d_wo0"), 16)
            A(wabs[:, :, 0:D], wo0_s[:, :, :], ACT.Abs).then_inc(S("wabs"), 1)

            for t in range(TT):
                act.wait_ge(S("tok"), t + 1)
                A(h[:, t, :], bank(t)[:, 0:D], ACT.Copy).then_inc(S("h0"), 1)

            act.wait_ge(S("xq_t"), 1)
            A(xqT[:, 0, :], psb[:, 5 * 2 * BK:5 * 2 * BK + TP], ACT.Copy).then_inc(S("xqT"), 1)

            act.wait_ge(S("d_sml"), 16)
            for j in range(H):
                act.wait_ge(S("pr"), j // 3 + 1)
                head = pr.rearrange("p (t j) -> p j t", j=H)[:, j, :]
                A(head, head, ACT.Identity, bias=sml[:, S_BQ + j:S_BQ + j + 1]).then_inc(S("biased"), 1)

            def evac_v(b):
                act.wait_ge(S("v_mm"), b + 1)
                for k in range(2):
                    dst, src, hm = value_rows(b, k)
                    last = A(dst, src, ACT.Copy, scale=hm)
                last.then_inc(S("va"), 1)

            def evac_qf(c):
                w = min(BK, G4 - c * BK)
                act.wait_ge(S("qf_mm"), c + 1)
                A(qf[:, c * BK:c * BK + w], bank(4 + c % 2)[:, 0:w], ACT.Copy).then_inc(S("qf"), 1)

            act.wait_ge(S("d_tables"), 16)
            evac_v(1)
            for c in range(4):
                evac_qf(c)
            evac_v(3)
            evac_qf(4)

            def expo(p):
                act.wait_ge(S("shifted"), p + 1)
                A(pe_[p % 2], pe_[p % 2], ACT.Exp, scale=0.25).then_inc(S("expd"), 1)

            def evac_pt(p):
                act.wait_ge(S("pt_mm"), p + 1)
                if p >= 2:
                    act.wait_ge(S("y_mm"), p - 1)
                A(ptT[p % 2][0:2 * N, :], bank(4, 2)[0:2 * N, :], ACT.Copy).then_inc(S("pt"), 1)

            expo(0)
            for p in range(PAIRS):
                evac_pt(p)
                if p + 1 < PAIRS:
                    expo(p + 1)

            act.wait_ge(S("yT_mm"), 1)
            A(yqT[:, 0, 0:T].rearrange("p (a b n) -> p a b n", a=PAIRS, b=2),
              bank(0, 2).rearrange("p (a b n) -> p a b n", a=PAIRS, b=2)[:, :, :, 0:N],
              ACT.Copy).then_inc(S("yT"), 1)

            def evac_T(stage, scale):
                act.wait_ge(S("nT_mm"), stage)
                A(xnT[:, 0, :], bank(4, 2)[:, 0:TP], ACT.Copy if scale is None else ACT.Identity,
                  scale=1.0 if scale is None else scale).then_inc(S("nT"), 1)

            evac_T(1, None)
            act.wait_ge(S("nT"), 2)
            A(xTh[:, :, :], xnT[:, :, :], ACT.Copy).then_inc(S("xTh"), 1)

            act.wait_ge(S("lg_shift"), 1)
            A(lg[:, :, :], lg[:, :, :], ACT.Exp).then_inc(S("lg_exp"), 1)

            act.wait_ge(S("xn"), TT)
            A(xh[:, :, :], xn[:, :, :], ACT.Copy).then_inc(S("xh"), 1)

            def silu(base, u, n, src):
                act.wait_ge(S("gu"), base + u + 1)
                A(gact[u % 2][:, 0:n], src[:, 0:n], ACT.Silu).then_inc(S("silu"), 1)

            def hid_hi(base, u, n, dst):
                act.wait_ge(S("hm"), base + u + 1)
                A(dst, h32[u % 2][:, 0:n], ACT.Copy).then_inc(S("hh"), 1)

            def weights_hi(x, piece, half, free):
                part, n = piece // 2, WPART[piece // 2] // 2
                o = WOFF[part] + piece % 2 * n
                act.wait_ge(S(f"d_raw{part}"), 16 * x + 16)
                if free is not None:
                    act.wait_ge(S("expert_done"), free)
                A(wset[half][0][:, o:o + n], raw[:, o:o + n], ACT.Copy).then_inc(S("w_hi"), 1)

            def shared_dst(u):
                return hs[0][:, u // 2, (u % 2) * HT:(u % 2 + 1) * HT]

            def gathered_hi(e):
                act.wait_ge(S("g_mm"), e + 1)
                A(xg[0].rearrange("p k s -> p (k s)"), bank(3), ACT.Copy).then_inc(S("xgh"), 1)

            for u in range(SU):
                silu(0, u, HT, bank(3 + 2 * (u % 2)))
                hid_hi(0, u, HT, shared_dst(u))
                if u < 6:
                    weights_hi(1, u, 1, None)
            gathered_hi(0)

            def routed(e, half, last):
                base = FC * e + SU
                for c in range(FC):
                    silu(base, c, CAP, bank(5 + c % 2))
                    hid_hi(base, c, CAP, hr[0][:, c, :])
                    if not last:
                        weights_hi(e + 2, c, half, e + 1)
                    if c == 3:
                        act.wait_ge(S("st_mm"), e + 1)
                        A(stf[:, 0, :], psb[:, 6 * BK:6 * BK + TP], ACT.Copy).then_inc(S("st0"), 1)
                if not last:
                    gathered_hi(e + 1)
                act.wait_ge(S("ym"), e + 1)
                A(yhl[0], y32[:, :, :], ACT.Copy).then_inc(S("yh"), 1)

            with act.Fori(0, E // 2 - 1) as i:
                routed(2 * i, 0, False)
                routed(2 * i + 1, 1, False)
            routed(E - 2, 0, False)
            routed(E - 1, 1, True)

            act.wait_ge(S("over"), 1)
            more = act.value_load(over[0:1, 0:1])
            with act.If(more > 0):
                with act.Fori(0, E) as i:
                    for u in range(SU):
                        act.wait_ge(S("f_gu"), SU * i + u + 1)
                        A(gact[u % 2][:, :], bank(3 + 2 * (u % 2))[:, 0:HT],
                          ACT.Silu).then_inc(S("f_silu"), 1)

            act.wait_ge(S("d_tables"), 16)
            nc.scalar.preload_act_table_set("natural_log_exp_and_others")

            def l1(li):
                evac_T(li + 2, sml[:, (S_N1, S_N2)[li]:(S_N1, S_N2)[li] + 1])
                if li == 0:
                    for hf in range(2):
                        act.wait_ge(S("lat_mm"), hf + 1)
                        A(latT[:, hf * HT:(hf + 1) * HT], bank(4 + hf)[0:LAT, 0:HT],
                          ACT.Copy).then_inc(S("lat"), 1)
                U = 2 * U5

                def square(u):
                    act.wait_ge(S("qkcs"), U * li + u + 1)
                    A(sqr[:, u // 2, (u % 2) * HT:(u % 2 + 1) * HT],
                      qk[:, u // 2, (u % 2) * HT:(u % 2 + 1) * HT], ACT.Square).then_inc(S("sqr"), 1)

                def sqroot(u):
                    act.wait_ge(S("ms_mm"), U * li + u + 1)
                    s = sqr[:, u // 2, (u % 2) * HT:(u % 2 + 1) * HT]
                    A(s, bank(4 + u % 4)[:, 0:HT], ACT.Ln,
                      bias=cst[:, C_EPS:C_EPS + 1]).then_inc(S("ln"), 1)
                    act.wait_ge(S("ln"), U * li + u + 1)
                    A(s, s, ACT.Exp, scale=-0.5).then_inc(S("rt"), 1)

                for u in range(U + 2):
                    if u < U:
                        square(u)
                    if u >= 2:
                        sqroot(u - 2)
                act.wait_ge(S("zeros"), 2)
                for hf in range(2):
                    act.wait_ge(S("kf_mm"), 2 * li + hf + 1)
                    for g in range(2):
                        A(own_keys(g, hf), folded(g, hf), ACT.Copy).then_inc(S("kf"), 1)

                def evac_o(grp):
                    for i in range(2):
                        act.wait_ge(S("o_mm"), 8 * li + 2 * grp + i + 1)
                        src = bank(4 + 2 * (grp % 2) + i)[:, 0:QT].rearrange(
                            "p (a u n) -> p a u n", a=2, u=4)
                        b = 4 * grp + 2 * i
                        dst = oz.rearrange("p u (b n) -> p b u n", b=B)[:, b:b + 2]
                        A(dst, src, ACT.Copy).then_inc(S("o"), 1)

                def inverse(grp):
                    s = zs[:, :, grp * 4 * N:(grp + 1) * 4 * N]
                    act.wait_ge(S("zs"), 4 * li + grp + 1)
                    A(s, s, ACT.Ln).then_inc(S("lnz"), 1)
                    act.wait_ge(S("lnz"), 4 * li + grp + 1)
                    A(s, s, ACT.Exp, scale=-1.0).then_inc(S("zi"), 1)

                for grp in range(6):
                    if grp < 4:
                        for g in range(KV):
                            act.wait_ge(S("s_mm"), 16 * li + 4 * grp + g + 1)
                            if grp >= 2:
                                act.wait_ge(S("o_mm"), 8 * li + 2 * (grp - 1))
                            A(ex[grp % 2][:, g, :], bank(g)[:, 0:QT], ACT.Exp,
                              scale=0.25).then_inc(S("ex"), 1)
                    if 1 <= grp <= 4:
                        evac_o(grp - 1)
                    if grp >= 2:
                        inverse(grp - 2)

            l1(0)
            l1(1)
            evac_T(4, None)

        @block.vector
        def _(dve):
            V = nc.vector
            chain = [0]

            def link(ins):
                chain[0] += 1
                ins.then_inc(S("dve_chain"), 1)
                dve.wait_ge(S("dve_chain"), chain[0])

            link(V.memset(bank(6, 2), 1.0))
            link(V.memset(m2[:, :], 0.0))
            link(V.memset(off[:, 0, :], 0.0))
            dve.wait_ge(S("d_cst"), 16)
            V.tensor_copy(identb[:, :], ident).then_inc(S("identb"), 1)

            def ternary(w, tmp_p, tmp_n, colsum, factor):
                link(V.reduce_sum(thr[:, 0:1], colsum, AX_X))
                link(V.tensor_scalar(thr[:, 1:2], thr[:, 0:1], factor, None, ALU.mult))
                link(V.tensor_scalar(thr[:, 2:3], thr[:, 1:2], -1.0, None, ALU.mult))
                link(V.tensor_scalar(tmp_p, w, thr[:, 1:2], None, ALU.is_ge))
                link(V.tensor_scalar(tmp_n, w, thr[:, 2:3], None, ALU.is_le))

            dve.wait_ge(S("wabs_used"), 1)
            picked = dg.rearrange("p t q -> p (t q)")[:, 0:H * R].rearrange("p (j r) -> p j r", r=R)
            link(V.tensor_tensor(picked, bank(5)[:, 0:H * R].rearrange("p (j r) -> p j r", r=R),
                                 cst[:, C_PICK:C_PICK + R].unsqueeze(1).to_broadcast([P, H, R]), ALU.mult))
            link(V.reduce_sum(alq[:, :], picked, AX_X))
            link(V.tensor_scalar(alq[:, :], alq[:, :], 1.0 / D, None, ALU.mult))
            ternary(wq0_s[:, :, :], sg[:, :, :], sgn[:, :, :], bank(5)[:, 0:H * R],
                    0.05 / (2.0 * D * D))
            V.tensor_tensor(sq0[:, :, :], sg[:, :, :], sgn[:, :, :], ALU.subtract).then_inc(S("sq0"), 1)
            dve.wait_ge(S("m2_mm"), 1)
            for q in range(4):
                r = slice(32 * q, 32 * q + 32)
                link(V.tensor_copy(m2[r, r], bank(7)[r, 0:R]))
            V.memset(bank(7)[:, 0:R], 1.0).then_inc(S("m2"), 1)

            dve.wait_ge(S("sq0"), 1)
            dve.wait_ge(S("wosum"), 1)
            ternary(wo0_s[:, :, :], sg[:, :, 0:D], sgn[:, :, 0:D], bank(5)[:, 0:D],
                    0.05 / (1.0 * D * D))
            link(V.tensor_tensor(wo0q[:, :, :], sg[:, :, 0:D], sgn[:, :, 0:D], ALU.subtract))
            link(V.tensor_scalar(dg[:, 0:2, :], bank(5)[:, 0:D].rearrange("p (a b) -> p a b", a=2),
                                 1.0 / D, None, ALU.mult))
            V.tensor_tensor(wo0q[:, :, :], wo0q[:, :, :],
                            dg[:, 0:2, :].rearrange("p a b -> p (a b)").unsqueeze(1).to_broadcast([P, DC, D]),
                            ALU.mult).then_inc(S("wo0q"), 1)

            norm_count = [0]

            def tile_stats(src, t):
                V.bn_stats(stats[:, t, :], src[:, t, :]).then_inc(S("bn"), 1)

            def aggregate():
                norm_count[0] += TT
                dve.wait_ge(S("bn"), norm_count[0])
                for t in range(TT):
                    V.bn_aggr(mv[:, t, :], stats[:, t, :]).then_inc(S("bn2"), 1)
                dve.wait_ge(S("bn2"), norm_count[0])

            def moments(src):
                for t in range(TT):
                    tile_stats(src, t)
                aggregate()

            def residual(dst, wait, src):
                for t in range(TT):
                    wait(t)
                    link(V.tensor_tensor(dst[:, t, :], dst[:, t, :], src(t), ALU.add))
                    tile_stats(dst, t)
                aggregate()

            pows = [0]

            def root():
                pows[0] += 1
                dve.wait_ge(S("rstd"), pows[0])

            def layernorm(src, dst, signal=None):
                V.tensor_scalar(vtmp[:, :], mv[:, :, 1], LN_EPS, None, ALU.add).then_inc(S("var"), 1)
                root()
                for t in range(TT):
                    last = V.tensor_scalar(dst[:, t, :], src[:, t, :], mv[:, t, 0:1], rstd[:, t:t + 1],
                                           ALU.subtract, ALU.mult)
                    if signal:
                        last.then_inc(S(signal), 1)
                return last

            def rms_root(mean_square):
                V.tensor_scalar(vtmp[:, :], mean_square, RMS_EPS, None, ALU.add).then_inc(S("var"), 1)
                root()

            def rms_scale(src, dst, signal):
                for t in range(TT):
                    V.tensor_scalar(dst[:, t, :], src[:, t, :], rstd[:, t:t + 1], None,
                                    ALU.mult).then_inc(S(signal), 1)

            dve.wait_ge(S("d_tables"), 16)
            V.tensor_copy(iota[:, :], cst[:, C_IOTA:C_IOTA + CAP]).then_inc(S("iota"), 1)
            for t in range(TT):
                dve.wait_ge(S("h0"), t + 1)
                tile_stats(h, t)
            aggregate()
            link(layernorm(h, xn))
            link(V.tensor_reduce(ma[:, :], xn[:, :, :], AX_X, ALU.max, apply_absolute_value=True))
            link(V.tensor_scalar(ma[:, :], ma[:, :], 1e-6, None, ALU.max))
            link(V.reciprocal(vtmp[:, :], ma[:, :]))
            link(V.tensor_scalar(vtmp[:, :], vtmp[:, :], 7.0, None, ALU.mult))
            for t in range(TT):
                last = V.tensor_scalar(xn[:, t, :], xn[:, t, :], vtmp[:, t:t + 1], MAGIC, ALU.mult, ALU.add)
            link(last)
            V.tensor_scalar(xq[:, :, :], xn[:, :, :], MAGIC, None, ALU.subtract).then_inc(S("xq"), 1)
            V.tensor_tensor(dg[:, :, :], ident.unsqueeze(1).to_broadcast([P, TT, P]),
                            ma[:, :].unsqueeze(2).to_broadcast([P, TT, P]), ALU.mult).then_inc(S("dg"), 1)
            dve.wait_ge(S("xq_t"), 2)
            V.tensor_copy(xqT[:, 1, :], psb[:, 6 * 2 * BK:6 * 2 * BK + TP]).then_inc(S("xqT"), 1)
            dve.wait_ge(S("xqT"), 2)
            dve.wait_ge(S("mab_mm"), 1)
            for q in range(4):
                r = slice(32 * q, 32 * q + 32)
                last = V.tensor_scalar(mab[r, :], ps[r, 3 * BK + q * G4T:3 * BK + (q + 1) * G4T],
                                       1.0 / 7.0, None, ALU.mult)
            last.then_inc(S("mab"), 1)
            link(V.memset(bank(6), 1.0))
            link(V.tensor_tensor(am.rearrange("p (t j) -> p t j", j=H),
                                 mab[:, :].unsqueeze(2).to_broadcast([P, G4T, H]),
                                 alq[:, :].unsqueeze(1).to_broadcast([P, G4T, H]), ALU.mult))
            def projected(jb):
                heads = slice(3 * jb, min(3 * jb + 3, H))
                dve.wait_ge(S("pr_mm"), jb + 1)
                V.tensor_tensor(
                    pr.rearrange("p (t j) -> p j t", j=H)[:, heads, :],
                    bank(jb)[:, 0:(heads.stop - heads.start) * G4T].rearrange("p (j t) -> p j t", t=G4T),
                    am.rearrange("p (t j) -> p j t", j=H)[:, heads, :], ALU.mult).then_inc(S("pr"), 1)

            def queries(jb):
                heads = slice(3 * jb, min(3 * jb + 3, H))
                dve.wait_ge(S("biased"), heads.stop)
                csq = cst[:, C_CSQ:C_CSQ + N].unsqueeze(1).to_broadcast([P, heads.stop - heads.start, N])
                for b in range(B4):
                    last = V.tensor_tensor(
                        qcs.rearrange("p (b j n) -> p b j n", b=B4, j=H)[:, b, heads],
                        pr.rearrange("p (b n j) -> p b j n", b=B4, j=H)[:, b, heads], csq, ALU.mult)
                last.then_inc(S("qcs"), 1)

            for jb in range(6):
                projected(jb)
                if jb >= 1:
                    queries(jb - 1)
            queries(5)
            vb = vbd.rearrange("p (b g k w) -> p b g k w", b=B, g=HG, k=2)
            for k in range(2):
                hm = cst[0:2 * N, C_HM + k:C_HM + k + 1]
                V.tensor_copy(vb[0:2 * N, :, :, k, DH].rearrange("p b g -> p (b g)"),
                              hm.to_broadcast([2 * N, B * HG]))
            for b in (0, 2):
                dve.wait_ge(S("v_mm"), b + 1)
                for k in range(2):
                    last = V.tensor_scalar(*value_rows(b, k), None, ALU.mult)
                last.then_inc(S("v"), 1)

            def shift(p):
                dve.wait_ge(S("sc_mm"), p + 1)
                s3 = bank(2 * (p % 2), 2).rearrange("p (a c) -> p a c", a=2)[:, :, 0:8 * N]
                for a in range(2):
                    last = V.reduce_max(mx[:, p % 2, 8 * a:8 * a + 8],
                                        s3[:, a].rearrange("p (j m) -> p j m", m=N), AX_X)
                link(last)
                if p >= 2:
                    dve.wait_ge(S("pt_mm"), p - 1)
                for a in range(2):
                    last = V.tensor_tensor(
                        pe_[p % 2].rearrange("p (a j m) -> p a j m", a=2, j=8)[:, a],
                        s3[:, a].rearrange("p (j m) -> p j m", m=N),
                        mx[:, p % 2, 8 * a:8 * a + 8].unsqueeze(2).to_broadcast([P, 8, N]), ALU.subtract)
                last.then_inc(S("shifted"), 1)

            def finish_y(p):
                dve.wait_ge(S("y_mm"), p + 1)
                yv = bank(6 + p % 2)[:, 0:H * VW].rearrange("p (j w) -> p j w", w=VW)
                link(V.reciprocal(rz[:, p % 2, :], yv[:, :, DH]))
                y = yq[:, p, :]
                V.tensor_tensor(y.rearrange("p (j w) -> p j w", w=DH), yv[:, :, 0:DH],
                                rz[:, p % 2, :].unsqueeze(2).to_broadcast([P, H, DH]),
                                ALU.mult).then_inc(S("y"), 1)
                dve.wait_ge(S("y"), p + 1)
                m = ma2[:, p:p + 1]
                link(V.tensor_reduce(m, y, AX_X, ALU.max, apply_absolute_value=True))
                link(V.tensor_scalar(m, m, 1e-6, None, ALU.max))
                link(V.reciprocal(rma[:, p:p + 1], m))
                link(V.tensor_scalar(y, y, rma[:, p:p + 1], 7.0, ALU.mult, ALU.mult))
                link(V.tensor_scalar(y, y, MAGIC, None, ALU.add))
                link(V.tensor_scalar(y, y, MAGIC, m, ALU.subtract, ALU.mult))
                V.tensor_scalar(y, y, 1.0 / 7.0, None, ALU.mult).then_inc(S("yq"), 1)

            for p in range(PAIRS + 2):
                if p < PAIRS:
                    shift(p)
                if p >= 2:
                    finish_y(p - 2)
            V.memset(yqT[:, :, T:TP], 0.0).then_inc(S("yqpad"), 1)
            dve.wait_ge(S("yT_mm"), 2)
            V.tensor_copy(yqT[:, 1, 0:T].rearrange("p (a b n) -> p a b n", a=PAIRS, b=2),
                          bank(2, 2).rearrange("p (a b n) -> p a b n", a=PAIRS, b=2)[:, :, :, 0:N]
                          ).then_inc(S("yT"), 1)
            residual(h, lambda t: dve.wait_ge(S("wo_mm"), t + 1), lambda t: bank(3 + t)[:, 0:D])

            def take_T(stage, scale=None):
                dve.wait_ge(S("nT_mm"), stage)
                if scale is None:
                    V.tensor_copy(xnT[:, 1, :], bank(6, 2)[:, 0:TP]).then_inc(S("nT"), 1)
                else:
                    V.tensor_scalar(xnT[:, 1, :], bank(6, 2)[:, 0:TP], scale, None,
                                    ALU.mult).then_inc(S("nT"), 1)

            layernorm(h, xn, "xn")
            take_T(1)

            dve.wait_ge(S("xTh"), 1)
            V.tensor_tensor(xTl[:, :, :], xnT[:, :, :], xTh[:, :, :].bitcast(F32),
                            ALU.subtract).then_inc(S("xTl"), 1)
            link(V.memset(hwork[:, :].bitcast(F32).rearrange("p (q t) -> p q t", t=TP)[:, :, T:TP], 0.0))

            dve.wait_ge(S("lg_mm"), 1)
            link(V.tensor_tensor(lg[:, :, :], bank(0)[:, 0:TT * E].rearrange("p (t e) -> p t e", e=E),
                                 sml[:, S_RB:S_RB + E].unsqueeze(1).to_broadcast([P, TT, E]), ALU.add))
            link(V.reduce_max(lmx[:, :], lg[:, :, :], AX_X))
            V.tensor_tensor(lg[:, :, :], lg[:, :, :], lmx[:, :].unsqueeze(2).to_broadcast([P, TT, E]),
                            ALU.subtract).then_inc(S("lg_shift"), 1)
            lt = cst[:, C_LT:C_LT + E * E].rearrange("p (e f) -> p e f", e=E)
            ranks = [P, TT * E, E]
            mine = lg[:, :, :].rearrange("p t e -> p (t e)").unsqueeze(2).to_broadcast(ranks)
            gt2, eq2 = (x[:, :, :, :].rearrange("p t e f -> p (t e) f") for x in (gt, eq))

            def parts_by_token():
                dve.wait_ge(S("xh"), 1)
                V.tensor_tensor(xl[:, :, :], xn[:, :, :], xh[:, :, :].bitcast(F32),
                                ALU.subtract).then_inc(S("xl"), 1)

            def router_probs():
                dve.wait_ge(S("lg_exp"), 1)
                link(V.reduce_sum(lmx[:, :], lg[:, :, :], AX_X))
                link(V.reciprocal(lmx[:, :], lmx[:, :]))
                link(V.tensor_tensor(lg[:, :, :], lg[:, :, :], lmx[:, :].unsqueeze(2).to_broadcast([P, TT, E]),
                                     ALU.mult))
                for t in range(TT):
                    other = lg[:, t, :].unsqueeze(1).to_broadcast([P, E, E])
                    V.tensor_copy(gt[:, t], other).then_inc(S("gt"), 1)
                dve.wait_ge(S("gt"), TT)

            def router_compare():
                link(V.tensor_tensor(eq2, gt2, mine, ALU.is_equal))
                link(V.tensor_tensor(gt2, gt2, mine, ALU.is_gt))
                eq3, gt3 = (x[:, :, :, :].rearrange("p t e f -> p t (e f)") for x in (eq, gt))
                link(V.tensor_tensor(eq3, eq3, lt.rearrange("p e f -> p (e f)").unsqueeze(1).to_broadcast(
                    [P, TT, E * E]), ALU.mult))
                link(V.tensor_tensor(gt3, gt3, eq3, ALU.add))

            def router_select():
                link(V.reduce_sum(sel_e[:, :, :], gt[:, :, :, :], AX_X))
                link(V.tensor_scalar(sel_e[:, :, :], sel_e[:, :, :], 2.0, None, ALU.is_lt))
                valid = cst[:, C_VALID:C_VALID + TT].unsqueeze(2).to_broadcast([P, TT, E])
                V.tensor_tensor(sel_e[:, :, :], sel_e[:, :, :], valid, ALU.mult).then_inc(S("sel"), 1)

            def router_weights():
                dve.wait_ge(S("sel"), 1)
                link(V.tensor_tensor(lg[:, :, :], lg[:, :, :], sel_e[:, :, :], ALU.mult))
                link(V.reduce_sum(lmx[:, :], lg[:, :, :], AX_X))
                link(V.tensor_scalar(lmx[:, :], lmx[:, :], 1e-20, None, ALU.add))
                link(V.reciprocal(lmx[:, :], lmx[:, :]))
                link(V.tensor_tensor(wts[:, :, :].rearrange("p e t -> p t e"), lg[:, :, :],
                                     lmx[:, :].unsqueeze(2).to_broadcast([P, TT, E]), ALU.mult))
                link(V.tensor_copy(wthl[:, :, :, 0], wts[:, :, :]))
                link(V.tensor_tensor(wthl[:, :, :, 1], wts[:, :, :], wthl[:, :, :, 0].bitcast(F32), ALU.subtract))

            def slots():
                dve.wait_ge(S("pos_mm"), 1)
                for t in range(TT):
                    link(V.tensor_tensor(off[:, t + 1, :], off[:, t, :],
                                         bank(7)[:, 64 + t * E:64 + (t + 1) * E], ALU.add))
                link(V.tensor_tensor(gt[:, 0, 0:TT, :], bank(7)[:, 0:TT * E].rearrange("p (t e) -> p t e", e=E),
                                     off[:, 0:TT, :], ALU.add))
                link(V.tensor_scalar(gt[:, 0, 0:TT, :], gt[:, 0, 0:TT, :], 1.0, None, ALU.add))
                link(V.tensor_tensor(gt[:, 0, 0:TT, :], gt[:, 0, 0:TT, :], sel_e[:, :, :], ALU.mult))
                link(V.tensor_scalar(slot[:, :, :].rearrange("p e t -> p t e"), gt[:, 0, 0:TT, :],
                                     1.0, None, ALU.subtract))
                link(V.scalar_tensor_tensor(wover[:, :, :].rearrange("p e t -> p (e t)"),
                                            slot[:, :, :].rearrange("p e t -> p (e t)"), float(CAP),
                                            wts[:, :, :].rearrange("p e t -> p (e t)"), ALU.is_ge, ALU.mult))
                link(V.reduce_max(lmx[:, 0:1], off[:, TT, :], AX_X))
                V.tensor_scalar(over[:, :], lmx[:, 0:1], float(CAP), None, ALU.is_gt).then_inc(S("over"), 1)

            def later(base, u):
                return not isinstance(base, int) or base + u >= 2

            def multiply(base, u, n, src):
                dve.wait_ge(S("silu"), base + u + 1)
                if later(base, u):
                    dve.wait_ge(S("hh"), base + u - 1)
                    dve.wait_ge(S("hl"), base + u - 1)
                V.tensor_tensor(h32[u % 2][:, 0:n], gact[u % 2][:, 0:n], src[:, 0:n],
                                ALU.mult).then_inc(S("hm"), 1)

            def hid_lo(base, u, n, dst, hi):
                dve.wait_ge(S("hh"), base + u + 1)
                V.tensor_tensor(dst, h32[u % 2][:, 0:n], hi.bitcast(F32), ALU.subtract).then_inc(S("hl"), 1)

            def one_hot(e, first):
                if not first:
                    dve.wait_ge(S("st_mm"), e)
                for t in range(TT):
                    last = V.tensor_scalar(sbf[:, t, :], iota[:, :], slot[:, e, t:t + 1], None, ALU.is_equal)
                last.then_inc(S("sbf"), 1)

            def one_hot_fr(e):
                dve.wait_ge(S("sbf"), e + 1)
                V.tensor_copy(wcur[:, :, :], wthl[:, e, :, :].bitcast(F32)).then_inc(S("wcur"), 1)
                V.tensor_copy(sf[:, :, :], sbf[:, :, :]).then_inc(S("sf"), 1)

            def gathered_lo(e):
                dve.wait_ge(S("g_mm"), e + 1)
                V.tensor_copy(xg[1].rearrange("p k s -> p (k s)"), bank(4)).then_inc(S("xgl"), 1)

            def shared_lo(u):
                s = (slice(None), u // 2, slice((u % 2) * HT, (u % 2 + 1) * HT))
                hid_lo(0, u, HT, hs[1][s], hs[0][s])

            for u in range(SU):
                multiply(0, u, HT, bank(4 + 2 * (u % 2)))
                shared_lo(u)
                steps = {0: router_probs, 1: router_compare, 2: router_select, 3: router_weights,
                         4: parts_by_token, 5: slots, 7: lambda: one_hot(0, True), 8: lambda: one_hot_fr(0)}
                if u in steps:
                    steps[u]()
            gathered_lo(0)

            def routed(e, last):
                base = FC * e + SU
                for c in range(FC):
                    multiply(base, c, CAP, bank(5 + c % 2)[:, CAP:2 * CAP])
                    hid_lo(base, c, CAP, hr[1][:, c, :], hr[0][:, c, :])
                    if c == 3:
                        dve.wait_ge(S("st_mm"), e + 1)
                        V.tensor_copy(stf[:, 1, :], psb[:, 8 * BK:8 * BK + TP]).then_inc(S("st1"), 1)
                        V.reduce_sum(wsl[:, :], bank(4)[:, TP // 2:TP // 2 + 2 * CT].rearrange(
                            "p (s w) -> p s w", w=2), AX_X).then_inc(S("wsl"), 1)
                        if not last:
                            one_hot(e + 1, False)
                    if c == 4 and not last:
                        one_hot_fr(e + 1)
                if not last:
                    gathered_lo(e + 1)
                dve.wait_ge(S("expert_done"), e + 2)
                dve.wait_ge(S("wsl"), e + 1)
                for s in range(CT):
                    last_ins = V.tensor_scalar(y32[:, s, :], bank(7)[:, s * D:(s + 1) * D], wsl[:, s:s + 1],
                                               None, ALU.mult)
                last_ins.then_inc(S("ym"), 1)
                dve.wait_ge(S("yh"), e + 1)
                V.tensor_tensor(yhl[1], y32[:, :, :], yhl[0].bitcast(F32), ALU.subtract).then_inc(S("yl"), 1)

            with dve.Fori(0, E // 2 - 1) as i:
                routed(2 * i, False)
                routed(2 * i + 1, False)
            routed(E - 2, False)
            routed(E - 1, True)
            for t in range(TT):
                dve.wait_ge(S("y_all"), t // 2 + 1)
                last = V.tensor_tensor(h[:, t, :], h[:, t, :], bank(t // 2)[:, (t % 2) * D:(t % 2 + 1) * D],
                                       ALU.add)
            last.then_inc(S("y_read"), 1)

            dve.wait_ge(S("y_read"), 1)
            more = dve.value_load(over[0:1, 0:1])
            with dve.If(more > 0):
                with dve.Fori(0, E) as i:
                    for u in range(SU):
                        dve.wait_ge(S("f_silu"), SU * i + u + 1)
                        V.tensor_tensor(hidf[u // 2 % 2][:, (u % 2) * HT:(u % 2 + 1) * HT], gact[u % 2][:, :],
                                        bank(4 + 2 * (u % 2))[:, 0:HT], ALU.mult).then_inc(S("f_hid"), 1)
                    dve.wait_ge(S("f_dn"), i + 1)
                    for t in range(TT):
                        last = V.scalar_tensor_tensor(
                            h[:, t, :], bank(t // 2)[:, (t % 2) * D:(t % 2 + 1) * D],
                            wover[:, i, t:t + 1], h[:, t, :], ALU.mult, ALU.add)
                    last.then_inc(S("f_col"), 1)
                    dve.wait_ge(S("f_col"), i + 1)
            V.memset(latT[:, T:TP], 0.0).then_inc(S("moe"), 1)
            link(V.memset(ozp[:, :, T:TP], 0.0))

            def l1(li):
                if li == 0:
                    moments(h)
                    layernorm(h, xres, "res")
                    link(V.tensor_tensor(vtmp[:, :], rstd[:, :], rstd[:, :], ALU.mult))
                    link(V.tensor_tensor(vtmp[:, :], vtmp[:, :], mv[:, :, 1], ALU.mult))
                    dve.wait_ge(S("res"), TT)
                    rms_root(vtmp[:, :])
                else:
                    link(V.tensor_tensor(vtmp[:, :], mv[:, :, 0], mv[:, :, 0], ALU.mult))
                    link(V.tensor_tensor(vtmp[:, :], vtmp[:, :], mv[:, :, 1], ALU.add))
                    rms_root(vtmp[:, :])
                rms_scale(xres, xn, "xn")
                take_T(li + 2, sml[:, (S_N1, S_N2)[li] + 1:(S_N1, S_N2)[li] + 2])
                cs = cst[:, (C_CSG, C_CSL)[li]:(C_CSG, C_CSL)[li] + N]
                dve.wait_ge(S("v1_mm"), li + 1)
                dve.wait_ge(S("zeros"), 2)
                for e in range(2):
                    r = slice(KS * e, KS * e + N)
                    last = V.tensor_copy(vo[r, :, :, e, 0:DH].rearrange("p b g d -> p (b g) d"),
                                         bank(7)[r, :].rearrange("p (c d) -> p c d", d=DH))
                last.then_inc(S("vo"), 1)
                U = 2 * U5
                for u in range(U):
                    dve.wait_ge(S("qk_mm"), U * li + u + 1)
                    V.tensor_tensor(qk[:, u // 2, (u % 2) * HT:(u % 2 + 1) * HT].rearrange("p (b n) -> p b n", n=N),
                                    bank(u % 4)[:, 0:HT].rearrange("p (b n) -> p b n", n=N),
                                    cs.unsqueeze(1).to_broadcast([P, 8, N]), ALU.mult).then_inc(S("qkcs"), 1)
                for u in range(U):
                    s = (slice(None), u // 2, slice((u % 2) * HT, (u % 2 + 1) * HT))
                    dve.wait_ge(S("rt"), U * li + u + 1)
                    V.tensor_tensor(qk[s], qk[s], sqr[s], ALU.mult).then_inc(S("qkn"), 1)
                for hf in range(2):
                    dve.wait_ge(S("kf_mm"), 2 * li + hf + 1)
                    for g in range(2, KV):
                        V.tensor_copy(own_keys(g, hf), folded(g, hf)).then_inc(S("kfd"), 1)

                def mask(grp):
                    for g in range(KV):
                        dve.wait_ge(S("ex"), 16 * li + 4 * grp + g + 1)
                        x = ex[grp % 2][:, g, :].rearrange("p (c n) -> p c n", n=N)
                        V.tensor_tensor(x, x, cst[:, C_MASK:C_MASK + N].unsqueeze(1).to_broadcast([P, 8, N]),
                                        ALU.mult).then_inc(S("exm"), 1)

                def sums(grp):
                    dve.wait_ge(S("o"), 8 * li + 2 * grp + 2)
                    s = (slice(None), slice(None), slice(grp * 4 * N, (grp + 1) * 4 * N))
                    V.stream_shuffle(zs[s], oz[s], [DH + i % DH for i in range(32)]).then_inc(S("zs"), 1)

                def divide(grp):
                    s = (slice(None), slice(None), slice(grp * 4 * N, (grp + 1) * 4 * N))
                    dve.wait_ge(S("zi"), 4 * li + grp + 1)
                    V.tensor_tensor(ozp[s], oz[s], zs[s], ALU.mult).then_inc(S("on"), 1)

                for grp in range(6):
                    if grp < 4:
                        mask(grp)
                    if 1 <= grp <= 4:
                        sums(grp - 1)
                    if grp >= 2:
                        divide(grp - 2)
                if li == 0:
                    residual(xres, lambda t: dve.wait_ge(S("wo1_mm"), t + 1), lambda t: bank(t)[:, 0:D])
                    V.tensor_tensor(h[:, :, :], h[:, :, :], xres[:, :, :], ALU.add).then_inc(S("h_half"), 1)
                else:
                    residual(h, lambda t: dve.wait_ge(S("wo1_mm"), TT + t + 1), lambda t: bank(t)[:, 0:D])

            l1(0)
            l1(1)
            layernorm(h, xn, "xn")
            take_T(4)
            for t in range(TT):
                dve.wait_ge(S("fin_mm"), t + 1)
                link(V.tensor_scalar(xn[:, t, :], bank(t)[:, 0:D], -100.0, 100.0, ALU.max, ALU.min))
                V.tensor_tensor(h[:, t, :], h[:, t, :], xn[:, t, :], ALU.add).then_inc(S("out_ready"), 1)

        @block.gpsimd
        def _(pool):
            pool.wait_ge(S("d_tables"), 16)
            for n in range(NORMS):
                pool.wait_ge(S("var"), n + 1)
                nc.gpsimd.tensor_tensor(rstd[:, :], vtmp[:, :], cst[:, C_HALF:C_HALF + TT],
                                        ALU.pow).then_inc(S("rstd"), 1)
                if n == 4:
                    pool.wait_ge(S("d_l1"), 16 * 9)
                    nc.gpsimd.tensor_scalar(wfs[:, :, :], wfin_s[:, :, :], 0.0, 2.0, ALU.is_ge,
                                            ALU.mult).then_inc(S("wfs_steps"), 1)
                    pool.wait_ge(S("wfs_steps"), 1)
                    nc.gpsimd.tensor_scalar(wfs[:, :, :], wfs[:, :, :], 1.0, None,
                                            ALU.subtract).then_inc(S("wfs_steps"), 1)
                    pool.wait_ge(S("wfs_steps"), 2)
                    nc.gpsimd.tensor_tensor(wfs[:, :, :], wfs[:, :, :],
                                            sml[:, S_SC:S_SC + D].unsqueeze(1).to_broadcast([P, DC, D]),
                                            ALU.mult).then_inc(S("wfs"), 1)
                if n == 3:
                    nc.gpsimd.memset(vo[:, :, :, :, :], 0.0).then_inc(S("cleared"), 1)
                    pool.wait_ge(S("cleared"), 1)
                    for e in range(2):
                        last = nc.gpsimd.memset(vo[KS * e:KS * e + N, :, :, e, DH:R].rearrange(
                            "p b g d -> p (b g) d"), 1.0)
                    last.then_inc(S("zeros"), 1)
                    pool.wait_ge(S("zeros"), 1)
                    nc.gpsimd.memset(km[:, :, :, :, :], 0.0).then_inc(S("zeros"), 1)
                if n == 0:
                    pool.wait_ge(S("biased"), H)
                    nc.gpsimd.tensor_tensor(
                        kcs.rearrange("p (b r) -> p b r", b=B4), pr.rearrange("p (b r) -> p b r", b=B4),
                        cst[:, C_CSK:C_CSK + T].unsqueeze(1).to_broadcast([P, B4, T]),
                        ALU.mult).then_inc(S("kcs"), 1)
                    pool.wait_ge(S("kcs"), 1)
                    pool.wait_ge(S("v_mm"), B4)
                    pool.wait_ge(S("qf"), 5)
                    for part in range(3):
                        pool.wait_ge(S(f"d_raw{part}"), 16)
                        o = WOFF[part]
                        w = (slice(None), slice(o, o + WPART[part]))
                        nc.gpsimd.tensor_copy(wset[0][0][w], raw[w]).then_inc(S("w_hi0"), 1)
                        pool.wait_ge(S("w_hi0"), part + 1)
                        nc.gpsimd.tensor_tensor(wset[0][1][w], raw[w], wset[0][0][w].bitcast(F32),
                                                ALU.subtract).then_inc(S("w_lo"), 1)
                if n == 1:
                    with pool.Fori(0, E // 2) as i:
                        for half in range(2):
                            for part in range(3):
                                o = WOFF[part]
                                w = (slice(None), slice(o, o + WPART[part]))
                                pool.wait_ge(S("w_hi"), 12 * i + 6 * half + 2 * part + 2)
                                nc.gpsimd.tensor_tensor(wset[1 - half][1][w], raw[w],
                                                        wset[1 - half][0][w].bitcast(F32),
                                                        ALU.subtract).then_inc(S("w_lo"), 1)

        @block.tensor
        def _(pe):
            M = nc.tensor.matmul
            pe.wait_ge(S("dve_chain"), 1)
            pe.wait_ge(S("d_cst"), 16)
            pe.wait_ge(S("wabs"), 1)
            for k in range(DC):
                last = M(bank(5)[:, 0:H * R], ones, wabs[:, k, :], start=(k == 0), stop=(k == DC - 1))
            last.then_inc(S("wabs_used"), 1)
            pe.wait_ge(S("d_u2t"), 16)
            for q in range(4):
                last = M(bank(7)[32 * q:32 * q + 32, 0:R], u2t_s[:, :], u2t_s[:, :], start=True, stop=True)
            last.then_inc(S("m2_mm"), 1)

            for c in range(PC):
                pe.wait_ge(S(f"d_x{c}"), 32)
                for t in range(TT):
                    M(bank(t)[:, 0:D], xT_s[:, c, t * P:(t + 1) * P], tokW_s[:, c, :],
                      start=(c == 0), stop=False)
                if c == PC // 2:
                    pe.wait_ge(S("wabs"), 2)
                    pe.wait_ge(S("sq0"), 1)
                    for k in range(DC):
                        last = M(bank(5)[:, 0:D], ones, wabs[:, k, 0:D], start=(k == 0), stop=(k == DC - 1))
                    last.then_inc(S("wosum"), 1)
            pe.wait_ge(S("d_pos"), 32)
            for t in range(TT):
                M(bank(t)[:, 0:D], sel_s[0:POSK, t * P:(t + 1) * P], posb_s[0:POSK, :],
                  start=False, stop=True).then_inc(S("tok"), 1)

            pe.wait_ge(S("xq"), 1)
            pe.wait_ge(S("wo0q"), 1)
            pe.wait_ge(S("identb"), 1)
            for k in range(DC):
                for t in range(TT):
                    last = nc.tensor.transpose(psb[:, (5 + k) * 2 * BK + t * P:(5 + k) * 2 * BK + (t + 1) * P],
                                               xq[:, t, k * P:(k + 1) * P], identb[:, :])
                last.then_inc(S("xq_t"), 1)
            pe.wait_ge(S("dg"), 1)
            M(bank(3), ones, dg[:, 0:4, :].rearrange("p a b -> p (a b)"), start=True, stop=True)
            M(bank(4)[:, 0:P], ones, dg[:, 4, :], start=True, stop=True).then_inc(S("mab_mm"), 1)
            pe.wait_ge(S("xqT"), 2)
            pe.wait_ge(S("mab"), 1)
            for j in range(H):
                for q in range(4):
                    for k in range(DC):
                        last = M(ps[32 * q:32 * q + 32, (j // 3) * BK + (j % 3) * G4T:(j // 3) * BK + (j % 3 + 1) * G4T],
                                 sq0[:, k, R * j:R * j + R], xqT[:, k, q * G4T:(q + 1) * G4T],
                                 start=(k == 0), stop=(k == DC - 1), skip_group_check=True)
                if j % 3 == 2 or j == H - 1:
                    last.then_inc(S("pr_mm"), 1)
            pe.wait_ge(S("m2"), 1)
            pe.wait_ge(S("biased"), H)
            def queries(c):
                w = min(BK, G4 - c * BK)
                if c >= 2:
                    pe.wait_ge(S("qf"), c - 1)
                M(bank(4 + c % 2)[:, 0:w], m2[:, :], qcs[:, c * BK:c * BK + w],
                  start=True, stop=True).then_inc(S("qf_mm"), 1)

            def value_keys(b):
                if b >= 2:
                    pe.wait_ge(S(("v", "va")[b % 2]), 1)
                for g in range(HG):
                    last = nc.tensor.transpose(
                        ps[0:2 * N, 2 * (b % 2) * BK + g * P:2 * (b % 2) * BK + (g + 1) * P],
                        pr[:, b * T + 2 * N * g:b * T + 2 * N * (g + 1)], ident)
                last.then_inc(S("v_mm"), 1)

            value_keys(0)
            value_keys(1)
            pe.wait_ge(S("qcs"), 6)
            queries(0)
            queries(1)
            value_keys(2)
            queries(2)
            queries(3)
            value_keys(3)
            queries(4)

            def scores(p):
                q = p // 2
                if p == 0:
                    pe.wait_ge(S("qf"), 5)
                    pe.wait_ge(S("kcs"), 1)
                if p < 2:
                    pe.wait_ge(S("v"), 2)
                    pe.wait_ge(S("va"), 2)
                else:
                    pe.wait_ge(S("shifted"), p - 1)
                for j in range(H):
                    for par in range(2):
                        b = 2 * (p % 2) + par
                        last = M(ps[64 * par:64 * par + N, (2 * (p % 2) + j // 8) * BK + (j % 8) * N:
                                    (2 * (p % 2) + j // 8) * BK + (j % 8 + 1) * N],
                                 qf[32 * q:32 * q + 32, (b * H + j) * N:(b * H + j + 1) * N],
                                 kcs[32 * q:32 * q + 32, b * T + j * N:b * T + (j + 1) * N],
                                 start=True, stop=True, skip_group_check=True)
                last.then_inc(S("sc_mm"), 1)

            def probs_T(p):
                pe.wait_ge(S("expd"), p + 1)
                if p >= 1:
                    pe.wait_ge(S("pt"), p)
                for g in range(HG):
                    last = nc.tensor.transpose(ps[0:2 * N, 4 * BK + g * P:4 * BK + (g + 1) * P],
                                               pe_[p % 2][:, 2 * N * g:2 * N * (g + 1)], ident)
                last.then_inc(S("pt_mm"), 1)

            def values(p):
                pe.wait_ge(S("pt"), p + 1)
                if p >= 2:
                    pe.wait_ge(S("y"), p - 1)
                for g in range(HG):
                    for par in range(2):
                        o = ((2 * p + par) * HG + g) * 2 * VW
                        last = M(ps[64 * par:64 * par + N, (6 + p % 2) * BK + 2 * VW * g:(6 + p % 2) * BK + 2 * VW * (g + 1)],
                                 ptT[p % 2][0:2 * N, g * P + 64 * par:g * P + 64 * par + N],
                                 vbd[0:2 * N, o:o + 2 * VW], start=True, stop=True, skip_group_check=True)
                last.then_inc(S("y_mm"), 1)

            scores(0)
            scores(1)
            for p in range(PAIRS):
                probs_T(p)
                if p + 2 < PAIRS:
                    scores(p + 2)
                values(p)
            pe.wait_ge(S("yq"), PAIRS)
            for k in range(DC):
                for p in range(PAIRS):
                    last = nc.tensor.transpose(ps[:, 2 * k * BK + p * P:2 * k * BK + (p + 1) * P],
                                               yq[:, p, k * P:(k + 1) * P], ident)
                last.then_inc(S("yT_mm"), 1)
            pe.wait_ge(S("yT"), 2)
            pe.wait_ge(S("yqpad"), 1)
            for t in range(TT):
                for k in range(DC):
                    last = M(bank(3 + t)[:, 0:D], yqT[:, k, t * P:(t + 1) * P],
                             wo0q[:, k, :], start=(k == 0), stop=(k == DC - 1))
                last.then_inc(S("wo_mm"), 1)

            def transposes(stage):
                for t in range(TT):
                    pe.wait_ge(S("xn"), TT * (stage - 1) + t + 1)
                    for k in range(DC):
                        last = nc.tensor.transpose(ps[:, (4 + 2 * k) * BK + t * P:(4 + 2 * k) * BK + (t + 1) * P],
                                                   xn[:, t, k * P:(k + 1) * P], ident)
                last.then_inc(S("nT_mm"), 1)

            transposes(1)
            pe.wait_ge(S("nT"), 2)
            pe.wait_ge(S("d_rw"), 16)
            for t in range(TT):
                for k in range(DC):
                    last = M(bank(0)[:, t * E:(t + 1) * E], xnT[:, k, t * P:(t + 1) * P], rw_s[:, k, :],
                             start=(k == 0), stop=(k == DC - 1), skip_group_check=True)
            last.then_inc(S("lg_mm"), 1)

            def split3(dst, a, b, start, stop, skip=False):
                M(dst, a[0], b[0], start=start, stop=False, skip_group_check=skip)
                M(dst, a[0], b[1], start=False, stop=False, skip_group_check=skip)
                return M(dst, a[1], b[0], start=False, stop=stop, skip_group_check=skip)

            def gate_up_chunk(w, part, k, c):
                o = WOFF[part] + k * FP + c * P
                return [w[i][:, o:o + P] for i in range(2)]

            def shared_gate_up(u):
                c, hf = u // 2, u % 2
                if u >= 2:
                    pe.wait_ge(S("hm"), u - 1)
                for part in range(2):
                    for k in range(DC):
                        last = split3(bank(3 + 2 * (u % 2) + part)[:, 0:HT],
                                      gate_up_chunk(wset[0], part, k, c),
                                      [x[:, k, hf * HT:(hf + 1) * HT] for x in (xTh, xTl)],
                                      k == 0, k == DC - 1)
                last.then_inc(S("gu"), 1)

            def shared_down(c):
                pe.wait_ge(S("hl"), 2 * c + 2)
                o = WOFF[2] + c * D
                for t in range(TT):
                    last = split3(bank(t // 2)[:, (t % 2) * D:(t % 2 + 1) * D],
                                  [x[:, c, t * P:(t + 1) * P] for x in hs],
                                  [w[:, o:o + D] for w in wset[0]],
                                  c == 0 and t % 2 == 0, False, True)
                if c == FC - 1:
                    last.then_inc(S("expert_done"), 1)

            def gather(e):
                pe.wait_ge(S("sf"), e + 1)
                for b, x in ((3, xh), (4, xl)):
                    for k in range(DC):
                        for t in range(TT):
                            last = M(bank(b)[:, k * CAP:(k + 1) * CAP], x[:, t, k * P:(k + 1) * P],
                                     sf[:, t, :], start=(t == 0), stop=(t == TT - 1), skip_group_check=True)
                last.then_inc(S("g_mm"), 1)

            def gate_up(e, c, half):
                w = wset[1 - half]
                base = FC * e + SU
                if c == 0:
                    pe.wait_ge(S("xgh"), e + 1)
                    pe.wait_ge(S("xgl"), e + 1)
                    pe.wait_ge(S("w_lo"), 3 * e + 5)
                pe.wait_ge(S("hm"), base + c - 1)
                for part in range(2):
                    for k in range(DC):
                        last = split3(bank(5 + c % 2)[:, part * CAP:(part + 1) * CAP],
                                      gate_up_chunk(w, part, k, c),
                                      [x[:, k, :] for x in xg], k == 0, k == DC - 1, True)
                last.then_inc(S("gu"), 1)

            def down(e, c, half):
                w = wset[1 - half]
                if c == 0:
                    pe.wait_ge(S("w_lo"), 3 * e + 6)
                pe.wait_ge(S("hl"), FC * e + SU + c + 1)
                o = WOFF[2] + c * D
                for s in range(CT):
                    last = split3(bank(7)[:, s * D:(s + 1) * D],
                                  [x[:, c, s * P:(s + 1) * P] for x in hr],
                                  [v[:, o:o + D] for v in w],
                                  c == 0 and s == 0, c == FC - 1, True)
                if c == FC - 1:
                    last.then_inc(S("expert_done"), 1)

            def slots_to_tokens(e):
                for s in range(CT):
                    for t in range(TT):
                        nc.tensor.transpose(psb[:, (3 + s) * 2 * BK + t * P:(3 + s) * 2 * BK + (t + 1) * P],
                                            sbf[:, t, s * P:(s + 1) * P], identb[:, :])
                for s in range(CT):
                    for t in range(TT):
                        last = M(bank(4)[:, TP // 2 + 2 * s:TP // 2 + 2 * s + 2], sf[:, t, s * P:(s + 1) * P],
                                 wcur[:, t, :], start=(t == 0), stop=(t == TT - 1), skip_group_check=True)
                last.then_inc(S("st_mm"), 1)

            def scatter(e, final=False):
                pe.wait_ge(S("yl"), e + 1)
                pe.wait_ge(S("st0"), e + 1)
                pe.wait_ge(S("st1"), e + 1)
                for t in range(TT):
                    for s in range(CT):
                        for y in yhl:
                            last = M(bank(t // 2)[:, (t % 2) * D:(t % 2 + 1) * D], stf[:, s, t * P:(t + 1) * P],
                                     y[:, s, :], start=False, stop=False, skip_group_check=True)
                    if final and (t % 2 == 1 or t == TT - 1):
                        last.then_inc(S("y_all"), 1)

            pe.wait_ge(S("lg_shift"), 1)
            pe.wait_ge(S("xTl"), 1)
            pe.wait_ge(S("w_lo"), 3)
            for u in range(SU):
                shared_gate_up(u)
                if u == 4:
                    pe.wait_ge(S("sel"), 1)
                    sel2 = sel_e[:, :, :].rearrange("p t e -> p (t e)")
                    M(bank(7)[:, 0:TT * E], cst[:, C_TRI:C_TRI + P], sel2, start=True, stop=True,
                      skip_group_check=True)
                    M(bank(7)[:, 64:64 + TT * E], ones, sel2, start=True, stop=True,
                      skip_group_check=True).then_inc(S("pos_mm"), 1)
                if u % 2 == 1 and u >= 3:
                    shared_down(u // 2 - 1)
            pe.wait_ge(S("xl"), 1)
            pe.wait_ge(S("hm"), SU)
            gather(0)
            shared_down(FC - 1)
            gate_up(0, 0, 0)

            def routed(e, half, last):
                for c in range(1, FC):
                    gate_up(e, c, half)
                    down(e, c - 1, half)
                    if c == 2:
                        slots_to_tokens(e)
                if last:
                    down(e, FC - 1, half)
                    scatter(e, True)
                else:
                    pe.wait_ge(S("st0"), e + 1)
                    pe.wait_ge(S("wsl"), e + 1)
                    gather(e + 1)
                    down(e, FC - 1, half)
                    gate_up(e + 1, 0, 1 - half)
                    scatter(e)

            with pe.Fori(0, E // 2 - 1) as i:
                routed(2 * i, 0, False)
                routed(2 * i + 1, 1, False)
            routed(E - 2, 0, False)
            routed(E - 1, 1, True)

            pe.wait_ge(S("over"), 1)
            more = pe.value_load(over[0:1, 0:1])
            with pe.If(more > 0):
                pe.wait_ge(S("y_read"), 1)
                with pe.Fori(0, E) as i:
                    pe.wait_ge(S("f_raw"), 16 * i + 16)
                    for u in range(SU):
                        c, hf = u // 2, u % 2
                        if u >= 2:
                            pe.wait_ge(S("f_hid"), SU * i + u - 1)
                        for part in range(2):
                            for k in range(DC):
                                o = WOFF[part] + k * FP + c * P
                                last = M(bank(3 + 2 * (u % 2) + part)[:, 0:HT], raw[:, o:o + P],
                                         xnT[:, k, hf * HT:(hf + 1) * HT], start=(k == 0), stop=(k == DC - 1))
                        last.then_inc(S("f_gu"), 1)
                        if hf == 1:
                            pe.wait_ge(S("f_hid"), SU * i + u + 1)
                            for t in range(TT):
                                m = min(P, T - t * P)
                                last = M(bank(t // 2)[0:m, (t % 2) * D:(t % 2 + 1) * D],
                                         hidf[c % 2][:, t * P:t * P + m],
                                         raw[:, WOFF[2] + c * D:WOFF[2] + (c + 1) * D],
                                         start=(c == 0 and t % 2 == 0), stop=(c == FC - 1),
                                         skip_group_check=True)
                    last.then_inc(S("f_dn"), 1)
                    pe.wait_ge(S("f_col"), i + 1)

            def l1(li):
                w = wl1["gl"[li]]
                transposes(li + 2)
                pe.wait_ge(S("nT"), 2 * (li + 2))
                if li == 0:
                    pe.wait_ge(S("d_l1"), 16 * 9)
                    for hf in range(2):
                        for k in range(DC):
                            last = M(bank(4 + hf)[0:LAT, 0:HT], kvd_s[:, k, :], xnT[:, k, hf * HT:(hf + 1) * HT],
                                     start=(k == 0), stop=(k == DC - 1))
                        last.then_inc(S("lat_mm"), 1)
                    pe.wait_ge(S("lat"), 2)
                for b in range(B):
                    for e in range(2):
                        dst = bank(7)[KS * e:KS * e + KS, 2 * DH * b:2 * DH * (b + 1)]
                        if li == 0:
                            last = M(dst, latT[:, b * N:b * N + KS],
                                     vug_s[:, :].rearrange("p (g e d) -> p e g d", e=2, d=DH)[:, e],
                                     start=True, stop=True, skip_group_check=True)
                        else:
                            for k in range(DC):
                                last = M(dst, xnT[:, k, b * N:b * N + KS],
                                         wvl_s[:, k, :].rearrange("p (g e d) -> p e g d", e=2, d=DH)[:, e],
                                         start=(k == 0), stop=(k == DC - 1), skip_group_check=True)
                last.then_inc(S("v1_mm"), 1)
                U = 2 * U5

                def mean_sq(u):
                    pe.wait_ge(S("sqr"), U * li + u + 1)
                    if u == 3:
                        pe.wait_ge(S("vo"), li + 1)
                    if u >= 4:
                        pe.wait_ge(S("rt"), U * li + u - 3)
                    M(bank(4 + u % 4)[:, 0:HT], mean16, sqr[:, u // 2, (u % 2) * HT:(u % 2 + 1) * HT],
                      start=True, stop=True).then_inc(S("ms_mm"), 1)

                for u in range(U):
                    hf = u % 2
                    if u >= 4:
                        pe.wait_ge(S("qkcs"), U * li + u - 3)
                    dst = bank(u % 4)[:, 0:HT]
                    if li == 0 and u // 2 == KV:
                        last = M(dst, kug_s[:, :], latT[:, hf * HT:(hf + 1) * HT], start=True, stop=True)
                    else:
                        for k in range(DC):
                            last = M(dst, w["wq"][:, k, u // 2, :], xnT[:, k, hf * HT:(hf + 1) * HT],
                                     start=(k == 0), stop=(k == DC - 1))
                    last.then_inc(S("qk_mm"), 1)
                    if u >= 2:
                        mean_sq(u - 2)
                mean_sq(U - 2)
                mean_sq(U - 1)
                for hf in range(2):
                    pe.wait_ge(S("qkn"), U * li + U - 1 + hf)
                    M(bank(4 + hf)[:, 0:HT], fold, qk[:, KV, hf * HT:(hf + 1) * HT],
                      start=True, stop=True).then_inc(S("kf_mm"), 1)
                pe.wait_ge(S("kf"), 4 * (li + 1))
                pe.wait_ge(S("kfd"), 4 * (li + 1))
                pe.wait_ge(S("vo"), li + 1)

                def scores(grp):
                    for i in range(4):
                        b = 4 * grp + i
                        if grp >= 1:
                            pe.wait_ge(S("ex"), 16 * li + 4 * (grp - 1) + i + 1)
                        for g in range(KV // 2):
                            last = M(bank(i)[:, g * 4 * N:(g + 1) * 4 * N],
                                     km[:, b, g].rearrange("p e k -> p (e k)"),
                                     qk[:, 0:KV, b * N:(b + 1) * N],
                                     start=True, stop=True, skip_group_check=True)
                        last.then_inc(S("s_mm"), 1)

                def values(grp):
                    if grp >= 2:
                        pe.wait_ge(S("o"), 8 * li + 2 * (grp - 1))
                    for i in range(4):
                        b = 4 * grp + i
                        pe.wait_ge(S("exm"), 16 * li + 4 * grp + i + 1)
                        dst = bank(4 + 2 * (grp % 2) + i // 2)[:, (i % 2) * 4 * N:(i % 2 + 1) * 4 * N]
                        for g in range(KV // 2):
                            last = M(dst[2 * R * g:2 * R * (g + 1)],
                                     vo[:, b, g].rearrange("p e r -> p (e r)"),
                                     ex[grp % 2][:, i, g * 4 * N:(g + 1) * 4 * N],
                                     start=True, stop=True, skip_group_check=True)
                        if i % 2 == 1:
                            last.then_inc(S("o_mm"), 1)

                for grp in range(5):
                    if grp < 4:
                        scores(grp)
                    if grp >= 1:
                        values(grp - 1)
                pe.wait_ge(S("on"), 4 * (li + 1))
                for t in range(TT):
                    for g in range(KV):
                        last = M(bank(t)[:, 0:D], ozp[:, g, t * P:(t + 1) * P],
                                 w["wo"][:, g, :], start=(g == 0), stop=(g == KV - 1))
                    last.then_inc(S("wo1_mm"), 1)

            l1(0)
            l1(1)
            transposes(4)
            pe.wait_ge(S("nT"), 8)
            pe.wait_ge(S("wfs"), 1)
            for t in range(TT):
                M(bank(t)[:, 0:D], ones[0:1, :], sml[0:1, S_BI:S_BI + D], start=True, stop=False)
                for k in range(DC):
                    last = M(bank(t)[:, 0:D], xnT[:, k, t * P:(t + 1) * P], wfs[:, k, :],
                             start=False, stop=(k == DC - 1))
                last.then_inc(S("fin_mm"), 1)


def constants():
    c = np.zeros((P, CW), np.float32)
    c[:, C_ID:C_ID + P] = np.eye(P)
    c[:, C_ONE:C_ONE + P] = 1.0
    p = np.arange(P)
    same = (p[:, None] // R) == (p[None, :] // R)
    c[:, C_FOLD:C_FOLD + P] = same & ((p[:, None] % DH) == (p[None, :] % DH))
    c[:, C_MEAN:C_MEAN + P] = np.where(same, 1.0 / DH, 0.0)
    c[:, C_PICK:C_PICK + R] = (p[:, None] % R) == np.arange(R)[None, :]
    half = DH // 2

    def rotary(base, pos):
        inv = (np.float32(1.0) / np.float32(base) ** (np.arange(half, dtype=np.float32) / np.float32(half)))
        ang = pos.astype(np.float32)[:, None] * inv.astype(np.float32)[None, :]
        cos, sin = np.cos(ang).T, np.sin(ang).T
        return np.tile(np.concatenate([cos, cos, -sin, sin]), (BG, 1))

    c[:, C_CSQ:C_CSQ + N] = rotary(10000.0, np.arange(N))
    c[:, C_CSK:C_CSK + T] = rotary(10000.0, np.arange(T) % N)
    c[:, C_CSG:C_CSG + N] = rotary(1000000.0, np.arange(N))
    c[:, C_CSL:C_CSL + N] = rotary(10000.0, np.arange(N))
    c[:, C_MASK:C_MASK + N] = (p[:, None] % 64) <= np.arange(N)[None, :]
    c[:, C_HM] = p < N
    c[:, C_HM + 1] = (p >= N) & (p < 2 * N)
    c[:, C_HALF:C_HALF + TT] = -0.5
    c[:, C_LT:C_LT + E * E] = np.tril(np.ones((E, E)), -1).reshape(-1)
    c[:, C_EPS] = RMS_EPS
    c[:, C_TRI:C_TRI + P] = np.triu(np.ones((P, P)), 1)
    c[:, C_IOTA:C_IOTA + CAP] = np.arange(CAP)
    c[:, C_VALID:C_VALID + TT] = (p[:, None] + P * np.arange(TT)[None, :]) < T
    s = np.zeros((POSK, TP), np.float32)
    for n in range(N):
        s[n, n:T:N] = 1.0
    s[N, 0:T] = 1.0
    s[N, 0:T:N] = 0.0
    s[N + 1, 0:T:N] = 1.0
    return c, s


def layout(i):
    def arr(n):
        return np.asarray(i[n])

    def chunks(w):
        return np.ascontiguousarray(w.reshape(-1, P, w.shape[1]).transpose(1, 0, 2))

    const, sel = constants()
    out = {"const": const, "sel": sel}
    g = 96 // 16
    x = arr("x").reshape(B, 3, g, 16, g, 16).transpose(1, 3, 5, 0, 2, 4).reshape(PC * P, B, g * g)
    xt = np.zeros((PC * P, TP), np.float32)
    xt[:, 0:T].reshape(PC * P, B, N)[:, :, 1:] = x
    out["xT"] = chunks(xt)
    out["tokW"] = chunks(arr("L0_tok_W").T)
    out["posb"] = np.concatenate([arr("L0_tok_pos_enc")[0], arr("L0_tok_b")[None], arr("L0_tok_cls_token")[0]])

    even, odd = np.arange(0, DH, 2), np.arange(1, DH, 2)
    rows = np.concatenate([even, odd, odd, even])
    perm = np.concatenate([even, odd])
    wq = arr("L0_attn_Wqkv_w").reshape(H, DH, D)[:, rows, :]
    out["wq0"] = chunks(wq.reshape(H * R, D).T)
    bq = arr("L0_attn_Wqkv_b").reshape(H, DH)[:, rows].T
    out["u2t"] = np.concatenate([arr("L0_attn_U")] * 2).T
    wo = arr("L0_attn_Wo_w").T.reshape(H, DH, D)[:, perm, :].reshape(D, D)
    out["wo0"] = chunks(wo)
    sm = np.zeros((P, SW), np.float32)
    sm[:, S_BQ:S_BQ + H] = np.tile(bq, (BG, 1))
    sm[:, S_N1:S_N1 + DC] = arr("L1_attn_norm1_w").reshape(DC, P).T
    sm[:, S_N2:S_N2 + DC] = arr("L1_attn_norm2_w").reshape(DC, P).T
    sm[:, S_SC:S_SC + D] = arr("L1_ffn_scale")
    sm[:, S_BI:S_BI + D] = arr("L1_ffn_bias")
    sm[:, S_RB:S_RB + E] = arr("L0_ffn_router_b")
    out["small"] = sm
    out["rw"] = chunks(arr("L0_ffn_router_w"))

    gw = np.concatenate([arr("L0_ffn_sh_gate_w")[None], arr("L0_ffn_gate_w")])
    uw = np.concatenate([arr("L0_ffn_sh_up_w")[None], arr("L0_ffn_up_w")])
    dw = np.concatenate([arr("L0_ffn_sh_down_w")[None], arr("L0_ffn_down_w")])
    we = np.zeros((E + 1, P, WX), np.float32)
    for e in range(E + 1):
        for part, w in enumerate((gw[e], uw[e])):
            z = np.zeros((D, FP), np.float32)
            z[:, 0:F] = w
            we[e, :, WOFF[part]:WOFF[part] + WPART[part]] = chunks(z).reshape(P, -1)
        z = np.zeros((FP, D), np.float32)
        z[0:F] = dw[e]
        we[e, :, WOFF[2]:] = chunks(z).reshape(P, -1)
    out["wexp"] = we

    def qrot(w):
        k = w.reshape(w.shape[0], KV, -1, DH)[:, :, :, rows].transpose(0, 2, 1, 3)
        return k.reshape(w.shape[0], -1, KV * R)

    def c3(w):
        return np.ascontiguousarray(w.reshape(-1, P, w.shape[1], w.shape[2]).transpose(1, 0, 2, 3))

    def wo1(w):
        z = np.zeros((KV, R, 4, D), np.float32)
        z[:, 0:DH] = w.reshape(KV, 4, DH, D).transpose(0, 2, 1, 3)
        return z.reshape(P, 4, D)

    out["wqg"] = c3(qrot(arr("L1_attn_g_wq")))
    out["kvd"] = chunks(arr("L1_attn_g_kv_down"))
    out["kug"] = qrot(arr("L1_attn_g_k_up"))[:, 0]
    out["vug"] = arr("L1_attn_g_v_up")
    out["wog"] = wo1(arr("L1_attn_g_wo"))
    out["wql"] = c3(np.concatenate([qrot(arr("L1_attn_l_wq")), qrot(arr("L1_attn_l_wk"))], 1))
    out["wvl"] = chunks(arr("L1_attn_l_wv"))
    out["wol"] = wo1(arr("L1_attn_l_wo"))
    out["wfin"] = chunks(arr("L1_ffn_weights").T)
    return {k: np.ascontiguousarray(v) for k, v in out.items()}


_NAMES = ["xT", "tokW", "sel", "posb", "const", "small", "wq0", "u2t", "wo0", "rw", "wexp",
          "wqg", "kvd", "kug", "vug", "wog", "wql", "wvl", "wol", "wfin"]
DEBUG = []


def kernel(**inputs):
    import concourse.bacc as _bacc
    from concourse.bass_utils import run_bass_kernel_spmd as _run

    nc = _bacc.Bacc("TRN2", target_bir_lowering=False, num_devices=1)
    laid = layout(inputs)
    arrays, args = {}, []
    for name in _NAMES:
        arrays[f"in_{name}"] = laid[name]
        args.append(nc.dram_tensor(f"in_{name}", laid[name].shape, F32, kind="ExternalInput").ap())
    out = nc.dram_tensor("out_0", (T, D), F32, kind="ExternalOutput").ap()
    tower(nc, *args, out, None)
    r = _run(nc, [arrays], core_ids=[0])
    return r.results[0]["out_0"].reshape(B, N, D)
```

```python
from contextlib import ExitStack

import numpy as np

import concourse.bass as bass
from concourse import mybir

F32 = mybir.dt.float32
FR = mybir.dt.float32r
I32 = mybir.dt.int32
BF16 = mybir.dt.bfloat16
ALU = mybir.AluOpType
ACT = mybir.ActivationFunctionType
AX_X = mybir.AxisListType.X

P = 128
B = 16
N = 37
D = 256
DC = D // P
T = B * N
TT = -(-T // P)
TP = TT * P
HT = T // 2
PC = 6
POSK = N + 2
H = 16
DH = D // H
R = 2 * DH
BG = 4
B4 = B // BG
G4T = B4 * N
PAIRS = B // 2
HK = P // N
HG = -(-H // HK)
KR = HK * N
KV = 4
KS = 64
LAT = 64
E = 8
F = 688
FC = -(-F // P)
GP = (FC - 1) * P
WPART = (DC * GP, DC * GP + DC * P, FC * D)
WOFF = (0, DC * GP, 2 * DC * GP + DC * P)
WMIX = 2 * DC * GP
UPPER = P // 2
assert F - GP <= UPPER
WX = sum(WPART)
CAP = 256
CT = CAP // P
SU = 2 * FC
MAGIC = 1.5 * 2.0 ** 23
LN_EPS = 1e-5
RMS_EPS = 1e-6
NORMS = 6
BK = 512

C_ID, C_ONE, C_FOLD, C_MEAN = 0, P, 2 * P, 3 * P
C_PICK = 4 * P
EARLY = C_PICK + R
C_CSQ = EARLY
C_CSK = C_CSQ + N
C_CSG = C_CSK + T
C_CSL = C_CSG + N
C_MASK = C_CSL + N
C_HM = C_MASK + N
C_HALF = C_HM + HK
C_LT = C_HALF + 5
C_EPS = C_LT + E * E
C_TRI = C_EPS + 1
C_IOTA = C_TRI + P
C_VALID = C_IOTA + CAP
CW = C_VALID + TT

S_BQ = 0
S_N1 = S_BQ + H
S_N2 = S_N1 + DC
S_SC = S_N2 + DC
S_BI = S_SC + D
S_RB = S_BI + D
SW = S_RB + E


def group_rows(g):
    return min(HK, H - HK * g) * N


def rows_of(c):
    return slice(0, P) if c < FC - 1 else slice(UPPER, P)


def tower(nc, xT, tokW, sel, posb, const, small, wq0, u2t, wo0, rw, wexp,
          wqg, kvd, kug, vug, wog, wql, wvl, wol, wfin, out):
    ctx = ExitStack()
    with ctx:
        def sb(name, shape, dt=F32):
            return ctx.enter_context(nc.sbuf_tensor(name, shape, dt))

        sems = {}

        def S(name):
            if name not in sems:
                sems[name] = ctx.enter_context(nc.semaphore(name))
            return sems[name]

        ps = ctx.enter_context(nc.psum_tensor("ps", [P, 8 * BK], F32))
        psb = ps[:, :].bitcast(BF16)

        def bank(i, n=1):
            return ps[:, i * BK:(i + n) * BK]

        cst = sb("cst", [P, CW])
        sml = sb("sml", [P, SW])
        ident = cst[:, C_ID:C_ID + P]
        ones = cst[:, C_ONE:C_ONE + P]
        fold = cst[:, C_FOLD:C_FOLD + P]
        mean16 = cst[:, C_MEAN:C_MEAN + P]
        identb = sb("identb", [P, P], BF16)

        h = sb("h", [P, TT, D])
        xn = sb("xn", [P, TT, D])
        xnT = sb("xnT", [P, DC, TP])
        stats = sb("stats", [P, TT, 6])
        mv = sb("mv", [P, TT, 2])
        rstd = sb("rstd", [P, TT])
        vtmp = sb("vtmp", [P, TT])

        xh, xl = sb("xh", [P, TT, D], FR), sb("xl", [P, TT, D], FR)
        xTh, xTl = sb("xTh", [P, DC, TP], FR), sb("xTl", [P, DC, TP], FR)
        raw = sb("raw", [P, WX])

        sq0 = sb("sq0", [P, DC, H * R], BF16)
        alq = sb("alq", [P, H])
        thr = sb("thr", [P, 4])
        u2t_s = sb("u2t_s", [R, R])
        m2 = sb("m2", [P, P])
        wo0_s = sb("wo0_s", [P, DC, D])
        wo0q = sb("wo0q", [P, DC, D])
        mab = sb("mab", [P, G4T])
        ma = sb("ma", [P, TT])
        mx = sb("mx", [P, 2, H])
        ma2 = sb("ma2", [P, PAIRS])
        rma = sb("rma", [P, PAIRS])
        rz = sb("rz", [P, 2, H])
        rw_s = sb("rw_s", [P, DC, E])
        lg = sb("lg", [P, TT, E])
        lmx = sb("lmx", [P, TT])
        gt = sb("gt", [P, TT, E, E])
        eq = sb("eq", [P, TT, E, E])
        sel_e = sb("sel_e", [P, TT, E])
        wts = sb("wts", [P, E, TT])
        wleft = sb("wleft", [P, E, TT])
        wparts = sb("wparts", [P, E, TT, 3], BF16)
        wover = sb("wover", [P, E, TT])
        off = sb("off", [P, TT + 1, E])
        slot = sb("slot", [P, E, TT])
        iota = sb("iota", [P, CAP], BF16)
        over = sb("over", [P, 1], I32)

        L0 = 25856
        stage0 = ExitStack()
        arena = stage0.enter_context(nc.sbuf_tensor("stage_l0", [P, L0], F32))
        stage0.close()
        expert_stage = ExitStack()

        def eb(name, shape, dt=FR):
            return expert_stage.enter_context(nc.sbuf_tensor(name, shape, dt))

        wset = [(eb(f"w{i}h", [P, WX]), eb(f"w{i}l", [P, WX])) for i in range(2)]
        hwork = eb("hwork", [P, 2 * FC * TP])
        sf = eb("sf", [P, TT, CAP])
        xg = [eb(f"xg{n}", [P, DC, CAP]) for n in "hl"]
        sbf = [eb(f"sbf{i}", [P, TT, CAP], BF16) for i in range(2)]
        gact = [eb(f"gact{i}", [P, HT], F32) for i in range(2)]
        h32 = [eb(f"h32_{i}", [P, HT], F32) for i in range(2)]
        y32 = eb("y32", [P, CT, D], F32)
        wcur = [eb(f"wcur{i}", [P, TT, 3], BF16) for i in range(2)]
        wsl = eb("wsl", [P, CT], F32)
        hs = [hwork[:, i * FC * TP:(i + 1) * FC * TP].rearrange("p (c t) -> p c t", c=FC) for i in range(2)]
        hr = [hwork[:, i * FC * CAP:(i + 1) * FC * CAP].rearrange("p (c t) -> p c t", c=FC) for i in range(2)]
        o = 2 * FC * CAP
        stf = hwork[:, o:o + CT * TP].rearrange("p (s t) -> p s t", s=CT)
        o += CT * TP
        yhl = [hwork[:, o + i * CT * D:o + (i + 1) * CT * D].rearrange("p (s d) -> p s d", s=CT)
               for i in range(2)]
        expert_stage.close()
        hidf = [xn[:, :, :].rearrange("p a b -> p (a b)")[:, i * TP:(i + 1) * TP] for i in range(2)]

        xT_s = arena[:, 0:PC * TP].rearrange("p (c t) -> p c t", c=PC)
        tokW_s = arena[:, PC * TP:PC * TP + PC * D].rearrange("p (c t) -> p c t", c=PC)
        o = PC * TP + PC * D
        sel_s = arena[:, o:o + TP]
        posb_s = arena[:, o + TP:o + TP + D]

        G4 = B4 * T // B * H
        VW = DH + 1
        at = {}
        o = 0
        for name, width in (("am", G4), ("pr", G4), ("qcs", G4), ("wq0", DC * H * R), ("wabs", DC * H * R),
                            ("sg", DC * H * R // 2), ("sgn", DC * H * R // 2), ("kcs", G4), ("qf", G4),
                            ("vbd", B * HG * HK * VW), ("pe", 2 * H * N), ("pt", 2 * HG * P),
                            ("yq", PAIRS * D), ("yqT", DC * TP)):
            at[name] = arena[:, o:o + width]
            o += width
        assert o == L0
        am = at["am"]
        pr = at["pr"]
        qcs = at["qcs"]
        kcs = at["kcs"]
        qf = at["qf"]
        vbd = at["vbd"]
        wq0_s = at["wq0"].rearrange("p (c m) -> p c m", c=DC)
        wabs = at["wabs"].rearrange("p (c m) -> p c m", c=DC)
        sg = at["sg"].bitcast(BF16).rearrange("p (c m) -> p c m", c=DC)
        sgn = at["sgn"].bitcast(BF16).rearrange("p (c m) -> p c m", c=DC)
        pe_ = [at["pe"][:, i * H * N:(i + 1) * H * N] for i in range(2)]
        ptT = [at["pt"][:, i * HG * P:(i + 1) * HG * P] for i in range(2)]
        yq = at["yq"].rearrange("p (a d) -> p a d", a=PAIRS)
        yqT = at["yqT"].rearrange("p (c t) -> p c t", c=DC)
        xq = at["kcs"][:, 0:TT * D // 2].bitcast(BF16).rearrange("p (t d) -> p t d", t=TT)
        xqT = at["kcs"][:, TT * D // 2:TT * D // 2 + DC * TP // 2].bitcast(BF16).rearrange(
            "p (c t) -> p c t", c=DC)
        dg = at["qf"][:, 0:TT * P].rearrange("p (t q) -> p t q", t=TT)

        stage1 = ExitStack()

        def ab(name, shape, dt=F32):
            return stage1.enter_context(nc.sbuf_tensor(name, shape, dt))

        wl1 = {}
        for n in "gl":
            kd = KV + 1 if n == "l" else KV
            wl1[n] = dict(
                wq=ab(f"wq_{n}", [P, DC, kd, P]),
                wo=ab(f"wo_{n}", [P, KV, D]),
            )
        kvd_s = ab("kvd_s", [P, DC, LAT])
        kug_s = ab("kug_s", [LAT, P])
        vug_s = ab("vug_s", [LAT, KV * DH])
        wvl_s = ab("wvl_s", [P, DC, KV * DH])
        latT = ab("latT", [LAT, TP])
        xres = ab("xres", [P, TT, D])
        U5 = KV + 1
        arena_a = ab("stage_l1a", [P, 2 * U5 * T])
        km = ab("km", [P, B, KV // 2, 2, KS])
        vo = ab("vo", [P, B, KV // 2, 2, R])
        arena_b = ab("stage_l1b", [P, 2 * KV * 2 * 4 * N + 8 * T])
        qk = arena_a[:, 0:U5 * T].rearrange("p (u t) -> p u t", u=U5)
        sqr = arena_a[:, U5 * T:2 * U5 * T].rearrange("p (u t) -> p u t", u=U5)
        QT = 2 * 4 * N
        ex = [arena_b[:, i * KV * QT:(i + 1) * KV * QT].rearrange("p (g c) -> p g c", g=KV)
              for i in range(2)]
        oz = arena_b[:, 2 * KV * QT:2 * KV * QT + 4 * T].rearrange("p (u t) -> p u t", u=4)
        zs = arena_b[:, 2 * KV * QT + 4 * T:2 * KV * QT + 8 * T].rearrange("p (u t) -> p u t", u=4)
        ozp = ab("ozp", [P, KV, TP])

        wfin_s = ab("wfin_s", [P, DC, D])
        wfs = ab("wfs", [P, DC, D])

        stage1.close()

        def value_rows(b, k):
            src = bank(2 * (b % 2), 2)[0:KR, 0:HG * P].rearrange("p (g q r) -> p g q r", g=HG, q=BG)
            dst = vbd.rearrange("p (q b g k w) -> p b k g q w", q=BG, b=B4, g=HG, k=HK)
            return dst[0:KR, b, k, :, :, 0:DH], src[:, :, :, 0:DH], cst[0:KR, C_HM + k:C_HM + k + 1]

        HALVES = [slice(0, HT), slice(HT, TP)]

        UNITS = [(0, 0), (KV, 0), (1, 0), (2, 0), (3, 0), (KV, 1), (0, 1), (1, 1), (2, 1), (3, 1)]
        U = len(UNITS)
        KEYS = [UNITS.index((KV, hf)) for hf in range(2)]

        def unit(x, u):
            q, hf = UNITS[u]
            return x[:, q, hf * HT:(hf + 1) * HT]

        def own_keys(g, hf):
            return km[R * g:R * (g + 1), hf * B // 2:(hf + 1) * B // 2, g // 2, g % 2, 0:N]

        def folded(g, hf):
            return bank(7)[R * g:R * (g + 1), 0:HT].rearrange("p (b n) -> p b n", n=N)

        block = ctx.enter_context(nc.Block())

        @block.sync
        def _(sp):
            for c in range(PC):
                sp.dma_start(xT_s[:, c, :], xT[:, c, :]).then_inc(S(f"d_x{c}"), 16)
                sp.dma_start(tokW_s[:, c, :], tokW[:, c, :]).then_inc(S(f"d_x{c}"), 16)
                if c == 0:
                    sp.dma_start(wq0_s[:, :, :], wq0).then_inc(S("d_wq0"), 16)
                    sp.dma_start(cst[:, 0:EARLY], const[:, 0:EARLY]).then_inc(S("d_cst"), 16)
            sp.dma_start(cst[:, EARLY:CW], const[:, EARLY:CW]).then_inc(S("d_tables"), 16)

            def load(x, part):
                o = WOFF[part]
                sp.dma_start(raw[:, o:o + WPART[part]], wexp[x, :, o:o + WPART[part]]).then_inc(
                    S(f"d_raw{part}"), 16)

            for part in range(3):
                load(0, part)
            with sp.Fori(0, E) as i:
                for part in range(3):
                    sp.wait_ge(S("w_lo"), 3 * i + part + 1)
                    load(i + 1, part)
            sp.wait_ge(S("over"), 1)
            more = sp.value_load(over[0:1, 0:1])
            with sp.If(more > 0):
                sp.wait_ge(S("w_lo"), 3 * (E + 1))
                sp.dma_start(raw[:, :], wexp[1]).then_inc(S("f_raw"), 16)
                with sp.Fori(0, E - 1) as i:
                    sp.wait_ge(S("f_dn"), i + 1)
                    sp.dma_start(raw[:, :], wexp[i + 2]).then_inc(S("f_raw"), 16)
            sp.wait_ge(S("moe"), 1)
            for dst, src in ((kvd_s, kvd), (wl1["g"]["wq"], wqg), (wl1["g"]["wo"], wog),
                             (wl1["l"]["wq"], wql), (wvl_s, wvl), (wl1["l"]["wo"], wol),
                             (wfin_s, wfin)):
                sp.dma_start(dst[:], src).then_inc(S("d_l1"), 16)
            sp.dma_start(kug_s[:, :], kug).then_inc(S("d_l1"), 16)
            sp.dma_start(vug_s[:, :], vug).then_inc(S("d_l1"), 16)
            for t in range(TT):
                rows = min(P, T - t * P)
                sp.wait_ge(S("out_ready"), t + 1)
                sp.dma_start(out[t * P:t * P + rows, :], h[0:rows, t, :]).then_inc(S("d_out"), 16)
            sp.wait_ge(S("d_out"), 16 * TT)

        @block.scalar
        def _(act):
            A = nc.scalar.activation
            act.dma_start(sel_s[0:POSK, :], sel).then_inc(S("d_pos"), 16)
            act.dma_start(posb_s[0:POSK, :], posb).then_inc(S("d_pos"), 16)
            act.dma_start(sml[:, :], small).then_inc(S("d_sml"), 16)
            act.dma_start(u2t_s[:, :], u2t).then_inc(S("d_u2t"), 16)
            act.dma_start(wo0_s[:, :, :], wo0).then_inc(S("d_wo0"), 16)
            act.dma_start(rw_s[:, :, :], rw).then_inc(S("d_rw"), 16)
            act.wait_ge(S("d_wq0"), 16)
            A(wabs[:, :, :], wq0_s[:, :, :], ACT.Abs).then_inc(S("wabs"), 1)
            act.wait_ge(S("wabs_used"), 1)
            act.wait_ge(S("d_wo0"), 16)
            A(wabs[:, :, 0:D], wo0_s[:, :, :], ACT.Abs).then_inc(S("wabs"), 1)

            for t in range(TT):
                act.wait_ge(S("tok"), t + 1)
                A(h[:, t, :], bank(t)[:, 0:D], ACT.Copy).then_inc(S("h0"), 1)

            act.wait_ge(S("xq_t"), 1)
            A(xqT[:, 0, :], psb[:, 5 * 2 * BK:5 * 2 * BK + TP], ACT.Copy).then_inc(S("xqT"), 1)

            act.wait_ge(S("d_sml"), 16)
            for j in range(H):
                act.wait_ge(S("pr"), j // 3 + 1)
                head = pr.rearrange("p (t j) -> p j t", j=H)[:, j, :]
                A(head, head, ACT.Identity, bias=sml[:, S_BQ + j:S_BQ + j + 1]).then_inc(S("biased"), 1)

            def evac_v(b):
                act.wait_ge(S("v_mm"), b + 1)
                for k in range(HK):
                    dst, src, hm = value_rows(b, k)
                    last = A(dst, src, ACT.Copy, scale=hm)
                last.then_inc(S("va"), 1)

            def evac_qf(c):
                w = min(BK, G4 - c * BK)
                act.wait_ge(S("qf_mm"), c + 1)
                A(qf[:, c * BK:c * BK + w], bank(4 + c % 2)[:, 0:w], ACT.Copy).then_inc(S("qf"), 1)

            act.wait_ge(S("d_tables"), 16)
            evac_v(1)
            for c in range(4):
                evac_qf(c)
            evac_v(3)
            evac_qf(4)

            def expo(p):
                act.wait_ge(S("shifted"), p + 1)
                A(pe_[p % 2], pe_[p % 2], ACT.Exp, scale=0.25).then_inc(S("expd"), 1)

            def evac_pt(p):
                act.wait_ge(S("pt_mm"), p + 1)
                if p >= 2:
                    act.wait_ge(S("y_mm"), p - 1)
                A(ptT[p % 2][0:KR, :], bank(4, 2)[0:KR, 0:HG * P], ACT.Copy).then_inc(S("pt"), 1)

            expo(0)
            for p in range(PAIRS):
                evac_pt(p)
                if p + 1 < PAIRS:
                    expo(p + 1)

            act.wait_ge(S("yT_mm"), 1)
            A(yqT[:, 0, 0:T].rearrange("p (a b n) -> p a b n", a=PAIRS, b=2),
              bank(0, 2).rearrange("p (a b n) -> p a b n", a=PAIRS, b=2)[:, :, :, 0:N],
              ACT.Copy).then_inc(S("yT"), 1)

            def evac_T(stage, scale):
                act.wait_ge(S("nT_mm"), stage)
                A(xnT[:, 0, :], bank(4, 2)[:, 0:TP], ACT.Copy if scale is None else ACT.Identity,
                  scale=1.0 if scale is None else scale).then_inc(S("nT"), 1)

            evac_T(1, None)
            act.wait_ge(S("nT"), 2)
            for cols in HALVES:
                A(xTh[:, :, cols], xnT[:, :, cols], ACT.Copy).then_inc(S("xTh"), 1)

            act.wait_ge(S("lg_shift"), 1)
            A(lg[:, :, :], lg[:, :, :], ACT.Exp).then_inc(S("lg_exp"), 1)

            act.wait_ge(S("xn"), TT)
            A(xh[:, :, :], xn[:, :, :], ACT.Copy).then_inc(S("xh"), 1)

            def silu(base, u, c, n, src):
                act.wait_ge(S("gu"), base + u + 1)
                gate = src if c < FC - 1 else src[0:UPPER]
                A(gact[u % 2][rows_of(c), 0:n], gate[:, 0:n], ACT.Silu).then_inc(S("silu"), 1)

            def hid_hi(base, u, c, n, dst):
                act.wait_ge(S("hm"), base + u + 1)
                A(dst[rows_of(c)], h32[u % 2][rows_of(c), 0:n], ACT.Copy).then_inc(S("hh"), 1)

            def weights_hi(x, piece, half, free):
                part, n = piece // 2, WPART[piece // 2] // 2
                o = WOFF[part] + piece % 2 * n
                act.wait_ge(S(f"d_raw{part}"), 16 * x + 16)
                if free is not None:
                    act.wait_ge(S("expert_done"), free)
                A(wset[half][0][:, o:o + n], raw[:, o:o + n], ACT.Copy).then_inc(S("w_hi"), 1)

            def shared_dst(u):
                return hs[0][:, u // 2, (u % 2) * HT:(u % 2 + 1) * HT]

            def gathered_hi(e):
                act.wait_ge(S("g_mm"), e + 1)
                A(xg[0].rearrange("p k s -> p (k s)"), bank(3), ACT.Copy).then_inc(S("xgh"), 1)

            for u in range(SU):
                silu(0, u, u // 2, HT, bank(3 + 2 * (u % 2)))
                hid_hi(0, u, u // 2, HT, shared_dst(u))
                if u < 6:
                    weights_hi(1, u, 1, None)
            gathered_hi(0)

            def routed(e, half, last):
                base = FC * e + SU
                for c in range(FC):
                    silu(base, c, c, CAP, bank(5 + c % 2))
                    hid_hi(base, c, c, CAP, hr[0][:, c, :])
                    if not last:
                        weights_hi(e + 2, c, half, e + 1)
                    if c == 3:
                        act.wait_ge(S("st_mm"), e + 1)
                        A(stf[:, 0, :], psb[:, 6 * BK:6 * BK + TP], ACT.Copy).then_inc(S("st0"), 1)
                if not last:
                    gathered_hi(e + 1)
                act.wait_ge(S("ym"), e + 1)
                A(yhl[0], y32[:, :, :], ACT.Copy).then_inc(S("yh"), 1)

            with act.Fori(0, E // 2 - 1) as i:
                routed(2 * i, 0, False)
                routed(2 * i + 1, 1, False)
            routed(E - 2, 0, False)
            routed(E - 1, 1, True)

            act.wait_ge(S("over"), 1)
            more = act.value_load(over[0:1, 0:1])
            with act.If(more > 0):
                with act.Fori(0, E) as i:
                    for u in range(SU):
                        act.wait_ge(S("f_gu"), SU * i + u + 1)
                        gate = bank(3 + 2 * (u % 2))[:, 0:HT]
                        A(gact[u % 2][rows_of(u // 2), :], gate if u // 2 < FC - 1 else gate[0:UPPER],
                          ACT.Silu).then_inc(S("f_silu"), 1)

            act.wait_ge(S("d_tables"), 16)
            nc.scalar.preload_act_table_set("natural_log_exp_and_others")

            def l1(li):
                evac_T(li + 2, sml[:, (S_N1, S_N2)[li]:(S_N1, S_N2)[li] + 1])
                if li == 0:
                    for hf in range(2):
                        act.wait_ge(S("lat_mm"), hf + 1)
                        A(latT[:, hf * HT:(hf + 1) * HT], bank(4 + hf)[0:LAT, 0:HT],
                          ACT.Copy).then_inc(S("lat"), 1)

                def square(u):
                    act.wait_ge(S("qkcs"), U * li + u + 1)
                    A(unit(sqr, u), unit(qk, u), ACT.Square).then_inc(S("sqr"), 1)

                def inverse_root(u):
                    act.wait_ge(S("ms_mm"), U * li + u + 1)
                    s = unit(sqr, u)
                    A(s, bank(4 + u % 3)[:, 0:HT], ACT.Ln,
                      bias=cst[:, C_EPS:C_EPS + 1]).then_inc(S("ln"), 1)
                    act.wait_ge(S("ln"), U * li + u + 1)
                    A(s, s, ACT.Exp, scale=-0.5).then_inc(S("rt"), 1)

                def take_keys(hf):
                    act.wait_ge(S("kf_mm"), 2 * li + hf + 1)
                    for g in range(2):
                        A(own_keys(g, hf), folded(g, hf), ACT.Copy).then_inc(S("kf"), 1)

                for u in range(U + 2):
                    if u < U:
                        square(u)
                    if u >= 2:
                        inverse_root(u - 2)
                    if u == 7:
                        act.wait_ge(S("zeros"), 2)
                        take_keys(0)
                take_keys(1)

                def evac_o(grp):
                    for i in range(2):
                        act.wait_ge(S("o_mm"), 8 * li + 2 * grp + i + 1)
                        src = bank(4 + 2 * (grp % 2) + i)[:, 0:QT].rearrange(
                            "p (a u n) -> p a u n", a=2, u=4)
                        b = 4 * grp + 2 * i
                        dst = oz.rearrange("p u (b n) -> p b u n", b=B)[:, b:b + 2]
                        A(dst, src, ACT.Copy).then_inc(S("o"), 1)

                def inverse(grp):
                    s = zs[:, :, grp * 4 * N:(grp + 1) * 4 * N]
                    act.wait_ge(S("zs"), 4 * li + grp + 1)
                    A(s, s, ACT.Ln).then_inc(S("lnz"), 1)
                    act.wait_ge(S("lnz"), 4 * li + grp + 1)
                    A(s, s, ACT.Exp, scale=-1.0).then_inc(S("zi"), 1)

                for grp in range(6):
                    if grp < 4:
                        for g in range(KV):
                            act.wait_ge(S("s_mm"), 16 * li + 4 * grp + g + 1)
                            if grp >= 2:
                                act.wait_ge(S("o_mm"), 8 * li + 2 * (grp - 1))
                            A(ex[grp % 2][:, g, :], bank(g)[:, 0:QT], ACT.Exp,
                              scale=0.25).then_inc(S("ex"), 1)
                    if 1 <= grp <= 4:
                        evac_o(grp - 1)
                    if grp >= 2:
                        inverse(grp - 2)

            l1(0)
            l1(1)
            evac_T(4, None)

        @block.vector
        def _(dve):
            V = nc.vector
            chain = [0]

            def link(ins):
                chain[0] += 1
                ins.then_inc(S("dve_chain"), 1)
                dve.wait_ge(S("dve_chain"), chain[0])

            link(V.memset(bank(6, 2), 1.0))
            link(V.memset(m2[:, :], 0.0))
            link(V.memset(off[:, 0, :], 0.0))
            dve.wait_ge(S("d_cst"), 16)
            V.tensor_copy(identb[:, :], ident).then_inc(S("identb"), 1)

            def ternary(w, tmp_p, tmp_n, colsum, factor):
                link(V.reduce_sum(thr[:, 0:1], colsum, AX_X))
                link(V.tensor_scalar(thr[:, 1:2], thr[:, 0:1], factor, None, ALU.mult))
                link(V.tensor_scalar(thr[:, 2:3], thr[:, 1:2], -1.0, None, ALU.mult))
                link(V.tensor_scalar(tmp_p, w, thr[:, 1:2], None, ALU.is_ge))
                link(V.tensor_scalar(tmp_n, w, thr[:, 2:3], None, ALU.is_le))

            dve.wait_ge(S("wabs_used"), 1)
            picked = dg.rearrange("p t q -> p (t q)")[:, 0:H * R].rearrange("p (j r) -> p j r", r=R)
            link(V.tensor_tensor(picked, bank(5)[:, 0:H * R].rearrange("p (j r) -> p j r", r=R),
                                 cst[:, C_PICK:C_PICK + R].unsqueeze(1).to_broadcast([P, H, R]), ALU.mult))
            link(V.reduce_sum(alq[:, :], picked, AX_X))
            link(V.tensor_scalar(alq[:, :], alq[:, :], 1.0 / D, None, ALU.mult))
            ternary(wq0_s[:, :, :], sg[:, :, :], sgn[:, :, :], bank(5)[:, 0:H * R],
                    0.05 / (2.0 * D * D))
            V.tensor_tensor(sq0[:, :, :], sg[:, :, :], sgn[:, :, :], ALU.subtract).then_inc(S("sq0"), 1)
            dve.wait_ge(S("m2_mm"), 1)
            for q in range(4):
                r = slice(32 * q, 32 * q + 32)
                link(V.tensor_copy(m2[r, r], bank(7)[r, 0:R]))
            V.memset(bank(7)[:, 0:R], 1.0).then_inc(S("m2"), 1)

            dve.wait_ge(S("sq0"), 1)
            dve.wait_ge(S("wosum"), 1)
            ternary(wo0_s[:, :, :], sg[:, :, 0:D], sgn[:, :, 0:D], bank(5)[:, 0:D],
                    0.05 / (1.0 * D * D))
            link(V.tensor_tensor(wo0q[:, :, :], sg[:, :, 0:D], sgn[:, :, 0:D], ALU.subtract))
            link(V.tensor_scalar(dg[:, 0:2, :], bank(5)[:, 0:D].rearrange("p (a b) -> p a b", a=2),
                                 1.0 / D, None, ALU.mult))
            V.tensor_tensor(wo0q[:, :, :], wo0q[:, :, :],
                            dg[:, 0:2, :].rearrange("p a b -> p (a b)").unsqueeze(1).to_broadcast([P, DC, D]),
                            ALU.mult).then_inc(S("wo0q"), 1)

            norm_count = [0]

            def tile_stats(src, t):
                V.bn_stats(stats[:, t, :], src[:, t, :]).then_inc(S("bn"), 1)

            def aggregate():
                norm_count[0] += TT
                dve.wait_ge(S("bn"), norm_count[0])
                for t in range(TT):
                    V.bn_aggr(mv[:, t, :], stats[:, t, :]).then_inc(S("bn2"), 1)
                dve.wait_ge(S("bn2"), norm_count[0])

            def moments(src):
                for t in range(TT):
                    tile_stats(src, t)
                aggregate()

            def residual(dst, wait, src):
                for t in range(TT):
                    wait(t)
                    link(V.tensor_tensor(dst[:, t, :], dst[:, t, :], src(t), ALU.add))
                    tile_stats(dst, t)
                aggregate()

            pows = [0]

            def root():
                pows[0] += 1
                dve.wait_ge(S("rstd"), pows[0])

            def layernorm(src, dst, signal=None):
                V.tensor_scalar(vtmp[:, :], mv[:, :, 1], LN_EPS, None, ALU.add).then_inc(S("var"), 1)
                root()
                for t in range(TT):
                    last = V.tensor_scalar(dst[:, t, :], src[:, t, :], mv[:, t, 0:1], rstd[:, t:t + 1],
                                           ALU.subtract, ALU.mult)
                    if signal:
                        last.then_inc(S(signal), 1)
                return last

            def rms_root(mean_square):
                V.tensor_scalar(vtmp[:, :], mean_square, RMS_EPS, None, ALU.add).then_inc(S("var"), 1)
                root()

            def rms_scale(src, dst, signal):
                for t in range(TT):
                    V.tensor_scalar(dst[:, t, :], src[:, t, :], rstd[:, t:t + 1], None,
                                    ALU.mult).then_inc(S(signal), 1)

            dve.wait_ge(S("d_tables"), 16)
            V.tensor_copy(iota[:, :], cst[:, C_IOTA:C_IOTA + CAP]).then_inc(S("iota"), 1)
            for t in range(TT):
                dve.wait_ge(S("h0"), t + 1)
                tile_stats(h, t)
            aggregate()
            link(layernorm(h, xn))
            link(V.tensor_reduce(ma[:, :], xn[:, :, :], AX_X, ALU.max, apply_absolute_value=True))
            link(V.tensor_scalar(ma[:, :], ma[:, :], 1e-6, None, ALU.max))
            link(V.reciprocal(vtmp[:, :], ma[:, :]))
            link(V.tensor_scalar(vtmp[:, :], vtmp[:, :], 7.0, None, ALU.mult))
            for t in range(TT):
                last = V.tensor_scalar(xn[:, t, :], xn[:, t, :], vtmp[:, t:t + 1], MAGIC, ALU.mult, ALU.add)
            link(last)
            V.tensor_scalar(xq[:, :, :], xn[:, :, :], MAGIC, None, ALU.subtract).then_inc(S("xq"), 1)
            V.tensor_tensor(dg[:, :, :], ident.unsqueeze(1).to_broadcast([P, TT, P]),
                            ma[:, :].unsqueeze(2).to_broadcast([P, TT, P]), ALU.mult).then_inc(S("dg"), 1)
            dve.wait_ge(S("xq_t"), 2)
            V.tensor_copy(xqT[:, 1, :], psb[:, 6 * 2 * BK:6 * 2 * BK + TP]).then_inc(S("xqT"), 1)
            dve.wait_ge(S("xqT"), 2)
            dve.wait_ge(S("mab_mm"), 1)
            for q in range(4):
                r = slice(32 * q, 32 * q + 32)
                last = V.tensor_scalar(mab[r, :], ps[r, 3 * BK + q * G4T:3 * BK + (q + 1) * G4T],
                                       1.0 / 7.0, None, ALU.mult)
            last.then_inc(S("mab"), 1)
            link(V.memset(bank(6), 1.0))
            link(V.tensor_tensor(am.rearrange("p (t j) -> p t j", j=H),
                                 mab[:, :].unsqueeze(2).to_broadcast([P, G4T, H]),
                                 alq[:, :].unsqueeze(1).to_broadcast([P, G4T, H]), ALU.mult))
            def projected(jb):
                heads = slice(3 * jb, min(3 * jb + 3, H))
                dve.wait_ge(S("pr_mm"), jb + 1)
                V.tensor_tensor(
                    pr.rearrange("p (t j) -> p j t", j=H)[:, heads, :],
                    bank(jb)[:, 0:(heads.stop - heads.start) * G4T].rearrange("p (j t) -> p j t", t=G4T),
                    am.rearrange("p (t j) -> p j t", j=H)[:, heads, :], ALU.mult).then_inc(S("pr"), 1)

            def queries(jb):
                heads = slice(3 * jb, min(3 * jb + 3, H))
                dve.wait_ge(S("biased"), heads.stop)
                csq = cst[:, C_CSQ:C_CSQ + N].unsqueeze(1).to_broadcast([P, heads.stop - heads.start, N])
                for b in range(B4):
                    last = V.tensor_tensor(
                        qcs.rearrange("p (b j n) -> p b j n", b=B4, j=H)[:, b, heads],
                        pr.rearrange("p (b n j) -> p b j n", b=B4, j=H)[:, b, heads], csq, ALU.mult)
                last.then_inc(S("qcs"), 1)

            for jb in range(6):
                projected(jb)
                if jb >= 2:
                    queries(jb - 2)
            queries(4)
            queries(5)
            vb = vbd.rearrange("p (b g k w) -> p b g k w", b=B, g=HG, k=HK)
            for k in range(HK):
                hm = cst[0:KR, C_HM + k:C_HM + k + 1]
                V.tensor_copy(vb[0:KR, :, :, k, DH].rearrange("p b g -> p (b g)"),
                              hm.to_broadcast([KR, B * HG]))
            for b in (0, 2):
                dve.wait_ge(S("v_mm"), b + 1)
                for k in range(HK):
                    last = V.tensor_scalar(*value_rows(b, k), None, ALU.mult)
                last.then_inc(S("v"), 1)

            def shift(p):
                dve.wait_ge(S("sc_mm"), p + 1)
                s3 = bank(2 * (p % 2), 2).rearrange("p (a c) -> p a c", a=2)[:, :, 0:8 * N]
                for a in range(2):
                    last = V.reduce_max(mx[:, p % 2, 8 * a:8 * a + 8],
                                        s3[:, a].rearrange("p (j m) -> p j m", m=N), AX_X)
                link(last)
                if p >= 2:
                    dve.wait_ge(S("pt_mm"), p - 1)
                for a in range(2):
                    last = V.tensor_tensor(
                        pe_[p % 2].rearrange("p (a j m) -> p a j m", a=2, j=8)[:, a],
                        s3[:, a].rearrange("p (j m) -> p j m", m=N),
                        mx[:, p % 2, 8 * a:8 * a + 8].unsqueeze(2).to_broadcast([P, 8, N]), ALU.subtract)
                last.then_inc(S("shifted"), 1)

            def finish_y(p):
                dve.wait_ge(S("y_mm"), p + 1)
                yv = bank(6 + p % 2)[:, 0:H * VW].rearrange("p (j w) -> p j w", w=VW)
                link(V.reciprocal(rz[:, p % 2, :], yv[:, :, DH]))
                y = yq[:, p, :]
                V.tensor_tensor(y.rearrange("p (j w) -> p j w", w=DH), yv[:, :, 0:DH],
                                rz[:, p % 2, :].unsqueeze(2).to_broadcast([P, H, DH]),
                                ALU.mult).then_inc(S("y"), 1)
                dve.wait_ge(S("y"), p + 1)
                m = ma2[:, p:p + 1]
                link(V.tensor_reduce(m, y, AX_X, ALU.max, apply_absolute_value=True))
                link(V.tensor_scalar(m, m, 1e-6, None, ALU.max))
                link(V.reciprocal(rma[:, p:p + 1], m))
                link(V.tensor_scalar(y, y, rma[:, p:p + 1], 7.0, ALU.mult, ALU.mult))
                link(V.tensor_scalar(y, y, MAGIC, None, ALU.add))
                link(V.tensor_scalar(y, y, MAGIC, m, ALU.subtract, ALU.mult))
                V.tensor_scalar(y, y, 1.0 / 7.0, None, ALU.mult).then_inc(S("yq"), 1)

            for p in range(PAIRS + 2):
                if p < PAIRS:
                    shift(p)
                if p >= 2:
                    finish_y(p - 2)
            V.memset(yqT[:, :, T:TP], 0.0).then_inc(S("yqpad"), 1)
            dve.wait_ge(S("yT_mm"), 2)
            V.tensor_copy(yqT[:, 1, 0:T].rearrange("p (a b n) -> p a b n", a=PAIRS, b=2),
                          bank(2, 2).rearrange("p (a b n) -> p a b n", a=PAIRS, b=2)[:, :, :, 0:N]
                          ).then_inc(S("yT"), 1)
            residual(h, lambda t: dve.wait_ge(S("wo_mm"), t + 1), lambda t: bank(3 + t)[:, 0:D])

            def take_T(stage, scale=None):
                dve.wait_ge(S("nT_mm"), stage)
                if scale is None:
                    V.tensor_copy(xnT[:, 1, :], bank(6, 2)[:, 0:TP]).then_inc(S("nT"), 1)
                else:
                    V.tensor_scalar(xnT[:, 1, :], bank(6, 2)[:, 0:TP], scale, None,
                                    ALU.mult).then_inc(S("nT"), 1)

            layernorm(h, xn, "xn")
            take_T(1)

            for hf, cols in enumerate(HALVES):
                dve.wait_ge(S("xTh"), hf + 1)
                V.tensor_tensor(xTl[:, :, cols], xnT[:, :, cols], xTh[:, :, cols].bitcast(F32),
                                ALU.subtract).then_inc(S("xTl"), 1)
            link(V.memset(hwork[:, :].bitcast(F32).rearrange("p (q t) -> p q t", t=TP)[:, :, T:TP], 0.0))

            dve.wait_ge(S("lg_mm"), 1)
            link(V.tensor_tensor(lg[:, :, :], bank(0)[:, 0:TT * E].rearrange("p (t e) -> p t e", e=E),
                                 sml[:, S_RB:S_RB + E].unsqueeze(1).to_broadcast([P, TT, E]), ALU.add))
            link(V.reduce_max(lmx[:, :], lg[:, :, :], AX_X))
            V.tensor_tensor(lg[:, :, :], lg[:, :, :], lmx[:, :].unsqueeze(2).to_broadcast([P, TT, E]),
                            ALU.subtract).then_inc(S("lg_shift"), 1)
            lt = cst[:, C_LT:C_LT + E * E].rearrange("p (e f) -> p e f", e=E)
            ranks = [P, TT * E, E]
            mine = lg[:, :, :].rearrange("p t e -> p (t e)").unsqueeze(2).to_broadcast(ranks)
            gt2, eq2 = (x[:, :, :, :].rearrange("p t e f -> p (t e) f") for x in (gt, eq))

            def parts_by_token():
                dve.wait_ge(S("xh"), 1)
                V.tensor_tensor(xl[:, :, :], xn[:, :, :], xh[:, :, :].bitcast(F32),
                                ALU.subtract).then_inc(S("xl"), 1)

            def router_probs():
                dve.wait_ge(S("lg_exp"), 1)
                link(V.reduce_sum(lmx[:, :], lg[:, :, :], AX_X))
                link(V.reciprocal(lmx[:, :], lmx[:, :]))
                link(V.tensor_tensor(lg[:, :, :], lg[:, :, :], lmx[:, :].unsqueeze(2).to_broadcast([P, TT, E]),
                                     ALU.mult))
                for t in range(TT):
                    other = lg[:, t, :].unsqueeze(1).to_broadcast([P, E, E])
                    V.tensor_copy(gt[:, t], other).then_inc(S("gt"), 1)
                dve.wait_ge(S("gt"), TT)

            def router_compare():
                link(V.tensor_tensor(eq2, gt2, mine, ALU.is_equal))
                link(V.tensor_tensor(gt2, gt2, mine, ALU.is_gt))
                eq3, gt3 = (x[:, :, :, :].rearrange("p t e f -> p t (e f)") for x in (eq, gt))
                link(V.tensor_tensor(eq3, eq3, lt.rearrange("p e f -> p (e f)").unsqueeze(1).to_broadcast(
                    [P, TT, E * E]), ALU.mult))
                link(V.tensor_tensor(gt3, gt3, eq3, ALU.add))

            def router_select():
                link(V.reduce_sum(sel_e[:, :, :], gt[:, :, :, :], AX_X))
                link(V.tensor_scalar(sel_e[:, :, :], sel_e[:, :, :], 2.0, None, ALU.is_lt))
                valid = cst[:, C_VALID:C_VALID + TT].unsqueeze(2).to_broadcast([P, TT, E])
                V.tensor_tensor(sel_e[:, :, :], sel_e[:, :, :], valid, ALU.mult).then_inc(S("sel"), 1)

            def router_weights():
                dve.wait_ge(S("sel"), 1)
                link(V.tensor_tensor(lg[:, :, :], lg[:, :, :], sel_e[:, :, :], ALU.mult))
                link(V.reduce_sum(lmx[:, :], lg[:, :, :], AX_X))
                link(V.tensor_scalar(lmx[:, :], lmx[:, :], 1e-20, None, ALU.add))
                link(V.reciprocal(lmx[:, :], lmx[:, :]))
                link(V.tensor_tensor(wts[:, :, :].rearrange("p e t -> p t e"), lg[:, :, :],
                                     lmx[:, :].unsqueeze(2).to_broadcast([P, TT, E]), ALU.mult))
                link(V.tensor_copy(wparts[:, :, :, 0], wts[:, :, :]))
                link(V.tensor_tensor(wleft[:, :, :], wts[:, :, :], wparts[:, :, :, 0], ALU.subtract))
                link(V.tensor_copy(wparts[:, :, :, 1], wleft[:, :, :]))
                link(V.tensor_tensor(wparts[:, :, :, 2], wleft[:, :, :], wparts[:, :, :, 1], ALU.subtract))

            def slots():
                dve.wait_ge(S("pos_mm"), 1)
                for t in range(TT):
                    link(V.tensor_tensor(off[:, t + 1, :], off[:, t, :],
                                         bank(7)[:, 64 + t * E:64 + (t + 1) * E], ALU.add))
                link(V.tensor_tensor(gt[:, 0, 0:TT, :], bank(7)[:, 0:TT * E].rearrange("p (t e) -> p t e", e=E),
                                     off[:, 0:TT, :], ALU.add))
                link(V.tensor_scalar(gt[:, 0, 0:TT, :], gt[:, 0, 0:TT, :], 1.0, None, ALU.add))
                link(V.tensor_tensor(gt[:, 0, 0:TT, :], gt[:, 0, 0:TT, :], sel_e[:, :, :], ALU.mult))
                link(V.tensor_scalar(slot[:, :, :].rearrange("p e t -> p t e"), gt[:, 0, 0:TT, :],
                                     1.0, None, ALU.subtract))
                link(V.scalar_tensor_tensor(wover[:, :, :].rearrange("p e t -> p (e t)"),
                                            slot[:, :, :].rearrange("p e t -> p (e t)"), float(CAP),
                                            wts[:, :, :].rearrange("p e t -> p (e t)"), ALU.is_ge, ALU.mult))
                link(V.reduce_max(lmx[:, 0:1], off[:, TT, :], AX_X))
                V.tensor_scalar(over[:, :], lmx[:, 0:1], float(CAP), None, ALU.is_gt).then_inc(S("over"), 1)

            def later(base, u):
                return not isinstance(base, int) or base + u >= 2

            def multiply(base, u, c, n, src):
                dve.wait_ge(S("silu"), base + u + 1)
                if later(base, u):
                    dve.wait_ge(S("hh"), base + u - 1)
                    dve.wait_ge(S("hl"), base + u - 1)
                r = rows_of(c)
                V.tensor_tensor(h32[u % 2][r, 0:n], gact[u % 2][r, 0:n], src[r, 0:n],
                                ALU.mult).then_inc(S("hm"), 1)

            def hid_lo(base, u, c, n, dst, hi):
                r = rows_of(c)
                dve.wait_ge(S("hh"), base + u + 1)
                V.tensor_tensor(dst[r], h32[u % 2][r, 0:n], hi[r].bitcast(F32),
                                ALU.subtract).then_inc(S("hl"), 1)

            def one_hot(e, turn):
                for t in range(TT):
                    last = V.tensor_scalar(sbf[turn][:, t, :], iota[:, :], slot[:, e, t:t + 1], None, ALU.is_equal)
                last.then_inc(S("sbf"), 1)

            def one_hot_fr(e, turn):
                dve.wait_ge(S("sbf"), e + 1)
                V.tensor_copy(wcur[turn][:, :, :], wparts[:, e, :, :]).then_inc(S("wcur"), 1)
                V.tensor_copy(sf[:, :, :], sbf[turn][:, :, :]).then_inc(S("sf"), 1)

            def gathered_lo(e):
                dve.wait_ge(S("g_mm"), e + 1)
                V.tensor_copy(xg[1].rearrange("p k s -> p (k s)"), bank(4)).then_inc(S("xgl"), 1)

            def shared_lo(u):
                s = (slice(None), u // 2, slice((u % 2) * HT, (u % 2 + 1) * HT))
                hid_lo(0, u, u // 2, HT, hs[1][s], hs[0][s])

            for u in range(SU):
                multiply(0, u, u // 2, HT, bank((4 if u // 2 < FC - 1 else 3) + 2 * (u % 2)))
                shared_lo(u)
                steps = {0: router_probs, 1: router_compare, 2: router_select, 3: router_weights,
                         4: parts_by_token, 5: slots, 7: lambda: one_hot(0, 0), 8: lambda: one_hot_fr(0, 0)}
                if u in steps:
                    steps[u]()
            gathered_lo(0)

            def routed(e, turn, last):
                base = FC * e + SU
                for c in range(FC):
                    up = CAP if c < FC - 1 else 0
                    multiply(base, c, c, CAP, bank(5 + c % 2)[:, up:up + CAP])
                    hid_lo(base, c, c, CAP, hr[1][:, c, :], hr[0][:, c, :])
                    if c == 3:
                        dve.wait_ge(S("st_mm"), e + 1)
                        V.tensor_copy(stf[:, 1, :], psb[:, 8 * BK:8 * BK + TP]).then_inc(S("st1"), 1)
                        V.reduce_sum(wsl[:, :], bank(4)[:, TP // 2:TP // 2 + 3 * CT].rearrange(
                            "p (s w) -> p s w", w=3), AX_X).then_inc(S("wsl"), 1)
                    if c == 1 and not last:
                        one_hot(e + 1, 1 - turn)
                    if c == 2 and not last:
                        one_hot_fr(e + 1, 1 - turn)
                if not last:
                    gathered_lo(e + 1)
                dve.wait_ge(S("expert_done"), e + 2)
                dve.wait_ge(S("wsl"), e + 1)
                for s in range(CT):
                    last_ins = V.tensor_scalar(y32[:, s, :], bank(7)[:, s * D:(s + 1) * D], wsl[:, s:s + 1],
                                               None, ALU.mult)
                last_ins.then_inc(S("ym"), 1)
                dve.wait_ge(S("yh"), e + 1)
                V.tensor_tensor(yhl[1], y32[:, :, :], yhl[0].bitcast(F32), ALU.subtract).then_inc(S("yl"), 1)

            with dve.Fori(0, E // 2 - 1) as i:
                routed(2 * i, 0, False)
                routed(2 * i + 1, 1, False)
            routed(E - 2, 0, False)
            routed(E - 1, 1, True)
            for t in range(TT):
                dve.wait_ge(S("y_all"), t // 2 + 1)
                last = V.tensor_tensor(h[:, t, :], h[:, t, :], bank(t // 2)[:, (t % 2) * D:(t % 2 + 1) * D],
                                       ALU.add)
            last.then_inc(S("y_read"), 1)

            dve.wait_ge(S("y_read"), 1)
            more = dve.value_load(over[0:1, 0:1])
            with dve.If(more > 0):
                with dve.Fori(0, E) as i:
                    for u in range(SU):
                        dve.wait_ge(S("f_silu"), SU * i + u + 1)
                        r = rows_of(u // 2)
                        up = bank((4 if u // 2 < FC - 1 else 3) + 2 * (u % 2))[r, 0:HT]
                        V.tensor_tensor(hidf[u // 2 % 2][r, (u % 2) * HT:(u % 2 + 1) * HT], gact[u % 2][r, :],
                                        up, ALU.mult).then_inc(S("f_hid"), 1)
                    dve.wait_ge(S("f_dn"), i + 1)
                    for t in range(TT):
                        last = V.scalar_tensor_tensor(
                            h[:, t, :], bank(t // 2)[:, (t % 2) * D:(t % 2 + 1) * D],
                            wover[:, i, t:t + 1], h[:, t, :], ALU.mult, ALU.add)
                    last.then_inc(S("f_col"), 1)
                    dve.wait_ge(S("f_col"), i + 1)
            V.memset(latT[:, T:TP], 0.0).then_inc(S("moe"), 1)
            link(V.memset(ozp[:, :, T:TP], 0.0))

            def l1(li):
                if li == 0:
                    moments(h)
                    layernorm(h, xres, "res")
                    link(V.tensor_tensor(vtmp[:, :], rstd[:, :], rstd[:, :], ALU.mult))
                    link(V.tensor_tensor(vtmp[:, :], vtmp[:, :], mv[:, :, 1], ALU.mult))
                    dve.wait_ge(S("res"), TT)
                    rms_root(vtmp[:, :])
                else:
                    link(V.tensor_tensor(vtmp[:, :], mv[:, :, 0], mv[:, :, 0], ALU.mult))
                    link(V.tensor_tensor(vtmp[:, :], vtmp[:, :], mv[:, :, 1], ALU.add))
                    rms_root(vtmp[:, :])
                rms_scale(xres, xn, "xn")
                take_T(li + 2, sml[:, (S_N1, S_N2)[li] + 1:(S_N1, S_N2)[li] + 2])
                if li == 1:
                    V.tensor_tensor(h[:, :, :], h[:, :, :], xres[:, :, :], ALU.add).then_inc(S("h_half"), 1)
                cs = cst[:, (C_CSG, C_CSL)[li]:(C_CSG, C_CSL)[li] + N]

                def rotate(u):
                    dve.wait_ge(S("qk_mm"), U * li + u + 1)
                    V.tensor_tensor(unit(qk, u).rearrange("p (b n) -> p b n", n=N),
                                    bank(u % 4)[:, 0:HT].rearrange("p (b n) -> p b n", n=N),
                                    cs.unsqueeze(1).to_broadcast([P, 8, N]), ALU.mult).then_inc(S("qkcs"), 1)

                def normalise(u):
                    dve.wait_ge(S("rt"), U * li + u + 1)
                    V.tensor_tensor(unit(qk, u), unit(qk, u), unit(sqr, u), ALU.mult).then_inc(S("qkn"), 1)

                def take_values():
                    dve.wait_ge(S("v1_mm"), li + 1)
                    for e in range(2):
                        r = slice(KS * e, KS * e + N)
                        last = V.tensor_copy(vo[r, :, :, e, 0:DH].rearrange("p b g d -> p (b g) d"),
                                             bank(3)[r, :].rearrange("p (c d) -> p c d", d=DH))
                    last.then_inc(S("vo"), 1)

                def take_keys(hf):
                    dve.wait_ge(S("kf_mm"), 2 * li + hf + 1)
                    for g in range(2, KV):
                        V.tensor_copy(own_keys(g, hf), folded(g, hf)).then_inc(S("kfd"), 1)

                for u in range(U + 3):
                    if u < U:
                        rotate(u)
                    if u >= 3:
                        normalise(u - 3)
                    if u == 7:
                        dve.wait_ge(S("zeros"), 2)
                        take_keys(0)
                    if u == U + 1:
                        take_values()
                take_keys(1)

                def mask(grp):
                    for g in range(KV):
                        dve.wait_ge(S("ex"), 16 * li + 4 * grp + g + 1)
                        x = ex[grp % 2][:, g, :].rearrange("p (c n) -> p c n", n=N)
                        V.tensor_tensor(x, x, cst[:, C_MASK:C_MASK + N].unsqueeze(1).to_broadcast([P, 8, N]),
                                        ALU.mult).then_inc(S("exm"), 1)

                def sums(grp):
                    dve.wait_ge(S("o"), 8 * li + 2 * grp + 2)
                    s = (slice(None), slice(None), slice(grp * 4 * N, (grp + 1) * 4 * N))
                    V.stream_shuffle(zs[s], oz[s], [DH + i % DH for i in range(32)]).then_inc(S("zs"), 1)

                def divide(grp):
                    s = (slice(None), slice(None), slice(grp * 4 * N, (grp + 1) * 4 * N))
                    dve.wait_ge(S("zi"), 4 * li + grp + 1)
                    V.tensor_tensor(ozp[s], oz[s], zs[s], ALU.mult).then_inc(S("on"), 1)

                for grp in range(6):
                    if grp < 4:
                        mask(grp)
                    if 1 <= grp <= 4:
                        sums(grp - 1)
                    if grp >= 2:
                        divide(grp - 2)
                if li == 0:
                    residual(xres, lambda t: dve.wait_ge(S("wo1_mm"), t + 1), lambda t: bank(t)[:, 0:D])
                else:
                    dve.wait_ge(S("h_half"), 1)
                    residual(h, lambda t: dve.wait_ge(S("wo1_mm"), TT + t + 1), lambda t: bank(t)[:, 0:D])

            l1(0)
            l1(1)
            layernorm(h, xn, "xn")
            take_T(4)
            for t in range(TT):
                dve.wait_ge(S("fin_mm"), t + 1)
                link(V.tensor_scalar(xn[:, t, :], bank(t)[:, 0:D], -100.0, 100.0, ALU.max, ALU.min))
                V.tensor_tensor(h[:, t, :], h[:, t, :], xn[:, t, :], ALU.add).then_inc(S("out_ready"), 1)

        @block.gpsimd
        def _(pool):
            pool.wait_ge(S("d_tables"), 16)
            for n in range(NORMS):
                pool.wait_ge(S("var"), n + 1)
                nc.gpsimd.tensor_tensor(rstd[:, :], vtmp[:, :], cst[:, C_HALF:C_HALF + TT],
                                        ALU.pow).then_inc(S("rstd"), 1)
                if n == 4:
                    pool.wait_ge(S("d_l1"), 16 * 9)
                    nc.gpsimd.tensor_scalar(wfs[:, :, :], wfin_s[:, :, :], 0.0, 2.0, ALU.is_ge,
                                            ALU.mult).then_inc(S("wfs_steps"), 1)
                    pool.wait_ge(S("wfs_steps"), 1)
                    nc.gpsimd.tensor_scalar(wfs[:, :, :], wfs[:, :, :], 1.0, None,
                                            ALU.subtract).then_inc(S("wfs_steps"), 1)
                    pool.wait_ge(S("wfs_steps"), 2)
                    nc.gpsimd.tensor_tensor(wfs[:, :, :], wfs[:, :, :],
                                            sml[:, S_SC:S_SC + D].unsqueeze(1).to_broadcast([P, DC, D]),
                                            ALU.mult).then_inc(S("wfs"), 1)
                if n == 3:
                    nc.gpsimd.memset(vo[:, :, :, :, :], 0.0).then_inc(S("cleared"), 1)
                    pool.wait_ge(S("cleared"), 1)
                    for e in range(2):
                        last = nc.gpsimd.memset(vo[KS * e:KS * e + N, :, :, e, DH:R].rearrange(
                            "p b g d -> p (b g) d"), 1.0)
                    last.then_inc(S("zeros"), 1)
                    pool.wait_ge(S("zeros"), 1)
                    nc.gpsimd.memset(km[:, :, :, :, :], 0.0).then_inc(S("zeros"), 1)
                if n == 0:
                    pool.wait_ge(S("biased"), H)
                    nc.gpsimd.tensor_tensor(
                        kcs.rearrange("p (b r) -> p b r", b=B4), pr.rearrange("p (b r) -> p b r", b=B4),
                        cst[:, C_CSK:C_CSK + T].unsqueeze(1).to_broadcast([P, B4, T]),
                        ALU.mult).then_inc(S("kcs"), 1)
                    pool.wait_ge(S("kcs"), 1)
                    pool.wait_ge(S("v_mm"), B4)
                    pool.wait_ge(S("qf"), 5)
                    for part in range(3):
                        pool.wait_ge(S(f"d_raw{part}"), 16)
                        o = WOFF[part]
                        w = (slice(None), slice(o, o + WPART[part]))
                        nc.gpsimd.tensor_copy(wset[0][0][w], raw[w]).then_inc(S("w_hi0"), 1)
                        pool.wait_ge(S("w_hi0"), part + 1)
                        nc.gpsimd.tensor_tensor(wset[0][1][w], raw[w], wset[0][0][w].bitcast(F32),
                                                ALU.subtract).then_inc(S("w_lo"), 1)
                if n == 1:
                    with pool.Fori(0, E // 2) as i:
                        for half in range(2):
                            for part in range(3):
                                o = WOFF[part]
                                w = (slice(None), slice(o, o + WPART[part]))
                                pool.wait_ge(S("w_hi"), 12 * i + 6 * half + 2 * part + 2)
                                nc.gpsimd.tensor_tensor(wset[1 - half][1][w], raw[w],
                                                        wset[1 - half][0][w].bitcast(F32),
                                                        ALU.subtract).then_inc(S("w_lo"), 1)

        @block.tensor
        def _(pe):
            M = nc.tensor.matmul

            def keep_clock(n, b):
                for _ in range(n):
                    M(bank(b), ones, cst[:, 0:BK], start=True, stop=True)

            pe.wait_ge(S("dve_chain"), 1)
            for c in range(PC):
                pe.wait_ge(S(f"d_x{c}"), 32)
                for t in range(TT):
                    M(bank(t)[:, 0:D], xT_s[:, c, t * P:(t + 1) * P], tokW_s[:, c, :],
                      start=(c == 0), stop=False)
                if c == 1:
                    pe.wait_ge(S("d_cst"), 16)
                    pe.wait_ge(S("wabs"), 1)
                    for k in range(DC):
                        last = M(bank(5)[:, 0:H * R], ones, wabs[:, k, :], start=(k == 0), stop=(k == DC - 1))
                    last.then_inc(S("wabs_used"), 1)
                    pe.wait_ge(S("d_u2t"), 16)
                    for q in range(4):
                        last = M(bank(7)[32 * q:32 * q + 32, 0:R], u2t_s[:, :], u2t_s[:, :],
                                 start=True, stop=True)
                    last.then_inc(S("m2_mm"), 1)
                if c == PC - 3:
                    pe.wait_ge(S("wabs"), 2)
                    pe.wait_ge(S("sq0"), 1)
                    for k in range(DC):
                        last = M(bank(5)[:, 0:D], ones, wabs[:, k, 0:D], start=(k == 0), stop=(k == DC - 1))
                    last.then_inc(S("wosum"), 1)
            pe.wait_ge(S("d_pos"), 32)
            for t in range(TT):
                M(bank(t)[:, 0:D], sel_s[0:POSK, t * P:(t + 1) * P], posb_s[0:POSK, :],
                  start=False, stop=True).then_inc(S("tok"), 1)

            pe.wait_ge(S("m2"), 1)
            keep_clock(9, 7)
            pe.wait_ge(S("xq"), 1)
            pe.wait_ge(S("wo0q"), 1)
            pe.wait_ge(S("identb"), 1)
            for k in range(DC):
                for t in range(TT):
                    last = nc.tensor.transpose(psb[:, (5 + k) * 2 * BK + t * P:(5 + k) * 2 * BK + (t + 1) * P],
                                               xq[:, t, k * P:(k + 1) * P], identb[:, :])
                last.then_inc(S("xq_t"), 1)
            pe.wait_ge(S("dg"), 1)
            M(bank(3), ones, dg[:, 0:4, :].rearrange("p a b -> p (a b)"), start=True, stop=True)
            M(bank(4)[:, 0:P], ones, dg[:, 4, :], start=True, stop=True).then_inc(S("mab_mm"), 1)
            pe.wait_ge(S("xqT"), 2)
            pe.wait_ge(S("mab"), 1)
            for j in range(H):
                for q in range(4):
                    for k in range(DC):
                        last = M(ps[32 * q:32 * q + 32, (j // 3) * BK + (j % 3) * G4T:(j // 3) * BK + (j % 3 + 1) * G4T],
                                 sq0[:, k, R * j:R * j + R], xqT[:, k, q * G4T:(q + 1) * G4T],
                                 start=(k == 0), stop=(k == DC - 1), skip_group_check=True)
                if j % 3 == 2 or j == H - 1:
                    last.then_inc(S("pr_mm"), 1)
            keep_clock(4, 7)
            pe.wait_ge(S("biased"), H)
            def queries(c):
                w = min(BK, G4 - c * BK)
                if c >= 2:
                    pe.wait_ge(S("qf"), c - 1)
                M(bank(4 + c % 2)[:, 0:w], m2[:, :], qcs[:, c * BK:c * BK + w],
                  start=True, stop=True).then_inc(S("qf_mm"), 1)

            def value_keys(b):
                if b >= 2:
                    pe.wait_ge(S(("v", "va")[b % 2]), 1)
                for g in range(HG):
                    last = nc.tensor.transpose(
                        ps[0:group_rows(g), 2 * (b % 2) * BK + g * P:2 * (b % 2) * BK + (g + 1) * P],
                        pr[:, b * T + KR * g:b * T + KR * g + group_rows(g)], ident)
                last.then_inc(S("v_mm"), 1)

            value_keys(0)
            value_keys(1)
            pe.wait_ge(S("qcs"), 6)
            queries(0)
            queries(1)
            value_keys(2)
            queries(2)
            queries(3)
            value_keys(3)
            queries(4)

            def scores(p):
                q = p // 2
                if p == 0:
                    pe.wait_ge(S("qf"), 5)
                    pe.wait_ge(S("kcs"), 1)
                if p < 2:
                    pe.wait_ge(S("v"), 2)
                    pe.wait_ge(S("va"), 2)
                else:
                    pe.wait_ge(S("shifted"), p - 1)
                for j in range(H):
                    for par in range(2):
                        b = 2 * (p % 2) + par
                        last = M(ps[64 * par:64 * par + N, (2 * (p % 2) + j // 8) * BK + (j % 8) * N:
                                    (2 * (p % 2) + j // 8) * BK + (j % 8 + 1) * N],
                                 qf[32 * q:32 * q + 32, (b * H + j) * N:(b * H + j + 1) * N],
                                 kcs[32 * q:32 * q + 32, b * T + j * N:b * T + (j + 1) * N],
                                 start=True, stop=True, skip_group_check=True)
                last.then_inc(S("sc_mm"), 1)

            def probs_T(p):
                pe.wait_ge(S("expd"), p + 1)
                if p >= 1:
                    pe.wait_ge(S("pt"), p)
                for g in range(HG):
                    last = nc.tensor.transpose(ps[0:group_rows(g), 4 * BK + g * P:4 * BK + (g + 1) * P],
                                               pe_[p % 2][:, KR * g:KR * g + group_rows(g)], ident)
                last.then_inc(S("pt_mm"), 1)

            def values(p):
                pe.wait_ge(S("pt"), p + 1)
                if p >= 2:
                    pe.wait_ge(S("y"), p - 1)
                for g in range(HG):
                    for par in range(2):
                        o = ((2 * p + par) * HG + g) * HK * VW
                        rows, width = group_rows(g), group_rows(g) // N * VW
                        y = (6 + p % 2) * BK + HK * VW * g
                        last = M(ps[64 * par:64 * par + N, y:y + width],
                                 ptT[p % 2][0:rows, g * P + 64 * par:g * P + 64 * par + N],
                                 vbd[0:rows, o:o + width], start=True, stop=True, skip_group_check=True)
                last.then_inc(S("y_mm"), 1)

            scores(0)
            scores(1)
            for p in range(PAIRS):
                probs_T(p)
                if p + 2 < PAIRS:
                    scores(p + 2)
                values(p)
            for p in range(PAIRS):
                pe.wait_ge(S("yq"), p + 1)
                for k in range(DC):
                    last = nc.tensor.transpose(ps[:, 2 * k * BK + p * P:2 * k * BK + (p + 1) * P],
                                               yq[:, p, k * P:(k + 1) * P], ident)
                    if p == PAIRS - 1:
                        last.then_inc(S("yT_mm"), 1)
            keep_clock(1, 7)
            pe.wait_ge(S("yT"), 2)
            pe.wait_ge(S("yqpad"), 1)
            for t in range(TT):
                for k in range(DC):
                    last = M(bank(3 + t)[:, 0:D], yqT[:, k, t * P:(t + 1) * P],
                             wo0q[:, k, :], start=(k == 0), stop=(k == DC - 1))
                last.then_inc(S("wo_mm"), 1)

            def transposes(stage):
                for t in range(TT):
                    pe.wait_ge(S("xn"), TT * (stage - 1) + t + 1)
                    for k in range(DC):
                        last = nc.tensor.transpose(ps[:, (4 + 2 * k) * BK + t * P:(4 + 2 * k) * BK + (t + 1) * P],
                                                   xn[:, t, k * P:(k + 1) * P], ident)
                last.then_inc(S("nT_mm"), 1)

            keep_clock(3, 0)
            transposes(1)
            pe.wait_ge(S("nT"), 2)
            pe.wait_ge(S("d_rw"), 16)
            for t in range(TT):
                for k in range(DC):
                    last = M(bank(0)[:, t * E:(t + 1) * E], xnT[:, k, t * P:(t + 1) * P], rw_s[:, k, :],
                             start=(k == 0), stop=(k == DC - 1), skip_group_check=True)
            last.then_inc(S("lg_mm"), 1)

            def split3(dst, a, b, start, stop, skip=False):
                M(dst, a[0], b[0], start=start, stop=False, skip_group_check=skip)
                M(dst, a[0], b[1], start=False, stop=False, skip_group_check=skip)
                return M(dst, a[1], b[0], start=False, stop=stop, skip_group_check=skip)

            def chunk_at(part, k, c):
                return WOFF[part] + k * GP + c * P if c < FC - 1 else WMIX + k * P

            def parts_of(c):
                return range(2 if c < FC - 1 else 1)

            def gate_up_chunk(w, part, k, c):
                o = chunk_at(part, k, c)
                return [w[i][:, o:o + P] for i in range(2)]

            def shared_gate_up(u):
                c, hf = u // 2, u % 2
                if u < 2:
                    pe.wait_ge(S("xTl"), hf + 1)
                if u >= 2:
                    pe.wait_ge(S("hm"), u - 1)
                for part in parts_of(c):
                    for k in range(DC):
                        last = split3(bank(3 + 2 * (u % 2) + part)[:, 0:HT],
                                      gate_up_chunk(wset[0], part, k, c),
                                      [x[:, k, hf * HT:(hf + 1) * HT] for x in (xTh, xTl)],
                                      k == 0, k == DC - 1)
                last.then_inc(S("gu"), 1)

            def shared_down(c):
                pe.wait_ge(S("hl"), 2 * c + 2)
                o = WOFF[2] + c * D
                for t in range(TT):
                    last = split3(bank(t // 2)[:, (t % 2) * D:(t % 2 + 1) * D],
                                  [x[rows_of(c), c, t * P:(t + 1) * P] for x in hs],
                                  [w[rows_of(c), o:o + D] for w in wset[0]],
                                  c == 0 and t % 2 == 0, False, True)
                if c == FC - 1:
                    last.then_inc(S("expert_done"), 1)

            def gather(e):
                pe.wait_ge(S("sf"), e + 1)
                for b, x in ((3, xh), (4, xl)):
                    for k in range(DC):
                        for t in range(TT):
                            last = M(bank(b)[:, k * CAP:(k + 1) * CAP], x[:, t, k * P:(k + 1) * P],
                                     sf[:, t, :], start=(t == 0), stop=(t == TT - 1), skip_group_check=True)
                last.then_inc(S("g_mm"), 1)

            def gate_up(e, c, half):
                w = wset[1 - half]
                base = FC * e + SU
                if c == 0:
                    pe.wait_ge(S("xgh"), e + 1)
                    pe.wait_ge(S("xgl"), e + 1)
                    pe.wait_ge(S("w_lo"), 3 * e + 5)
                pe.wait_ge(S("hm"), base + c - 1)
                for part in parts_of(c):
                    for k in range(DC):
                        last = split3(bank(5 + c % 2)[:, part * CAP:(part + 1) * CAP],
                                      gate_up_chunk(w, part, k, c),
                                      [x[:, k, :] for x in xg], k == 0, k == DC - 1, True)
                last.then_inc(S("gu"), 1)

            def down(e, c, half):
                w = wset[1 - half]
                if c == 0:
                    pe.wait_ge(S("w_lo"), 3 * e + 6)
                pe.wait_ge(S("hl"), FC * e + SU + c + 1)
                o = WOFF[2] + c * D
                for s in range(CT):
                    last = split3(bank(7)[:, s * D:(s + 1) * D],
                                  [x[rows_of(c), c, s * P:(s + 1) * P] for x in hr],
                                  [v[rows_of(c), o:o + D] for v in w],
                                  c == 0 and s == 0, c == FC - 1, True)
                if c == FC - 1:
                    last.then_inc(S("expert_done"), 1)

            def slots_to_tokens(e, turn):
                for s in range(CT):
                    for t in range(TT):
                        nc.tensor.transpose(psb[:, (3 + s) * 2 * BK + t * P:(3 + s) * 2 * BK + (t + 1) * P],
                                            sbf[turn][:, t, s * P:(s + 1) * P], identb[:, :])
                for s in range(CT):
                    for t in range(TT):
                        last = M(bank(4)[:, TP // 2 + 3 * s:TP // 2 + 3 * s + 3],
                                 sbf[turn][:, t, s * P:(s + 1) * P], wcur[turn][:, t, :],
                                 start=(t == 0), stop=(t == TT - 1), skip_group_check=True)
                last.then_inc(S("st_mm"), 1)

            def scatter(e, final=False):
                pe.wait_ge(S("yl"), e + 1)
                pe.wait_ge(S("st0"), e + 1)
                pe.wait_ge(S("st1"), e + 1)
                for t in range(TT):
                    for s in range(CT):
                        for y in yhl:
                            last = M(bank(t // 2)[:, (t % 2) * D:(t % 2 + 1) * D], stf[:, s, t * P:(t + 1) * P],
                                     y[:, s, :], start=False, stop=False, skip_group_check=True)
                    if final and (t % 2 == 1 or t == TT - 1):
                        last.then_inc(S("y_all"), 1)

            pe.wait_ge(S("lg_shift"), 1)
            pe.wait_ge(S("w_lo"), 3)
            for u in range(SU):
                shared_gate_up(u)
                if u == 4:
                    pe.wait_ge(S("sel"), 1)
                    sel2 = sel_e[:, :, :].rearrange("p t e -> p (t e)")
                    M(bank(7)[:, 0:TT * E], cst[:, C_TRI:C_TRI + P], sel2, start=True, stop=True,
                      skip_group_check=True)
                    M(bank(7)[:, 64:64 + TT * E], ones, sel2, start=True, stop=True,
                      skip_group_check=True).then_inc(S("pos_mm"), 1)
                if u % 2 == 1 and u >= 3:
                    shared_down(u // 2 - 1)
            pe.wait_ge(S("xl"), 1)
            pe.wait_ge(S("hm"), SU)
            gather(0)
            shared_down(FC - 1)
            gate_up(0, 0, 0)
            gate_up(0, 1, 0)

            def routed(e, half, last):
                down(e, 0, half)
                for c in range(2, FC):
                    gate_up(e, c, half)
                    if c < FC - 1:
                        down(e, c - 1, half)
                    if c == 2:
                        slots_to_tokens(e, half)
                if not last:
                    pe.wait_ge(S("st0"), e + 1)
                    pe.wait_ge(S("wsl"), e + 1)
                    gather(e + 1)
                down(e, FC - 2, half)
                down(e, FC - 1, half)
                if not last:
                    gate_up(e + 1, 0, 1 - half)
                    gate_up(e + 1, 1, 1 - half)
                if last:
                    keep_clock(2, 5)
                scatter(e, last)

            with pe.Fori(0, E // 2 - 1) as i:
                routed(2 * i, 0, False)
                routed(2 * i + 1, 1, False)
            routed(E - 2, 0, False)
            routed(E - 1, 1, True)

            pe.wait_ge(S("over"), 1)
            more = pe.value_load(over[0:1, 0:1])
            with pe.If(more > 0):
                pe.wait_ge(S("y_read"), 1)
                with pe.Fori(0, E) as i:
                    pe.wait_ge(S("f_raw"), 16 * i + 16)
                    for u in range(SU):
                        c, hf = u // 2, u % 2
                        if u >= 2:
                            pe.wait_ge(S("f_hid"), SU * i + u - 1)
                        for part in parts_of(c):
                            for k in range(DC):
                                o = chunk_at(part, k, c)
                                last = M(bank(3 + 2 * (u % 2) + part)[:, 0:HT], raw[:, o:o + P],
                                         xnT[:, k, hf * HT:(hf + 1) * HT], start=(k == 0), stop=(k == DC - 1))
                        last.then_inc(S("f_gu"), 1)
                        if hf == 1:
                            pe.wait_ge(S("f_hid"), SU * i + u + 1)
                            for t in range(TT):
                                m = min(P, T - t * P)
                                last = M(bank(t // 2)[0:m, (t % 2) * D:(t % 2 + 1) * D],
                                         hidf[c % 2][rows_of(c), t * P:t * P + m],
                                         raw[rows_of(c), WOFF[2] + c * D:WOFF[2] + (c + 1) * D],
                                         start=(c == 0 and t % 2 == 0), stop=(c == FC - 1),
                                         skip_group_check=True)
                    last.then_inc(S("f_dn"), 1)
                    pe.wait_ge(S("f_col"), i + 1)

            def l1(li):
                w = wl1["gl"[li]]
                keep_clock((9, 4)[li], (3, 7)[li])
                transposes(li + 2)
                pe.wait_ge(S("nT"), 2 * (li + 2))
                if li == 0:
                    pe.wait_ge(S("d_l1"), 16 * 9)
                    for hf in range(2):
                        for k in range(DC):
                            last = M(bank(4 + hf)[0:LAT, 0:HT], kvd_s[:, k, :], xnT[:, k, hf * HT:(hf + 1) * HT],
                                     start=(k == 0), stop=(k == DC - 1))
                        last.then_inc(S("lat_mm"), 1)

                def project(u):
                    q, hf = UNITS[u]
                    if u >= 4:
                        pe.wait_ge(S("qkcs"), U * li + u - 3)
                    dst = bank(u % 4)[:, 0:HT]
                    if li == 0 and q == KV:
                        pe.wait_ge(S("lat"), hf + 1)
                        last = M(dst, kug_s[:, :], latT[:, hf * HT:(hf + 1) * HT], start=True, stop=True)
                    else:
                        for k in range(DC):
                            last = M(dst, w["wq"][:, k, q, :], xnT[:, k, hf * HT:(hf + 1) * HT],
                                     start=(k == 0), stop=(k == DC - 1))
                    last.then_inc(S("qk_mm"), 1)

                def mean_square(u):
                    pe.wait_ge(S("sqr"), U * li + u + 1)
                    if li == 0 and u == 0:
                        pe.wait_ge(S("lat"), 2)
                    if u >= 3:
                        pe.wait_ge(S("rt"), U * li + u - 2)
                    M(bank(4 + u % 3)[:, 0:HT], mean16, unit(sqr, u),
                      start=True, stop=True).then_inc(S("ms_mm"), 1)

                def fold_keys(hf):
                    pe.wait_ge(S("qkn"), U * li + KEYS[hf] + 1)
                    if hf == 1:
                        pe.wait_ge(S("kf"), 4 * li + 2)
                        pe.wait_ge(S("kfd"), 4 * li + 2)
                    M(bank(7)[:, 0:HT], fold, qk[:, KV, hf * HT:(hf + 1) * HT],
                      start=True, stop=True).then_inc(S("kf_mm"), 1)

                def project_values():
                    pe.wait_ge(S("qkcs"), U * li + 8)
                    for b in range(B):
                        for e in range(2):
                            dst = bank(3)[KS * e:KS * e + KS, 2 * DH * b:2 * DH * (b + 1)]
                            if li == 0:
                                last = M(dst, latT[:, b * N:b * N + KS],
                                         vug_s[:, :].rearrange("p (g e d) -> p e g d", e=2, d=DH)[:, e],
                                         start=True, stop=True, skip_group_check=True)
                            else:
                                for k in range(DC):
                                    last = M(dst, xnT[:, k, b * N:b * N + KS],
                                             wvl_s[:, k, :].rearrange("p (g e d) -> p e g d", e=2, d=DH)[:, e],
                                             start=(k == 0), stop=(k == DC - 1), skip_group_check=True)
                    last.then_inc(S("v1_mm"), 1)

                for u in range(U):
                    project(u)
                    if u >= 2:
                        mean_square(u - 2)
                    if u == 6:
                        fold_keys(0)
                project_values()
                mean_square(U - 2)
                mean_square(U - 1)
                fold_keys(1)

                def scores(grp):
                    if grp == 0:
                        pe.wait_ge(S("qkn"), U * li + U // 2)
                        pe.wait_ge(S("kf"), 4 * li + 2)
                        pe.wait_ge(S("kfd"), 4 * li + 2)
                        pe.wait_ge(S("qkcs"), U * (li + 1))
                    if grp == 2:
                        pe.wait_ge(S("qkn"), U * (li + 1))
                        pe.wait_ge(S("kf"), 4 * (li + 1))
                        pe.wait_ge(S("kfd"), 4 * (li + 1))
                    for i in range(4):
                        b = 4 * grp + i
                        if grp >= 1:
                            pe.wait_ge(S("ex"), 16 * li + 4 * (grp - 1) + i + 1)
                        if grp == 0 and i == 3:
                            pe.wait_ge(S("vo"), li + 1)
                        for g in range(KV // 2):
                            last = M(bank(i)[:, g * 4 * N:(g + 1) * 4 * N],
                                     km[:, b, g].rearrange("p e k -> p (e k)"),
                                     qk[:, 0:KV, b * N:(b + 1) * N],
                                     start=True, stop=True, skip_group_check=True)
                        last.then_inc(S("s_mm"), 1)

                def values(grp):
                    if grp == 0:
                        pe.wait_ge(S("rt"), U * (li + 1))
                    if grp >= 2:
                        pe.wait_ge(S("o"), 8 * li + 2 * (grp - 1))
                    for i in range(4):
                        b = 4 * grp + i
                        pe.wait_ge(S("exm"), 16 * li + 4 * grp + i + 1)
                        dst = bank(4 + 2 * (grp % 2) + i // 2)[:, (i % 2) * 4 * N:(i % 2 + 1) * 4 * N]
                        for g in range(KV // 2):
                            last = M(dst[2 * R * g:2 * R * (g + 1)],
                                     vo[:, b, g].rearrange("p e r -> p (e r)"),
                                     ex[grp % 2][:, i, g * 4 * N:(g + 1) * 4 * N],
                                     start=True, stop=True, skip_group_check=True)
                        if i % 2 == 1:
                            last.then_inc(S("o_mm"), 1)

                for grp in range(5):
                    if grp < 4:
                        scores(grp)
                    if grp >= 1:
                        values(grp - 1)
                for t in range(TT):
                    pe.wait_ge(S("on"), 4 * li + (min((t + 1) * P, T) - 1) // (4 * N) + 1)
                    for g in range(KV):
                        last = M(bank(t)[:, 0:D], ozp[:, g, t * P:(t + 1) * P],
                                 w["wo"][:, g, :], start=(g == 0), stop=(g == KV - 1))
                    last.then_inc(S("wo1_mm"), 1)

            l1(0)
            l1(1)
            keep_clock(3, 7)
            transposes(4)

            def bias(t):
                M(bank(t)[:, 0:D], ones[0:1, :], sml[0:1, S_BI:S_BI + D], start=True, stop=False)

            for t in range(4):
                bias(t)
            pe.wait_ge(S("nT"), 8)
            pe.wait_ge(S("wfs"), 1)
            for t in range(TT):
                if t >= 4:
                    bias(t)
                for k in range(DC):
                    last = M(bank(t)[:, 0:D], xnT[:, k, t * P:(t + 1) * P], wfs[:, k, :],
                             start=False, stop=(k == DC - 1))
                last.then_inc(S("fin_mm"), 1)


def constants():
    c = np.zeros((P, CW), np.float32)
    c[:, C_ID:C_ID + P] = np.eye(P)
    c[:, C_ONE:C_ONE + P] = 1.0
    p = np.arange(P)
    same = (p[:, None] // R) == (p[None, :] // R)
    c[:, C_FOLD:C_FOLD + P] = same & ((p[:, None] % DH) == (p[None, :] % DH))
    c[:, C_MEAN:C_MEAN + P] = np.where(same, 1.0 / DH, 0.0)
    c[:, C_PICK:C_PICK + R] = (p[:, None] % R) == np.arange(R)[None, :]
    half = DH // 2

    def rotary(base, pos):
        inv = (np.float32(1.0) / np.float32(base) ** (np.arange(half, dtype=np.float32) / np.float32(half)))
        ang = pos.astype(np.float32)[:, None] * inv.astype(np.float32)[None, :]
        cos, sin = np.cos(ang).T, np.sin(ang).T
        return np.tile(np.concatenate([cos, cos, -sin, sin]), (BG, 1))

    c[:, C_CSQ:C_CSQ + N] = rotary(10000.0, np.arange(N))
    c[:, C_CSK:C_CSK + T] = rotary(10000.0, np.arange(T) % N)
    c[:, C_CSG:C_CSG + N] = rotary(1000000.0, np.arange(N))
    c[:, C_CSL:C_CSL + N] = rotary(10000.0, np.arange(N))
    c[:, C_MASK:C_MASK + N] = (p[:, None] % 64) <= np.arange(N)[None, :]
    c[:, C_HM:C_HM + HK] = (p // N)[:, None] == np.arange(HK)[None, :]
    c[:, C_HALF:C_HALF + TT] = -0.5
    c[:, C_LT:C_LT + E * E] = np.tril(np.ones((E, E)), -1).reshape(-1)
    c[:, C_EPS] = RMS_EPS
    c[:, C_TRI:C_TRI + P] = np.triu(np.ones((P, P)), 1)
    c[:, C_IOTA:C_IOTA + CAP] = np.arange(CAP)
    c[:, C_VALID:C_VALID + TT] = (p[:, None] + P * np.arange(TT)[None, :]) < T
    s = np.zeros((POSK, TP), np.float32)
    for n in range(N):
        s[n, n:T:N] = 1.0
    s[N, 0:T] = 1.0
    s[N, 0:T:N] = 0.0
    s[N + 1, 0:T:N] = 1.0
    return c, s


def layout(i):
    def arr(n):
        return np.asarray(i[n])

    def chunks(w):
        return np.ascontiguousarray(w.reshape(-1, P, w.shape[1]).transpose(1, 0, 2))

    const, sel = constants()
    out = {"const": const, "sel": sel}
    g = 96 // 16
    x = arr("x").reshape(B, 3, g, 16, g, 16).transpose(1, 3, 5, 0, 2, 4).reshape(PC * P, B, g * g)
    xt = np.zeros((PC * P, TP), np.float32)
    xt[:, 0:T].reshape(PC * P, B, N)[:, :, 1:] = x
    out["xT"] = chunks(xt)
    out["tokW"] = chunks(arr("L0_tok_W").T)
    out["posb"] = np.concatenate([arr("L0_tok_pos_enc")[0], arr("L0_tok_b")[None], arr("L0_tok_cls_token")[0]])

    even, odd = np.arange(0, DH, 2), np.arange(1, DH, 2)
    rows = np.concatenate([even, odd, odd, even])
    perm = np.concatenate([even, odd])
    wq = arr("L0_attn_Wqkv_w").reshape(H, DH, D)[:, rows, :]
    out["wq0"] = chunks(wq.reshape(H * R, D).T)
    bq = arr("L0_attn_Wqkv_b").reshape(H, DH)[:, rows].T
    out["u2t"] = np.concatenate([arr("L0_attn_U")] * 2).T
    wo = arr("L0_attn_Wo_w").T.reshape(H, DH, D)[:, perm, :].reshape(D, D)
    out["wo0"] = chunks(wo)
    sm = np.zeros((P, SW), np.float32)
    sm[:, S_BQ:S_BQ + H] = np.tile(bq, (BG, 1))
    sm[:, S_N1:S_N1 + DC] = arr("L1_attn_norm1_w").reshape(DC, P).T
    sm[:, S_N2:S_N2 + DC] = arr("L1_attn_norm2_w").reshape(DC, P).T
    sm[:, S_SC:S_SC + D] = arr("L1_ffn_scale")
    sm[:, S_BI:S_BI + D] = arr("L1_ffn_bias")
    sm[:, S_RB:S_RB + E] = arr("L0_ffn_router_b")
    out["small"] = sm
    out["rw"] = chunks(arr("L0_ffn_router_w"))

    gw = np.concatenate([arr("L0_ffn_sh_gate_w")[None], arr("L0_ffn_gate_w")])
    uw = np.concatenate([arr("L0_ffn_sh_up_w")[None], arr("L0_ffn_up_w")])
    dw = np.concatenate([arr("L0_ffn_sh_down_w")[None], arr("L0_ffn_down_w")])
    we = np.zeros((E + 1, P, WX), np.float32)
    for e in range(E + 1):
        mix = np.zeros((D, P), np.float32)
        for part, w in enumerate((gw[e], uw[e])):
            we[e, :, WOFF[part]:WOFF[part] + DC * GP] = chunks(w[:, 0:GP]).reshape(P, -1)
            mix[:, UPPER * part:UPPER * part + F - GP] = w[:, GP:F]
        we[e, :, WMIX:WMIX + DC * P] = chunks(mix).reshape(P, -1)
        z = np.zeros((FC * P, D), np.float32)
        z[0:GP] = dw[e][0:GP]
        z[GP + UPPER:F + UPPER] = dw[e][GP:F]
        we[e, :, WOFF[2]:] = chunks(z).reshape(P, -1)
    out["wexp"] = we

    def qrot(w):
        k = w.reshape(w.shape[0], KV, -1, DH)[:, :, :, rows].transpose(0, 2, 1, 3)
        return k.reshape(w.shape[0], -1, KV * R)

    def c3(w):
        return np.ascontiguousarray(w.reshape(-1, P, w.shape[1], w.shape[2]).transpose(1, 0, 2, 3))

    def wo1(w):
        z = np.zeros((KV, R, 4, D), np.float32)
        z[:, 0:DH] = w.reshape(KV, 4, DH, D).transpose(0, 2, 1, 3)
        return z.reshape(P, 4, D)

    out["wqg"] = c3(qrot(arr("L1_attn_g_wq")))
    out["kvd"] = chunks(arr("L1_attn_g_kv_down"))
    out["kug"] = qrot(arr("L1_attn_g_k_up"))[:, 0]
    out["vug"] = arr("L1_attn_g_v_up")
    out["wog"] = wo1(arr("L1_attn_g_wo"))
    out["wql"] = c3(np.concatenate([qrot(arr("L1_attn_l_wq")), qrot(arr("L1_attn_l_wk"))], 1))
    out["wvl"] = chunks(arr("L1_attn_l_wv"))
    out["wol"] = wo1(arr("L1_attn_l_wo"))
    out["wfin"] = chunks(arr("L1_ffn_weights").T)
    return {k: np.ascontiguousarray(v) for k, v in out.items()}


_NAMES = ["xT", "tokW", "sel", "posb", "const", "small", "wq0", "u2t", "wo0", "rw", "wexp",
          "wqg", "kvd", "kug", "vug", "wog", "wql", "wvl", "wol", "wfin"]


def kernel(**inputs):
    import concourse.bacc as _bacc
    from concourse.bass_utils import run_bass_kernel_spmd as _run

    nc = _bacc.Bacc("TRN2", target_bir_lowering=False, num_devices=1)
    laid = layout(inputs)
    arrays, args = {}, []
    for name in _NAMES:
        arrays[f"in_{name}"] = laid[name]
        args.append(nc.dram_tensor(f"in_{name}", laid[name].shape, F32, kind="ExternalInput").ap())
    out = nc.dram_tensor("out_0", (T, D), F32, kind="ExternalOutput").ap()
    tower(nc, *args, out)
    r = _run(nc, [arrays], core_ids=[0])
    return r.results[0]["out_0"].reshape(B, N, D)
```
